# Optimizing a Trainium2 kernel written in Bass

```python
import numpy as np
import jax
import jax.numpy as jnp

def _softmax(x, axis=-1):
    return jax.nn.softmax(x, axis=axis)

def _gelu(x):
    return jax.nn.gelu(x, approximate=True)

def _silu(x):
    return jax.nn.silu(x)

def _sigmoid(x):
    return jax.nn.sigmoid(x)

def _layernorm(x, axis=-1, eps=1e-05):
    m = jnp.mean(x, axis=axis, keepdims=True)
    v = jnp.var(x, axis=axis, keepdims=True)
    return (x - m) / jnp.sqrt(v + eps)

def _scatter_add(tgt, idx, src, axis=0):
    return tgt.at[idx].add(src)

def _segment_sum(src, seg, n):
    return jax.ops.segment_sum(src, seg, n)
kernel_name = 'mk_prb_d1_jaxref_r8_60b734'

def setup_inputs(seed: int=0):
    np.random.seed(seed)
    _w = jnp.asarray

    def _L0_attn_setup():
        import jax, jax.numpy as jnp
        import numpy as np
        B, S, HID = (1, 256, 512)
        H, NOPE, ROPE, VD = (32, 128, 64, 128)
        QKD = NOPE + ROPE
        Q_RANK, KV_RANK = (192, 64)
        IDX_H, IDX_D, TOPK = (16, 128, 128)
        EPS, THETA = (1e-05, 10000.0)

        def rmsnorm(x, w):
            return x * jax.lax.rsqrt(jnp.mean(x * x, axis=-1, keepdims=True) + EPS) * w

        def rope_interleaved(x, pos):
            d = x.shape[-1]
            inv_freq = 1.0 / THETA ** (jnp.arange(0, d, 2, dtype=jnp.float32) / d)
            ang = pos[:, None] * inv_freq[None, :]
            cos, sin = (jnp.cos(ang), jnp.sin(ang))
            x2 = x.reshape(*x.shape[:-1], d // 2, 2)
            x0, x1 = (x2[..., 0], x2[..., 1])
            return jnp.stack([x0 * cos - x1 * sin, x1 * cos + x0 * sin], axis=-1).reshape(x.shape)
        key = jax.random.key(seed)
        ks = jax.random.split(key, 12)
        s = 0.02
        return {'hidden_states': jax.random.normal(ks[0], (B, S, HID), jnp.float32), 'q_a_w': jax.random.normal(ks[1], (HID, Q_RANK), jnp.float32) * s, 'q_a_norm_w': jnp.ones((Q_RANK,), jnp.float32), 'q_b_w': jax.random.normal(ks[2], (Q_RANK, H * QKD), jnp.float32) * s, 'kv_a_w': jax.random.normal(ks[3], (HID, KV_RANK + ROPE), jnp.float32) * s, 'kv_a_norm_w': jnp.ones((KV_RANK,), jnp.float32), 'kv_b_w': jax.random.normal(ks[4], (KV_RANK, H * (NOPE + VD)), jnp.float32) * s, 'o_w': jax.random.normal(ks[5], (H * VD, HID), jnp.float32) * s, 'idx_wq_w': jax.random.normal(ks[6], (HID, IDX_H * IDX_D), jnp.float32) * s, 'idx_wk_w': jax.random.normal(ks[7], (HID, IDX_D), jnp.float32) * s, 'idx_weights_w': jax.random.normal(ks[8], (HID, IDX_H), jnp.float32) * s}
    _L0_attn_in = _L0_attn_setup()

    def _L0_ffn_setup():
        import jax, jax.numpy as jnp
        import numpy as np
        B_, S, D = (4, 512, 512)
        E, R, O = (8, 16, 512)
        TOP_K = 2
        SCALING = 8.0 / R
        key = jax.random.key(seed)
        ks = jax.random.split(key, 5)
        x = jax.random.normal(ks[0], (B_, S, D), dtype=jnp.float32)
        router_w = jax.random.normal(ks[1], (E, D), dtype=jnp.float32) * (1.0 / np.sqrt(D))
        router_b = jax.random.normal(ks[2], (E,), dtype=jnp.float32) * 0.01
        A = jax.random.normal(ks[3], (E, R, D), dtype=jnp.float32) * (1.0 / np.sqrt(D))
        Bm = jax.random.normal(ks[4], (E, O, R), dtype=jnp.float32) * 0.02
        return {'x': x, 'router_w': router_w, 'router_b': router_b, 'A': A, 'Bm': Bm}
    _L0_ffn_in = _L0_ffn_setup()
    _d = {'L0_attn_hidden_states': _L0_attn_in['hidden_states'], 'L0_attn_q_a_w': _L0_attn_in['q_a_w'], 'L0_attn_q_a_norm_w': _L0_attn_in['q_a_norm_w'], 'L0_attn_q_b_w': _L0_attn_in['q_b_w'], 'L0_attn_kv_a_w': _L0_attn_in['kv_a_w'], 'L0_attn_kv_a_norm_w': _L0_attn_in['kv_a_norm_w'], 'L0_attn_kv_b_w': _L0_attn_in['kv_b_w'], 'L0_attn_o_w': _L0_attn_in['o_w'], 'L0_attn_idx_wq_w': _L0_attn_in['idx_wq_w'], 'L0_attn_idx_wk_w': _L0_attn_in['idx_wk_w'], 'L0_attn_idx_weights_w': _L0_attn_in['idx_weights_w'], 'L0_ffn_router_w': _L0_ffn_in['router_w'], 'L0_ffn_router_b': _L0_ffn_in['router_b'], 'L0_ffn_A': _L0_ffn_in['A'], 'L0_ffn_Bm': _L0_ffn_in['Bm']}
    _x0 = _d['L0_attn_hidden_states']
    _d['L0_attn_hidden_states'] = jax.random.normal(jax.random.fold_in(jax.random.key(seed), 1), (1, 1024, 512), dtype=_x0.dtype)
    del _x0
    return _d

def reference(L0_attn_hidden_states, L0_attn_q_a_w, L0_attn_q_a_norm_w, L0_attn_q_b_w, L0_attn_kv_a_w, L0_attn_kv_a_norm_w, L0_attn_kv_b_w, L0_attn_o_w, L0_attn_idx_wq_w, L0_attn_idx_wk_w, L0_attn_idx_weights_w, L0_ffn_router_w, L0_ffn_router_b, L0_ffn_A, L0_ffn_Bm):

    def _L0_attn_ref(hidden_states, q_a_w, q_a_norm_w, q_b_w, kv_a_w, kv_a_norm_w, kv_b_w, o_w, idx_wq_w, idx_wk_w, idx_weights_w):
        import jax, jax.numpy as jnp
        import numpy as np
        B, S, HID = (1, 256, 512)
        H, NOPE, ROPE, VD = (32, 128, 64, 128)
        QKD = NOPE + ROPE
        Q_RANK, KV_RANK = (192, 64)
        IDX_H, IDX_D, TOPK = (16, 128, 128)
        EPS, THETA = (1e-05, 10000.0)

        def rmsnorm(x, w):
            return x * jax.lax.rsqrt(jnp.mean(x * x, axis=-1, keepdims=True) + EPS) * w

        def rope_interleaved(x, pos):
            d = x.shape[-1]
            inv_freq = 1.0 / THETA ** (jnp.arange(0, d, 2, dtype=jnp.float32) / d)
            ang = pos[:, None] * inv_freq[None, :]
            cos, sin = (jnp.cos(ang), jnp.sin(ang))
            x2 = x.reshape(*x.shape[:-1], d // 2, 2)
            x0, x1 = (x2[..., 0], x2[..., 1])
            return jnp.stack([x0 * cos - x1 * sin, x1 * cos + x0 * sin], axis=-1).reshape(x.shape)
        b, s, _ = hidden_states.shape
        pos = jnp.arange(s, dtype=jnp.float32)
        q_lat = rmsnorm(hidden_states @ q_a_w, q_a_norm_w)
        q = (q_lat @ q_b_w).reshape(b, s, H, QKD).transpose(0, 2, 1, 3)
        q_nope, q_pe = (q[..., :NOPE], q[..., NOPE:])
        ckv = hidden_states @ kv_a_w
        kv_lat, k_pe = (ckv[..., :KV_RANK], ckv[..., KV_RANK:])
        kv = (rmsnorm(kv_lat, kv_a_norm_w) @ kv_b_w).reshape(b, s, H, NOPE + VD).transpose(0, 2, 1, 3)
        k_nope, v = (kv[..., :NOPE], kv[..., NOPE:])
        q_pe = rope_interleaved(q_pe, pos)
        k_pe = rope_interleaved(k_pe[:, None, :, :], pos)
        scores = (jnp.einsum('bhqd,bhkd->bhqk', q_nope, k_nope) + jnp.einsum('bhqd,bhkd->bhqk', q_pe, k_pe)) * QKD ** (-0.5)
        iq = (hidden_states @ idx_wq_w).reshape(b, s, IDX_H, IDX_D)
        ik = hidden_states @ idx_wk_w
        iw = hidden_states @ idx_weights_w * IDX_H ** (-0.5)
        idx_scores = jnp.einsum('bqn,bnqk->bqk', iw, jax.nn.relu(jnp.einsum('bqnd,bkd->bnqk', iq, ik))) * IDX_D ** (-0.5)
        causal = pos[:, None] >= pos[None, :]
        idx_scores = jnp.where(causal, idx_scores, -jnp.inf)
        _, topk_idx = jax.lax.top_k(idx_scores, TOPK)
        bi = jnp.arange(b)[:, None, None]
        qi = jnp.arange(s)[None, :, None]
        topk_mask = jnp.zeros((b, s, s), bool).at[bi, qi, topk_idx].set(True)
        mask = topk_mask & causal
        scores = jnp.where(mask[:, None], scores, -jnp.inf)
        attn = jax.nn.softmax(scores, axis=-1)
        out = jnp.einsum('bhqk,bhkd->bqhd', attn, v).reshape(b, s, H * VD)
        return out @ o_w

    def _L0_ffn_ref(x, router_w, router_b, A, Bm):
        import jax, jax.numpy as jnp
        import numpy as np
        B_, S, D = (4, 512, 512)
        E, R, O = (8, 16, 512)
        TOP_K = 2
        SCALING = 8.0 / R
        flat = x.reshape(-1, x.shape[-1])
        N = flat.shape[0]
        logits = flat @ router_w.T + router_b
        probs = jax.nn.softmax(logits, axis=-1)
        topv, topi = jax.lax.top_k(probs, TOP_K)
        gates = topv / jnp.sum(topv, axis=-1, keepdims=True)
        w = jnp.zeros((N, E), dtype=flat.dtype).at[jnp.arange(N)[:, None], topi].add(gates)
        h = jnp.einsum('nd,erd->ner', flat, A)
        hw = h * w[:, :, None]
        out = jnp.einsum('ner,eor->no', hw, Bm) * SCALING
        return out.reshape(*x.shape[:-1], O)
    x = L0_attn_hidden_states
    xn = _layernorm(x, axis=-1)
    x = x + _L0_attn_ref(xn, L0_attn_q_a_w, L0_attn_q_a_norm_w, L0_attn_q_b_w, L0_attn_kv_a_w, L0_attn_kv_a_norm_w, L0_attn_kv_b_w, L0_attn_o_w, L0_attn_idx_wq_w, L0_attn_idx_wk_w, L0_attn_idx_weights_w) + _L0_ffn_ref(xn, L0_ffn_router_w, L0_ffn_router_b, L0_ffn_A, L0_ffn_Bm)
    return x

_drawn_inputs = setup_inputs


def setup_inputs(seed=0):
    import zlib

    import numpy as np

    out = dict(_drawn_inputs(seed))
    spreads = {'L0_attn_q_a_norm_w': (1.0, 0.6), 'L0_attn_kv_a_norm_w': (1.0, 0.6)}
    factors = {'L0_attn_q_a_w': 8.0,
     'L0_attn_q_b_w': 8.0,
     'L0_attn_idx_wq_w': 3.203,
     'L0_attn_idx_wk_w': 3.188,
     'L0_attn_idx_weights_w': 3.206,
     'L0_ffn_router_b': 8.0}
    for name, (base, spread) in spreads.items():
        noise = np.random.default_rng([zlib.crc32(name.encode()), seed]).standard_normal(out[name].shape)
        drawn = base * np.exp(spread * noise) if base else spread * noise
        out[name] = jnp.asarray(drawn.astype(out[name].dtype))
    for name, factor in factors.items():
        out[name] = (out[name] * factor).astype(out[name].dtype)
    return out
```

```python
from contextlib import ExitStack

import numpy as np

import concourse.bass as bass
from concourse import mybir

F32 = mybir.dt.float32
F16 = mybir.dt.float16
ALU = mybir.AluOpType
ACT = mybir.ActivationFunctionType
AX = mybir.AxisListType

P = 128
S, HID = 1024, 512
NT = S // P
KT = HID // P
H, NOPE, ROPE, VD = 32, 128, 64, 128
NP = H // 2
QR, KVR = 192, 64
IH, ID, TOPK = 16, 128, 128
E, R = 8, 16
EPS = 1e-5
SCALING = 8.0 / R

C_Q, C_KV, C_IW, C_R, C_H = 0, QR, QR + KVR + ROPE, QR + KVR + ROPE + IH, QR + KVR + ROPE + IH + E
CW = C_H + E * R

NEG = -1e30
TAKEN = -3e38
HALF_TAKEN = -2e38

X_S, W_S, IQ_S, QL_S, WQ_S, Q_S, K_S = 64.0, 128.0, 32.0, 32.0, 64.0, 16.0, 16.0
PR_S, O_S, WVO_S, HW_S, B_S = 1024.0, 16.0, 256.0, 32.0, 128.0
OUT_S = O_S * WVO_S
assert HW_S * B_S == OUT_S

ORDER = [7, 0, 6, 1, 5, 2, 4, 3]
CH = 512
ARENA = 15040


def block_kernel(nc, x, wcat, wik, wiq, qbT, wkT, wvT, qpe, ow, bm, qnorm, kvnorm, rbias,
                 cosq, sinq, cosk, sink, ident_d, causal_d, out):
    with ExitStack() as ctx:
        def sb(name, shape, dt=F32):
            return ctx.enter_context(nc.sbuf_tensor(name, shape, dt))

        def sem(name):
            return ctx.enter_context(nc.semaphore(name))

        big = sb("big", [P, 2, NP, S], F16)
        iq = big[:, :, 0:IH, :]
        w1hi = sb("w1hi", [P, NP, 256], F16)
        w1lo = sb("w1lo", [P, NP, 256], F16)
        w2s = sb("w2s", [P, NP, 256], F16)
        TOFF = [P * t * (t + 1) // 2 for t in range(NT + 1)]
        bias = sb("bias", [P, TOFF[NT]])
        cq = sb("cq", [P, S])
        sq = sb("sq", [P, S])
        keyT = sb("keyT", [P, 2, 2, S], F16)
        val = sb("val", [P, 2, NT, KVR], F16)
        qlT = sb("qlT", [P, 4, S], F16)
        hwT = sb("hwT", [P, 2, S], F16)
        bmp = sb("bmp", [P, 2, HID], F16)
        ikT = sb("ikT", [P, 2, S], F16)
        ident = sb("ident", [P, P])
        causal = sb("causal", [P, P])
        m8 = sb("m8", [P, 8])
        small = sb("small", [P, 512])
        arena = sb("arena", [P, ARENA])

        def view(at, n, dt=F32):
            words = n if dt == F32 else n // 2
            assert at + words <= ARENA
            v = arena[:, at:at + words]
            return v if dt == F32 else v.bitcast(dt)

        half0 = big[:, 0, :, :].rearrange("p a b -> p (a b)")
        half1 = big[:, 1, :, :].rearrange("p a b -> p (a b)")
        x_sb = half0[:, 0:2 * NT * HID].bitcast(F32).rearrange("p (t d) -> p t d", t=NT)
        xn = half0[:, 8192:8192 + 4 * HID].bitcast(F32).rearrange("p (u d) -> p u d", u=2)
        wc = half1[:, 0:2 * KT * CW].bitcast(F32).rearrange("p (k n) -> p k n", k=KT)
        wcp = half1[:, 2 * KT * CW:4 * KT * CW].rearrange("p (s k n) -> p s k n", s=2, k=KT)
        wk32 = half1[:, 4 * KT * CW:4 * KT * CW + 2 * KT * ID].bitcast(F32).rearrange("p (k n) -> p k n", k=KT)
        bm32 = half1[:, 4 * KT * CW + 2 * KT * ID:4 * KT * CW + 2 * KT * ID + 2 * HID].bitcast(F32)
        xnT = view(0, 2 * KT * S, F16).rearrange("p (s k q) -> p s k q", s=2, k=KT)
        proj = view(4096, NT * CW).rearrange("p (t n) -> p t n", t=NT)
        o = 4096 + NT * CW
        qn = view(o, NT * 256).rearrange("p (t n) -> p t n", t=NT)
        relu = view(o, 2 * S).rearrange("p (u n) -> p u n", u=2)
        kc = view(o + 2048, NT * 192).rearrange("p (t n) -> p t n", t=NT)
        tmp = view(o + 2048 + 1536, NT * QR).rearrange("p (t n) -> p t n", t=NT)
        o += 2048 + 1536 + 1536
        wq32 = view(o, 2 * HID).rearrange("p (u k n) -> p u k n", u=2, k=KT)
        wqp = view(o + 1024, 4 * HID, F16).rearrange("p (u s k n) -> p u s k n", u=2, s=2, k=KT)
        wikp = keyT[:, 0, 0, :].rearrange("p (s k n) -> p s k n", s=2, k=KT)
        qb_s = view(0, 2 * 512).rearrange("p (u h r) -> p u h r", u=2, h=2)
        wk_s = view(1024, 2 * 128).rearrange("p (u h r) -> p u h r", u=2, h=2)
        pe_s = view(1280, 2 * 256).rearrange("p (u k n) -> p u k n", u=2, k=2)
        Q = view(0, 8 * S, F16).rearrange("p (v s h q) -> p v s h q", v=2, s=2, h=2)
        raw = view(4096, S)
        swp = view(4096 + S, S)
        pr = view(6144, 2 * S).rearrange("p (u k) -> p u k", u=2)
        pT = view(8192, 4 * S, F16).rearrange("p (u s k) -> p u s k", u=2, s=2)
        op = view(10240, NT * P).rearrange("p (k r) -> p k r", k=NT)
        wvo = view(0, 2 * NP * HID, F16).rearrange("p (s k n) -> p s k n", s=2, k=NP)
        ow_s = view(8192, 2 * 2 * HID).rearrange("p (u h n) -> p u h n", u=2, h=2)
        wv_s = view(10240, 2 * P).rearrange("p (u h r) -> p u h r", u=2, h=2)
        xr = view(10496, 2 * HID).rearrange("p (u n) -> p u n", u=2)
        res = view(10496 + 2 * HID, 2 * HID).rearrange("p (u n) -> p u n", u=2)

        st = small[:, 0:NT * 6].rearrange("p (t n) -> p t n", t=NT)
        mv = small[:, 48:64].rearrange("p (t n) -> p t n", t=NT)
        ve = small[:, 64:72]
        sd = small[:, 72:80]
        rstd = small[:, 80:88]
        ssq = small[:, 88:104].rearrange("p (w t) -> p w t", w=2)
        sdn = small[:, 104:120].rearrange("p (w t) -> p w t", w=2)
        rsn = small[:, 120:136].rearrange("p (w t) -> p w t", w=2)
        gm = small[:, 136:144]
        gden = small[:, 144:152]
        grd = small[:, 152:160]
        gl = small[:, 160:224].rearrange("p (t e) -> p t e", t=NT)
        gmx = small[:, 224:288].rearrange("p (t e) -> p t e", t=NT)
        gw = small[:, 288:352].rearrange("p (t e) -> p t e", t=NT)
        rbs = small[:, 352:360]
        nmax = small[:, 360:362]
        rsum = small[:, 364:380].rearrange("p (h t) -> p h t", h=2)
        rinv = small[:, 380:388]
        gwork = sb("gwork", [P, NT, 16])
        grep = sb("grep", [P, NT, 8])
        gout = sb("gout", [P, NT, 16])
        qnw = sb("qnw", [P, QR])
        kvw = sb("kvw", [P, KVR])
        ckv = w2s[:].rearrange("p a b -> p (a b)")
        ck = ckv[:, 0:512].bitcast(F32).rearrange("p (t j) -> p t j", t=NT)
        sk = ckv[:, 512:1024].bitcast(F32).rearrange("p (t j) -> p t j", t=NT)

        psS = [ctx.enter_context(nc.psum_tensor(f"psS{u}", [P, S], F32)) for u in range(2)]
        psT = [ctx.enter_context(nc.psum_tensor(f"psT{u}", [P, CH], F32)) for u in range(2)]
        psO = ctx.enter_context(nc.psum_tensor("psO", [P, CH], F32))
        psM = ctx.enter_context(nc.psum_tensor("psM", [P, CH], F32))

        ld_x = [sem("ld_x0"), sem("ld_x1")]
        ld_wc = sem("ld_wc"); ld_c = sem("ld_c"); ld_cq = sem("ld_cq")
        wc_hi = sem("wc_hi"); wc_lo = sem("wc_lo")
        st_done = sem("st_done"); ve_done = sem("ve_done"); sd_done = sem("sd_done"); rs_done = sem("rs_done")
        xn_done = sem("xn_done"); xT_done = sem("xT_done"); xhi_done = sem("xhi_done"); xlo_done = sem("xlo_done")
        pj_mm = sem("pj_mm"); pj_done = sem("pj_done")
        bar = sem("bar")
        wik_lo = sem("wik_lo")
        ik_mm = sem("ik_mm"); ik_hi = sem("ik_hi"); ik_lo = sem("ik_lo")
        ld_wq = [sem("ld_wq0"), sem("ld_wq1")]
        wq_sc = sem("wq_sc"); wq_hi = sem("wq_hi"); wq_lo = sem("wq_lo")
        iq_mm = sem("iq_mm"); iq_hi = sem("iq_hi"); iq_lo = sem("iq_lo")
        idx_init = sem("idx_init"); idx_mm = sem("idx_mm"); relu_done = sem("relu_done"); acc_done = sem("acc_done")
        tk_max = sem("tk_max"); tk_rep = sem("tk_rep"); mask_done = sem("mask_done")
        nrm = sem("nrm"); n_sqrt = sem("n_sqrt"); g_exp = sem("g_exp"); g_sub = sem("g_sub")
        tr_mm = sem("tr_mm"); tr_hi = sem("tr_hi"); tr_lo = sem("tr_lo"); v_hi = sem("v_hi")
        kc_done = sem("kc_done"); qn_done = sem("qn_done"); hw_done = sem("hw_done")
        ld_qw = [sem("ld_qw0"), sem("ld_qw1")]
        qw_mm = sem("qw_mm"); qw_hi = sem("qw_hi"); qw_lo = sem("qw_lo")
        s_mm = sem("s_mm"); max_done = sem("max_done"); exp_done = sem("exp_done")
        t_mm = sem("t_mm"); p_hi = sem("p_hi"); p_lo = sem("p_lo"); av_mm = sem("av_mm")
        ri_done = sem("ri_done"); o_done = sem("o_done")
        ot_mm = sem("ot_mm"); ot_hi = sem("ot_hi"); ot_lo = sem("ot_lo")
        qp_mm = sem("qp_mm"); qa_mm = sem("qa_mm"); raw_done = sem("raw_done"); qa_hi = sem("qa_hi"); qa_lo = sem("qa_lo")
        sw_done = sem("sw_done"); rot = sem("rot"); q_rot = sem("q_rot")
        ld_ow = [sem("ld_ow0"), sem("ld_ow1")]
        vo_mm = sem("vo_mm"); vo_hi = sem("vo_hi"); vo_lo = sem("vo_lo")
        ld_xr = [sem("ld_xr0"), sem("ld_xr1")]
        fin_mm = sem("fin_mm"); fin_done = sem("fin_done"); stored = [sem("stored0"), sem("stored1")]

        stood = {}

        def wait_alone(eng, semaphore, value):
            if eng not in stood:
                stood[eng] = sem(f"stood{len(stood)}")
            eng.wait_ge(semaphore, value).then_inc(stood[eng], 1)

        block = ctx.enter_context(nc.Block())
        ds = bass.ds

        def barrier(eng, n):
            eng.drain().then_inc(bar, 1)
            eng.wait_ge(bar, 5 * n)

        NB = [t + 1 for t in ORDER]
        NCH = [(b + 3) // 4 for b in NB]
        CUM = [sum(NCH[:k]) for k in range(9)]
        CPH = CUM[8]
        assert CPH % 2 == 0

        def chunks_before(head, k):
            return head * CPH + CUM[k]

        n_const = 9

        @block.sync
        def _(sp):
            xv = x.rearrange("(t p) d -> p t d", p=P)
            sp.dma_start(x_sb[:, 0:4, :], xv[:, 0:4, :]).then_inc(ld_x[0], 16)
            sp.dma_start(x_sb[:, 4:8, :], xv[:, 4:8, :]).then_inc(ld_x[1], 16)
            sp.dma_start(wc, wcat.rearrange("(k p) n -> p k n", p=P)).then_inc(ld_wc, 16)
            sp.dma_start(wk32, wik.rearrange("(k p) n -> p k n", p=P)).then_inc(ld_c, 16)
            sp.dma_start(ident[:], ident_d).then_inc(ld_c, 16)
            sp.dma_start(causal[:], causal_d).then_inc(ld_c, 16)
            sp.dma_start(qnw[:], qnorm).then_inc(ld_c, 16)
            sp.dma_start(kvw[:], kvnorm).then_inc(ld_c, 16)
            sp.dma_start(rbs, rbias).then_inc(ld_c, 16)
            sp.dma_start(ck, cosk.rearrange("(t p) j -> p t j", p=P)).then_inc(ld_c, 16)
            sp.dma_start(sk, sink.rearrange("(t p) j -> p t j", p=P)).then_inc(ld_c, 16)
            sp.dma_start(bm32, bm).then_inc(ld_c, 16)
            sp.dma_start(cq[:], cosq).then_inc(ld_cq, 16)
            sp.dma_start(sq[:], sinq).then_inc(ld_cq, 16)
            barrier(sp, 1)

            wiq_v = wiq.rearrange("(k p) n -> p k n", p=P)

            def load_iq(n, u, first):
                if not first:
                    wait_alone(sp, wq_lo, n - 1)
                sp.dma_start(wq32[:, u], wiq_v[:, :, ds(n * ID, ID)]).then_inc(ld_wq[u], 16)

            load_iq(0, 0, True)
            load_iq(1, 1, True)
            with sp.Fori(1, IH // 2) as i:
                load_iq(2 * i, 0, False)
                load_iq(2 * i + 1, 1, False)

            wait_alone(sp, iq_mm, 2 * IH)

            def load_qw(p, u, first):
                if not first:
                    wait_alone(sp, qw_lo, 4 * p - 4)
                sp.dma_start(qb_s[:, u], qbT[:, ds(2 * p, 2), :]).then_inc(ld_qw[u], 16)
                sp.dma_start(wk_s[:, u], wkT[:, ds(2 * p, 2), :]).then_inc(ld_qw[u], 16)
                sp.dma_start(pe_s[:, u].rearrange("p k (h r) -> p k h r", h=2),
                             qpe[:, :, ds(2 * p, 2), :]).then_inc(ld_qw[u], 16)

            load_qw(0, 0, True)
            load_qw(1, 1, True)
            with sp.Fori(1, NP // 2) as i:
                load_qw(2 * i, 0, False)
                load_qw(2 * i + 1, 1, False)
            barrier(sp, 2)

            def swap(p):
                wait_alone(sp, raw_done, 2 * p + 2)
                if not (isinstance(p, int) and p == 0):
                    wait_alone(sp, rot, 3 * p)
                sp.dma_start(swp[0:P:2, :], raw[1:P:2, :]).then_inc(sw_done, 16)
                sp.dma_start(swp[1:P:2, :], raw[0:P:2, :]).then_inc(sw_done, 16)

            swap(0)
            with sp.Fori(1, NP) as p:
                swap(p)
            barrier(sp, 3)

            ow_v = ow.rearrange("(h d) n -> d h n", d=P)

            def load_ow(p, u, first):
                if not first:
                    wait_alone(sp, vo_mm, p - 1)
                sp.dma_start(ow_s[:, u], ow_v[:, ds(2 * p, 2), :]).then_inc(ld_ow[u], 16)
                sp.dma_start(wv_s[:, u], wvT[:, ds(2 * p, 2), :]).then_inc(ld_ow[u], 16)

            load_ow(0, 0, True)
            load_ow(1, 1, True)
            with sp.Fori(1, NP // 2) as i:
                load_ow(2 * i, 0, False)
                load_ow(2 * i + 1, 1, False)

            def rows(t, u, first):
                if not first:
                    wait_alone(sp, fin_done, t - 1)
                sp.dma_start(xr[:, u], x[ds(t * P, P), :]).then_inc(ld_xr[u], 16)

            def store(t, u):
                wait_alone(sp, fin_done, t + 1)
                sp.dma_start(out[ds(t * P, P), :], res[:, u]).then_inc(stored[u], 16)

            rows(0, 0, True)
            rows(1, 1, True)
            with sp.Fori(1, NT // 2) as i:
                store(2 * i - 2, 0)
                rows(2 * i, 0, False)
                store(2 * i - 1, 1)
                rows(2 * i + 1, 1, False)
            store(NT - 2, 0)
            store(NT - 1, 1)
            for u in range(2):
                wait_alone(sp, stored[u], 16 * NT // 2)

        @block.tensor
        def _(pe):
            mm = nc.tensor.matmul

            pe.wait_ge(ld_c, 16 * n_const)

            def rows_T(t, u, first):
                pe.wait_ge(xn_done, t + 1)
                if not first:
                    pe.wait_ge(xlo_done, t - 1)
                for k in range(KT):
                    last = nc.tensor.transpose(psT[u][:, k * P:(k + 1) * P], xn[:, u, k * P:(k + 1) * P], ident[:])
                last.then_inc(xT_done, 1)

            def rows_proj(t, u, first):
                pe.wait_ge(xlo_done, t + 1)
                if not first:
                    pe.wait_ge(pj_done, t - 1)
                ins = 0
                for k in range(KT):
                    for a, b in ((0, 0), (0, 1), (1, 0)):
                        last = mm(psS[u][:, 0:CW], xnT[:, a, k, ds(t * P, P)], wcp[:, b, k, :],
                                  start=ins == 0, stop=ins == 3 * KT - 1)
                        ins += 1
                last.then_inc(pj_mm, 1)

            def rows_pair(i, first):
                rows_T(2 * i, 0, first)
                rows_T(2 * i + 1, 1, first)
                if first:
                    pe.wait_ge(wc_lo, 1)
                rows_proj(2 * i, 0, first)
                rows_proj(2 * i + 1, 1, first)

            rows_pair(0, True)
            with pe.Fori(1, NT // 2) as i:
                rows_pair(i, False)
            barrier(pe, 1)

            def indexer(dst, w, c, semaphore):
                ins = 0
                for k in range(KT):
                    for a, b in ((0, 0), (0, 1), (1, 0)):
                        last = mm(dst, w[:, a, k, :], xnT[:, b, k, c * CH:(c + 1) * CH],
                                  start=ins == 0, stop=ins == 3 * KT - 1)
                        ins += 1
                last.then_inc(semaphore, 1)

            for c in range(2):
                indexer(psT[c][:], wikp, c, ik_mm)

            def iq_head(n, u, first):
                pe.wait_ge(wq_lo, n + 1)
                for c in range(2):
                    if not first:
                        pe.wait_ge(iq_lo, 2 * n + c - 3)
                    indexer(psS[u][:, c * CH:(c + 1) * CH], wqp[:, u], c, iq_mm)

            iq_head(0, 0, True)
            iq_head(1, 1, True)
            with pe.Fori(1, IH // 2) as i:
                iq_head(2 * i, 0, False)
                iq_head(2 * i + 1, 1, False)

            def idx_head(t, n, u, base):
                kw = P * (t + 1)
                pe.wait_ge(relu_done, base + n - 1) if not (isinstance(n, int) and base + n - 1 <= 0) else None
                for a, b in ((0, 0), (0, 1), (1, 0)):
                    for c in range(0, kw, CH):
                        w = min(CH, kw - c)
                        last = mm(psS[u][:, c:c + w], iq[:, a, n, t * P:(t + 1) * P], ikT[:, b, c:c + w],
                                  start=(a, b) == (0, 0), stop=(a, b) == (1, 0))
                last.then_inc(idx_mm, 1)

            pe.wait_ge(iq_lo, 2 * IH)
            pe.wait_ge(ik_lo, 2)
            base = 0
            for t in range(NT - 1, 0, -1):
                idx_head(t, 0, 0, base)
                idx_head(t, 1, 1, base)
                with pe.Fori(1, IH // 2) as i:
                    idx_head(t, 2 * i, 0, base)
                    idx_head(t, 2 * i + 1, 1, base)
                base += IH

            job = 0
            for src, ready in ((qn[:, :, 0:P], qn_done), (qn[:, :, P:2 * P], qn_done),
                               (kc[:, :, 0:P], kc_done), (kc[:, :, KVR:KVR + P], kc_done),
                               (tmp[:, :, 0:P], hw_done)):
                pe.wait_ge(ready, 1)
                for c in range(2):
                    if job >= 2:
                        pe.wait_ge(tr_lo, job - 1)
                    for j in range(4):
                        last = nc.tensor.transpose(psT[job % 2][:, j * P:(j + 1) * P], src[:, 4 * c + j, :], ident[:])
                    last.then_inc(tr_mm, 1)
                    job += 1

            def qw_pair(p, u, first):
                pe.wait_ge(ld_qw[u], 48 * (p // 2 + 1) if isinstance(p, int) else 24 * (p - u) + 48)
                if not first:
                    pe.wait_ge(qw_lo, 4 * p - 4)
                for h in range(2):
                    for k in range(2):
                        last = mm(psS[u][:, 128 * k + 64 * (1 - h):128 * k + 64 * (2 - h)],
                                  qb_s[:, u, h, 128 * k:128 * (k + 1)], wk_s[:, u, h, :], start=True, stop=True)
                last.then_inc(qw_mm, 1)

            qw_pair(0, 0, True)
            qw_pair(1, 1, True)
            with pe.Fori(1, NP // 2) as i:
                qw_pair(2 * i, 0, False)
                qw_pair(2 * i + 1, 1, False)
            barrier(pe, 2)

            def q_chunk(p, group, c, semaphore):
                lo, n = 128 * group, 128
                cs = slice(c * CH, (c + 1) * CH)
                ws = slice(lo, lo + n)
                mm(psM[:], w1hi[:, p, ws], qlT[:, 0, cs], start=True, stop=False)
                mm(psM[:], w1hi[:, p, ws], qlT[:, 1, cs], start=False, stop=False)
                mm(psM[:], w1lo[:, p, ws], qlT[:, 0, cs], start=False, stop=False)
                mm(psM[:], w2s[:, p, ws], qlT[:, 2, cs], start=False, stop=False)
                mm(psM[:], w2s[0:64, p, ws], qlT[0:64, 3, cs], start=False, stop=True).then_inc(semaphore, 1)

            def q_job(p, j):
                if j == 1:
                    pe.wait_ge(raw_done, 2 * p + 1)
                if j == 2:
                    pe.wait_ge(raw_done, 2 * p + 2)
                if j == 3:
                    pe.wait_ge(qa_lo, 4 * p + 2)
                q_chunk(p, j // 2, j % 2, qp_mm if j < 2 else qa_mm)

            def scores(p, v, h, k, wait_q):
                t = ORDER[k]
                kw = P * (t + 1)
                if wait_q:
                    pe.wait_ge(q_rot, 4 * p + 4)
                    pe.wait_ge(qa_lo, 4 * p + 4)
                for a, b in ((0, 0), (0, 1), (1, 0)):
                    for c in range(0, kw, CH):
                        w = min(CH, kw - c)
                        last = mm(psS[k % 2][:, c:c + w], Q[:, v, a, h, t * P:(t + 1) * P], keyT[:, b, h, c:c + w],
                                  start=(a, b) == (0, 0), stop=(a, b) == (1, 0))
                last.then_inc(s_mm, 1)

            def probs_T(head, k):
                step = 8 * head + k
                pe.wait_ge(exp_done, step + 1)
                for c in range(NCH[k]):
                    idx = chunks_before(head, k) + c
                    if not (isinstance(idx, int) and idx < 2):
                        pe.wait_ge(p_lo, idx - 1)
                    bank = psT[(CUM[k] + c) % 2]
                    for j in range(4 * c, min(4 * c + 4, NB[k])):
                        last = nc.tensor.transpose(bank[:, (j % 4) * P:(j % 4 + 1) * P],
                                                   pr[:, k % 2, j * P:(j + 1) * P], ident[:])
                    last.then_inc(t_mm, 1)

            def values(head, k):
                pe.wait_ge(p_lo, chunks_before(head, k + 1))
                if k == 0 and not (isinstance(head, int) and head == 0):
                    pe.wait_ge(o_done, head)
                dst = psO[:, k * KVR:(k + 1) * KVR]
                for j in range(NB[k]):
                    for n, (a, b) in enumerate(((0, 0), (0, 1), (1, 0))):
                        last = mm(dst, pT[:, k % 2, a, j * P:(j + 1) * P], val[:, b, j, :],
                                  start=j == 0 and n == 0, stop=j == NB[k] - 1 and n == 2)
                last.then_inc(av_mm, 1)

            def out_T(p, c):
                if c == 0:
                    pe.wait_ge(o_done, 2 * p + 2)
                else:
                    pe.wait_ge(ot_lo, 2 * p + 1)
                for j in range(4):
                    k = ORDER.index(4 * c + j)
                    last = nc.tensor.transpose(psM[:, j * P:(j + 1) * P], op[:, k, :], ident[:])
                last.then_inc(ot_mm, 1)

            def pair(p, v, first, last_pair):
                for s in range(16):
                    h, k = s // 8, s % 8
                    head = 2 * p + h
                    probs_T(head, k)
                    if s + 2 < 16:
                        pe.wait_ge(max_done, 8 * head + k + 1)
                        scores(p, v, (s + 2) // 8, (s + 2) % 8, False)
                    elif not last_pair:
                        pe.wait_ge(max_done, 8 * head + k + 1)
                        scores(p + 1, 1 - v, 0, s - 14, s == 14)
                    if not (first and s == 0):
                        values(head if k else head - 1, (k - 1) % 8)
                    if not first and s == 3:
                        pe.wait_ge(qa_lo, 4 * p + 4)
                        out_T(p - 1, 0)
                    if not first and s == 4:
                        out_T(p - 1, 1)
                    if not last_pair:
                        if s == 5:
                            if not first:
                                pe.wait_ge(ot_lo, 2 * p)
                            q_job(p + 1, 0)
                        if s in (6, 8, 10):
                            q_job(p + 1, {6: 1, 8: 2, 10: 3}[s])

            for j in range(4):
                q_job(0, j)
            scores(0, 0, 0, 0, True)
            scores(0, 0, 0, 1, False)
            pair(0, 0, True, False)
            with pe.Fori(0, NP // 2 - 1) as i:
                pair(2 * i + 1, 1, False, False)
                pair(2 * i + 2, 0, False, False)
            pair(NP - 1, 1, False, True)
            values(H - 1, 7)
            out_T(NP - 1, 0)
            out_T(NP - 1, 1)
            barrier(pe, 3)

            def vo_pair(p, u, first):
                pe.wait_ge(ld_ow[u], 32 * (p // 2 + 1) if isinstance(p, int) else 16 * (p - u) + 32)
                if not first:
                    pe.wait_ge(vo_lo, p - 1)
                for h in range(2):
                    last = mm(psT[u][64 * h:64 * (h + 1), :], wv_s[:, u, h, :], ow_s[:, u, h, :], start=True, stop=True)
                last.then_inc(vo_mm, 1)

            vo_pair(0, 0, True)
            vo_pair(1, 1, True)
            with pe.Fori(1, NP // 2) as i:
                vo_pair(2 * i, 0, False)
                vo_pair(2 * i + 1, 1, False)
            pe.wait_ge(vo_lo, NP)

            def final(t, u, first):
                if not first:
                    pe.wait_ge(fin_done, t - 1)
                rows_ = ds(t * P, P)
                for n in range(NP):
                    for a, b in ((0, 0), (0, 1), (1, 0)):
                        mm(psS[u][:, 0:CH], big[:, a, n, rows_], wvo[:, b, n, :], start=n == 0 and (a, b) == (0, 0), stop=False)
                for a, b in ((0, 0), (0, 1), (1, 0)):
                    last = mm(psS[u][:, 0:CH], hwT[:, a, rows_], bmp[:, b, :], start=False, stop=(a, b) == (1, 0))
                last.then_inc(fin_mm, 1)

            final(0, 0, True)
            final(1, 1, True)
            with pe.Fori(1, NT // 2) as i:
                final(2 * i, 0, False)
                final(2 * i + 1, 1, False)

        @block.scalar
        def _(act):
            def copy(dst, src, scale):
                return nc.scalar.activation(dst, src, ACT.Copy, scale=scale)

            act.wait_ge(ld_wc, 16)
            copy(wcp[:, 0], wc, W_S).then_inc(wc_hi, 1)
            act.wait_ge(ld_c, 16 * n_const)
            copy(wikp[:, 0], wk32, W_S).then_inc(wc_hi, 1)
            copy(bmp[:, 0, :], bm32, B_S).then_inc(wc_hi, 1)
            act.wait_ge(ve_done, 1)
            nc.scalar.activation(sd, ve, ACT.Sqrt).then_inc(sd_done, 1)

            def rows_hi(t, u):
                act.wait_ge(xT_done, t + 1)
                copy(xnT[:, 0, :, ds(t * P, P)], psT[u][:].rearrange("p (k q) -> p k q", k=KT), X_S).then_inc(xhi_done, 1)

            def rows_pj(t, u):
                act.wait_ge(pj_mm, t + 1)
                copy(proj[:, t, :], psS[u][:, 0:CW], 1.0 / (X_S * W_S)).then_inc(pj_done, 1)

            def rows_pair(i):
                rows_hi(2 * i, 0)
                rows_hi(2 * i + 1, 1)
                rows_pj(2 * i, 0)
                rows_pj(2 * i + 1, 1)

            with act.Fori(0, NT // 2) as i:
                rows_pair(i)
            barrier(act, 1)

            sc = IQ_S / (X_S * W_S)
            for c in range(2):
                act.wait_ge(ik_mm, c + 1)
                copy(ikT[:, 0, c * CH:(c + 1) * CH], psT[c][:], sc).then_inc(ik_hi, 1)
            with act.Fori(0, IH // 2) as i:
                for u in range(2):
                    for c in range(2):
                        act.wait_ge(iq_mm, 4 * i + 2 * u + c + 1)
                        copy(iq[:, 0, 2 * i + u, c * CH:(c + 1) * CH], psS[u][:, c * CH:(c + 1) * CH], sc).then_inc(iq_hi, 1)

            rsc = IH ** -0.5 * ID ** -0.5 / (IQ_S * IQ_S)
            base = 0
            for t in range(NT - 1, 0, -1):
                kw = P * (t + 1)

                def relu_head(n, u):
                    act.wait_ge(idx_mm, base + n + 1)
                    if not (isinstance(n, int) and base + n < 2):
                        act.wait_ge(acc_done, base + n - 1)
                    nc.scalar.activation(relu[:, u, 0:kw], psS[u][:, 0:kw], ACT.Relu, scale=rsc).then_inc(relu_done, 1)

                relu_head(0, 0)
                relu_head(1, 1)
                with act.Fori(1, IH // 2) as i:
                    relu_head(2 * i, 0)
                    relu_head(2 * i + 1, 1)
                base += IH

            act.wait_ge(nrm, 5)
            nc.scalar.activation(sdn, ssq, ACT.Sqrt).then_inc(n_sqrt, 1)
            act.wait_ge(kc_done, 1)
            copy(val[:, 0], kc[:, :, KVR:2 * KVR], K_S).then_inc(v_hi, 1)
            act.wait_ge(g_sub, 1)
            nc.scalar.activation(gwork[:, :, 0:E], gl, ACT.Exp).then_inc(g_exp, 1)
            for job, (dst, s) in enumerate(((qlT[:, 0], QL_S), (qlT[:, 2], QL_S), (keyT[:, 0, 0], K_S),
                                            (keyT[:, 0, 1], K_S), (hwT[:, 0], HW_S * SCALING))):
                for c in range(2):
                    act.wait_ge(tr_mm, 2 * job + c + 1)
                    copy(dst[:, c * CH:(c + 1) * CH], psT[c][:], s).then_inc(tr_hi, 1)

            with act.Fori(0, NP // 2) as i:
                for u in range(2):
                    p = 2 * i + u
                    act.wait_ge(qw_mm, p + 1)
                    copy(w1hi[:, p, 128:256], psS[u][:, 0:128], WQ_S).then_inc(qw_hi, 1)
                    copy(w2s[:, p, 128:256], psS[u][:, 128:256], WQ_S).then_inc(qw_hi, 1)
                    act.wait_ge(ld_qw[u], 48 * i + 48)
                    copy(w1hi[:, p, 0:128], pe_s[:, u, 0, :], WQ_S).then_inc(qw_hi, 1)
                    copy(w2s[:, p, 0:128], pe_s[:, u, 1, :], WQ_S).then_inc(qw_hi, 1)
            barrier(act, 2)

            qs = 1.0 / (QL_S * WQ_S)

            def q_evac(p, v, j):
                cs = slice((j % 2) * CH, (j % 2 + 1) * CH)
                if j < 2:
                    act.wait_ge(qp_mm, 2 * p + j + 1)
                    if j == 0 and not (isinstance(p, int) and p == 0):
                        act.wait_ge(rot, 3 * p)
                    copy(raw[:, cs], psM[:], qs * Q_S).then_inc(raw_done, 1)
                else:
                    act.wait_ge(qa_mm, 2 * p + j - 1)
                    copy(Q[64:128, v, 0, 0, cs], psM[64:128, :], qs * Q_S).then_inc(qa_hi, 1)
                    copy(Q[0:64, v, 0, 1, cs], psM[0:64, :], qs * Q_S).then_inc(qa_hi, 1)

            def exp_step(p, h, k):
                head = 2 * p + h
                step = 8 * head + k
                kw = P * NB[k]
                act.wait_ge(max_done, step + 1)
                nc.scalar.activation(pr[:, k % 2, 0:kw], pr[:, k % 2, 0:kw], ACT.Exp, bias=nmax[:, k % 2:k % 2 + 1],
                                     scale=-1.0, accum_out=rsum[:, h, k:k + 1]).then_inc(exp_done, 1)

            def p_hi_step(p, h, k):
                head = 2 * p + h
                for c in range(NCH[k]):
                    w = P * min(4, NB[k] - 4 * c)
                    act.wait_ge(t_mm, chunks_before(head, k) + c + 1)
                    if c == 0 and not (isinstance(head, int) and 8 * head + k < 2):
                        act.wait_ge(av_mm, 8 * head + k - 1)
                    copy(pT[:, k % 2, 0, c * CH:c * CH + w], psT[(CUM[k] + c) % 2][:, 0:w], PR_S).then_inc(p_hi, 1)

            def ot_evac(p, c):
                act.wait_ge(ot_mm, 2 * p + c + 1)
                copy(big[:, 0, p, c * CH:(c + 1) * CH], psM[:], O_S / (PR_S * K_S)).then_inc(ot_hi, 1)

            def pair(p, v, first, last_pair):
                for s in range(16):
                    h, k = s // 8, s % 8
                    p_hi_step(p, h, k)
                    if s < 15:
                        exp_step(p, (s + 1) // 8, (s + 1) % 8)
                    elif not last_pair:
                        exp_step(p + 1, 0, 0)
                    if not first and s in (3, 4):
                        ot_evac(p - 1, s - 3)
                    if not last_pair and s in (5, 6, 8, 10):
                        q_evac(p + 1, 1 - v, {5: 0, 6: 1, 8: 2, 10: 3}[s])

            for j in range(4):
                q_evac(0, 0, j)
            exp_step(0, 0, 0)
            pair(0, 0, True, False)
            with act.Fori(0, NP // 2 - 1) as i:
                pair(2 * i + 1, 1, False, False)
                pair(2 * i + 2, 0, False, False)
            pair(NP - 1, 1, False, True)
            ot_evac(NP - 1, 0)
            ot_evac(NP - 1, 1)
            barrier(act, 3)

            with act.Fori(0, NP // 2) as i:
                for u in range(2):
                    act.wait_ge(vo_mm, 2 * i + u + 1)
                    copy(wvo[:, 0, 2 * i + u, :], psT[u][:], WVO_S).then_inc(vo_hi, 1)

        @block.vector
        def _(dve):
            v = nc.vector
            count = {}

            def link(ins, s=nrm):
                count[s] = count.get(s, 0) + 1
                ins.then_inc(s, 1)
                dve.wait_ge(s, count[s])

            def low(dst, src, scale, hi):
                return v.scalar_tensor_tensor(out=dst, in0=src, scalar=scale, in1=hi, op0=ALU.mult, op1=ALU.subtract)

            for c in range(2):
                dve.wait_ge(ld_x[c], 16)
                with dve.Fori(4 * c, 4 * c + 4) as t:
                    v.bn_stats(st[:, t, :], x_sb[:, t, :]).then_inc(st_done, 1)
            dve.wait_ge(st_done, NT)
            for t in range(NT):
                v.bn_aggr(mv[:, t, :], st[:, t, :]).then_inc(st_done, 1)
            dve.wait_ge(st_done, 2 * NT)
            v.tensor_scalar(ve, mv[:, :, 1], EPS, None, ALU.add).then_inc(ve_done, 1)
            dve.wait_ge(wc_hi, 3)
            low(wcp[:, 1].rearrange("p k n -> p (k n)"), wc.rearrange("p k n -> p (k n)"), W_S,
                wcp[:, 0].rearrange("p k n -> p (k n)")).then_inc(wc_lo, 1)
            low(wikp[:, 1].rearrange("p k n -> p (k n)"), wk32.rearrange("p k n -> p (k n)"), W_S,
                wikp[:, 0].rearrange("p k n -> p (k n)")).then_inc(wc_lo, 1)
            low(bmp[:, 1, :], bm32, B_S, bmp[:, 0, :]).then_inc(wc_lo, 1)
            dve.wait_ge(sd_done, 1)
            v.reciprocal(rstd, sd).then_inc(rs_done, 1)
            dve.wait_ge(rs_done, 1)

            def rows_n(t, u, first):
                if not first:
                    dve.wait_ge(xT_done, t - 1)
                v.tensor_scalar(xn[:, u, :], x_sb[:, t, :], mv[:, t, 0:1], rstd[:, ds(t, 1)],
                                ALU.subtract, ALU.mult).then_inc(xn_done, 1)

            def rows_lo(t, u):
                dve.wait_ge(xhi_done, t + 1)
                low(xnT[:, 1, :, ds(t * P, P)], psT[u][:].rearrange("p (k q) -> p k q", k=KT), X_S,
                    xnT[:, 0, :, ds(t * P, P)]).then_inc(xlo_done, 1)

            def rows_pair(i, first):
                rows_n(2 * i, 0, first)
                rows_n(2 * i + 1, 1, first)
                rows_lo(2 * i, 0)
                rows_lo(2 * i + 1, 1)

            rows_pair(0, True)
            with dve.Fori(1, NT // 2) as i:
                rows_pair(i, False)
            barrier(dve, 1)

            sc = IQ_S / (X_S * W_S)
            for c in range(2):
                dve.wait_ge(ik_hi, c + 1)
                low(ikT[:, 1, c * CH:(c + 1) * CH], psT[c][:], sc, ikT[:, 0, c * CH:(c + 1) * CH]).then_inc(ik_lo, 1)
            with dve.Fori(0, IH // 2) as i:
                for u in range(2):
                    for c in range(2):
                        dve.wait_ge(iq_hi, 4 * i + 2 * u + c + 1)
                        low(iq[:, 1, 2 * i + u, c * CH:(c + 1) * CH], psS[u][:, c * CH:(c + 1) * CH], sc,
                            iq[:, 0, 2 * i + u, c * CH:(c + 1) * CH]).then_inc(iq_lo, 1)

            dve.wait_ge(idx_init, 2)
            base = 0
            for t in range(NT - 1, 0, -1):
                row = bias[:, TOFF[t]:TOFF[t + 1]]

                def acc(n, u):
                    dve.wait_ge(relu_done, base + n + 1)
                    if not (isinstance(n, int) and base + n == 0):
                        dve.wait_ge(acc_done, base + n)
                    v.scalar_tensor_tensor(out=row, in0=relu[:, u, 0:P * (t + 1)], scalar=proj[:, t, ds(C_IW + n, 1)],
                                           in1=row, op0=ALU.mult, op1=ALU.add).then_inc(acc_done, 1)

                acc(0, 0)
                acc(1, 1)
                with dve.Fori(1, IH // 2) as i:
                    acc(2 * i, 0)
                    acc(2 * i + 1, 1)
                base += IH
                dve.wait_ge(acc_done, base)
                rounds = TOPK // 8
                done = rounds * (NT - 1 - t)
                with dve.Fori(0, rounds) as r:
                    v.max(m8[:], row).then_inc(tk_max, 1)
                    wait_alone(dve, tk_max, done + 1 + r)
                    v.match_replace(out=row, in_to_replace=m8[:], in_values=row, imm_value=TAKEN).then_inc(tk_rep, 1)
                    wait_alone(dve, tk_rep, done + 1 + r)
                v.tensor_scalar(row, row, HALF_TAKEN, NEG, ALU.is_gt, ALU.mult).then_inc(mask_done, 1)

            pq = proj[:, :, C_Q:C_Q + QR]
            pkv = proj[:, :, C_KV:C_KV + KVR]
            link(v.tensor_tensor(tmp, pq, pq, ALU.mult))
            link(v.tensor_reduce(ssq[:, 0], tmp, AX.X, ALU.add))
            link(v.tensor_tensor(tmp[:, :, 0:KVR], pkv, pkv, ALU.mult))
            link(v.tensor_reduce(ssq[:, 1], tmp[:, :, 0:KVR], AX.X, ALU.add))
            v.tensor_scalar(ssq[:, 0], ssq[:, 0], 1.0 / QR, EPS, ALU.mult, ALU.add).then_inc(st_done, 1)
            dve.wait_ge(st_done, 2 * NT + 1)
            link(v.tensor_scalar(ssq[:, 1], ssq[:, 1], 1.0 / KVR, EPS, ALU.mult, ALU.add))
            dve.wait_ge(n_sqrt, 1)
            link(v.reciprocal(rsn, sdn))
            link(v.tensor_tensor(tmp, pq, rsn[:, 0].unsqueeze(2).broadcast_to([P, NT, QR]), ALU.mult))
            link(v.tensor_tensor(qn[:, :, 0:QR], tmp, qnw[:].unsqueeze(1).broadcast_to([P, NT, QR]), ALU.mult))
            v.tensor_copy(qn[:, :, QR:256], qn[:, :, P:QR]).then_inc(qn_done, 1)
            link(v.tensor_tensor(tmp[:, :, 0:KVR], pkv, rsn[:, 1].unsqueeze(2).broadcast_to([P, NT, KVR]), ALU.mult))
            link(v.tensor_tensor(kc[:, :, KVR:2 * KVR], tmp[:, :, 0:KVR], kvw[:].unsqueeze(1).broadcast_to([P, NT, KVR]), ALU.mult))
            kp = proj[:, :, C_KV + KVR:C_KV + KVR + ROPE].rearrange("p t (j two) -> p t j two", two=2)
            t4 = tmp[:, :, 0:128].rearrange("p t (f j) -> p t f j", f=4)
            link(v.tensor_tensor(t4[:, :, 0], kp[:, :, :, 0], ck, ALU.mult))
            link(v.tensor_tensor(t4[:, :, 1], kp[:, :, :, 1], sk, ALU.mult))
            link(v.tensor_tensor(t4[:, :, 2], kp[:, :, :, 1], ck, ALU.mult))
            link(v.tensor_tensor(t4[:, :, 3], kp[:, :, :, 0], sk, ALU.mult))
            ko = kc[:, :, 0:ROPE].rearrange("p t (j two) -> p t j two", two=2)
            link(v.tensor_tensor(ko[:, :, :, 0], t4[:, :, 0], t4[:, :, 1], ALU.subtract))
            link(v.tensor_tensor(ko[:, :, :, 1], t4[:, :, 2], t4[:, :, 3], ALU.add))
            v.tensor_copy(kc[:, :, 2 * KVR:3 * KVR], kc[:, :, 0:ROPE]).then_inc(kc_done, 1)
            dve.wait_ge(v_hi, 1)
            low(val[:, 1], kc[:, :, KVR:2 * KVR], K_S, val[:, 0])

            link(v.tensor_tensor(gl, proj[:, :, C_R:C_R + E], rbs.unsqueeze(1).broadcast_to([P, NT, E]), ALU.add))
            link(v.tensor_reduce(gm, gl, AX.X, ALU.max))
            v.tensor_tensor(gl, gl, gm.unsqueeze(2).broadcast_to([P, NT, E]), ALU.subtract).then_inc(g_sub, 1)
            v.memset(gwork[:, :, E:2 * E], -1.0).then_inc(st_done, 1)
            v.memset(grep[:], -1.0).then_inc(st_done, 1)
            dve.wait_ge(st_done, 2 * NT + 3)
            dve.wait_ge(g_exp, 1)
            for t in range(NT):
                ins = v.max(gmx[:, t, :], gwork[:, t, 0:E])
                if t < NT - 1:
                    ins.then_inc(st_done, 1)
            link(ins)
            dve.wait_ge(st_done, 3 * NT + 2)
            link(v.tensor_copy(grep[:, :, 0:2], gmx[:, :, 0:2]))
            for t in range(NT):
                ins = v.match_replace(out=gout[:, t, :], in_to_replace=grep[:, t, :], in_values=gwork[:, t, :], imm_value=2.0)
                if t < NT - 1:
                    ins.then_inc(st_done, 1)
            link(ins)
            dve.wait_ge(st_done, 4 * NT + 1)
            link(v.tensor_scalar(gout[:, :, 0:E], gout[:, :, 0:E], 2.0, None, ALU.is_ge))
            link(v.tensor_tensor(gw, gout[:, :, 0:E], gwork[:, :, 0:E], ALU.mult))
            link(v.tensor_tensor(gden, gmx[:, :, 0], gmx[:, :, 1], ALU.add))
            link(v.reciprocal(grd, gden))
            link(v.tensor_tensor(gw, gw, grd.unsqueeze(2).broadcast_to([P, NT, E]), ALU.mult))
            for t in range(NT):
                ins = v.tensor_tensor(tmp[:, t, 0:P].rearrange("p (e r) -> p e r", e=E),
                                      proj[:, t, C_H:C_H + P].rearrange("p (e r) -> p e r", e=E),
                                      gw[:, t, :].unsqueeze(2).broadcast_to([P, E, R]), ALU.mult)
                if t < NT - 1:
                    ins.then_inc(st_done, 1)
            dve.wait_ge(st_done, 5 * NT)
            ins.then_inc(hw_done, 1)

            for job, (dh, dl, s, rows_) in enumerate((
                    (qlT[:, 0], qlT[:, 1], QL_S, P), (qlT[:, 2], qlT[:, 3], QL_S, 64), (keyT[:, 0, 0], keyT[:, 1, 0], K_S, P),
                    (keyT[:, 0, 1], keyT[:, 1, 1], K_S, P), (hwT[:, 0], hwT[:, 1], HW_S * SCALING, P))):
                for c in range(2):
                    dve.wait_ge(tr_hi, 2 * job + c + 1)
                    low(dl[0:rows_, c * CH:(c + 1) * CH], psT[c][0:rows_, :], s, dh[0:rows_, c * CH:(c + 1) * CH]).then_inc(tr_lo, 1)

            with dve.Fori(0, NP // 2) as i:
                for u in range(2):
                    p = 2 * i + u
                    dve.wait_ge(qw_hi, 8 * i + 4 * u + 4)
                    low(w1lo[:, p, 128:256], psS[u][:, 0:128], WQ_S, w1hi[:, p, 128:256]).then_inc(qw_lo, 1)
                    low(w2s[64:128, p, 128:256], psS[u][64:128, 128:256], WQ_S, w2s[64:128, p, 128:256]).then_inc(qw_lo, 1)
                    low(w1lo[:, p, 0:128], pe_s[:, u, 0, :], WQ_S, w1hi[:, p, 0:128]).then_inc(qw_lo, 1)
                    low(w2s[64:128, p, 0:128], pe_s[64:128, u, 1, :], WQ_S, w2s[64:128, p, 0:128]).then_inc(qw_lo, 1)
            barrier(dve, 2)

            c_s = (NOPE + ROPE) ** -0.5 / (Q_S * K_S)
            qs = Q_S / (QL_S * WQ_S)

            def q_low(p, v_, j):
                cs = slice((j % 2) * CH, (j % 2 + 1) * CH)
                dve.wait_ge(qa_hi, 4 * p + 2 * j - 2)
                low(Q[64:128, v_, 1, 0, cs], psM[64:128, :], qs, Q[64:128, v_, 0, 0, cs]).then_inc(qa_lo, 1)
                low(Q[0:64, v_, 1, 1, cs], psM[0:64, :], qs, Q[0:64, v_, 0, 1, cs]).then_inc(qa_lo, 1)

            def row_max(p, h, k):
                head = 2 * p + h
                step = 8 * head + k
                t, kw = ORDER[k], P * NB[k]
                wait_alone(dve, s_mm, step + 1)
                if not (isinstance(head, int) and step < 2):
                    prev = chunks_before(head, k - 1) if k else chunks_before(head - 1, 7)
                    wait_alone(dve, t_mm, prev)
                    wait_alone(dve, exp_done, step - 1)
                v.tensor_tensor_reduce(out=pr[:, k % 2, 0:kw], in0=psS[k % 2][:, 0:kw], in1=bias[:, TOFF[t]:TOFF[t + 1]],
                                       scale=-c_s, scalar=3e38, op0=ALU.add, op1=ALU.min,
                                       accum_out=nmax[:, k % 2:k % 2 + 1]).then_inc(max_done, 1)

            def p_low(p, h, k):
                head = 2 * p + h
                for c in range(NCH[k]):
                    w = P * min(4, NB[k] - 4 * c)
                    dve.wait_ge(p_hi, chunks_before(head, k) + c + 1)
                    low(pT[:, k % 2, 1, c * CH:c * CH + w], psT[(CUM[k] + c) % 2][:, 0:w], PR_S,
                        pT[:, k % 2, 0, c * CH:c * CH + w]).then_inc(p_lo, 1)

            def head_out(p, h):
                head = 2 * p + h
                dve.wait_ge(exp_done, 8 * head + 8)
                v.reciprocal(rinv, rsum[:, h, :]).then_inc(ri_done, 1)
                dve.wait_ge(av_mm, 8 * head + 8)
                dve.wait_ge(ri_done, head + 1)
                if not (isinstance(p, int) and p == 0):
                    dve.wait_ge(ot_mm, 2 * p)
                v.tensor_tensor(op[:, :, h * KVR:(h + 1) * KVR], psO[:].rearrange("p (k r) -> p k r", k=NT),
                                rinv.unsqueeze(2).broadcast_to([P, NT, KVR]), ALU.mult).then_inc(o_done, 1)

            def ot_low(p, c):
                dve.wait_ge(ot_hi, 2 * p + c + 1)
                low(big[:, 1, p, c * CH:(c + 1) * CH], psM[:], O_S / (PR_S * K_S),
                    big[:, 0, p, c * CH:(c + 1) * CH]).then_inc(ot_lo, 1)

            def pair(p, v_, first, last_pair):
                for s in range(16):
                    h, k = s // 8, s % 8
                    p_low(p, h, k)
                    if s < 14:
                        row_max(p, (s + 2) // 8, (s + 2) % 8)
                    elif not last_pair:
                        row_max(p + 1, 0, s - 14)
                    if k == 0 and not (first and s == 0):
                        head_out(p if h else p - 1, 1 - h)
                    if not first and s in (3, 4):
                        ot_low(p - 1, s - 3)
                    if not last_pair and s in (8, 10):
                        q_low(p + 1, 1 - v_, {8: 2, 10: 3}[s])

            for j in (2, 3):
                q_low(0, 0, j)
            row_max(0, 0, 0)
            row_max(0, 0, 1)
            pair(0, 0, True, False)
            with dve.Fori(0, NP // 2 - 1) as i:
                pair(2 * i + 1, 1, False, False)
                pair(2 * i + 2, 0, False, False)
            pair(NP - 1, 1, False, True)
            head_out(NP - 1, 1)
            ot_low(NP - 1, 0)
            ot_low(NP - 1, 1)
            barrier(dve, 3)

            with dve.Fori(0, NP // 2) as i:
                for u in range(2):
                    dve.wait_ge(vo_hi, 2 * i + u + 1)
                    low(wvo[:, 1, 2 * i + u, :], psT[u][:], WVO_S, wvo[:, 0, 2 * i + u, :]).then_inc(vo_lo, 1)

            def final(t, u, first):
                dve.wait_ge(fin_mm, t + 1)
                dve.wait_ge(ld_xr[u], 16 if first else 8 * (t - u) + 16)
                if not first:
                    dve.wait_ge(stored[u], 8 * (t - u))
                v.scalar_tensor_tensor(out=res[:, u], in0=psS[u][:, 0:CH], scalar=1.0 / OUT_S, in1=xr[:, u],
                                       op0=ALU.mult, op1=ALU.add).then_inc(fin_done, 1)

            final(0, 0, True)
            final(1, 1, True)
            with dve.Fori(1, NT // 2) as i:
                final(2 * i, 0, False)
                final(2 * i + 1, 1, False)

        @block.gpsimd
        def _(pool):
            g = nc.gpsimd
            g.memset(bias[:], 0.0).then_inc(idx_init, 1)
            pool.wait_ge(idx_init, 1)
            pool.wait_ge(ld_c, 16 * n_const)
            for t in range(NT):
                ins = g.tensor_copy(bias[:, TOFF[t + 1] - P:TOFF[t + 1]], causal[:])
            ins.then_inc(idx_init, 1)
            barrier(pool, 1)

            def wq_parts(n, u, first):
                wait_alone(pool, ld_wq[u], 16 if first else 8 * (n - u) + 16)
                g.tensor_scalar(wq32[:, u], wq32[:, u], W_S, 1.0, ALU.mult, ALU.mult).then_inc(wq_sc, 1)
                wait_alone(pool, wq_sc, n + 1)
                if not first:
                    wait_alone(pool, iq_mm, 2 * n - 2)
                g.tensor_copy(wqp[:, u, 0], wq32[:, u]).then_inc(wq_hi, 1)
                pool.wait_ge(wq_hi, n + 1)
                g.tensor_tensor(wqp[:, u, 1], wq32[:, u], wqp[:, u, 0], ALU.subtract).then_inc(wq_lo, 1)

            wq_parts(0, 0, True)
            wq_parts(1, 1, True)
            with pool.Fori(1, IH // 2) as i:
                wq_parts(2 * i, 0, False)
                wq_parts(2 * i + 1, 1, False)
            barrier(pool, 2)

            pool.wait_ge(ld_cq, 32)

            def rope(p, v_):
                pool.wait_ge(sw_done, 32 * p + 32)
                g.tensor_tensor(swp, swp, sq[:], ALU.mult).then_inc(rot, 1)
                g.tensor_tensor(raw, raw, cq[:], ALU.mult).then_inc(rot, 1)
                pool.wait_ge(rot, 3 * p + 2)
                g.tensor_tensor(rt, raw, swp, ALU.add).then_inc(rot, 1)
                wait_alone(pool, rot, 3 * p + 3)
                if not (isinstance(p, int) and p < 2):
                    wait_alone(pool, s_mm, 16 * p - 16)
                g.tensor_copy(Q[0:64, v_, 0, 0, :], rt[0:64, :]).then_inc(q_rot, 1)
                g.tensor_copy(Q[64:128, v_, 0, 1, :], rt[64:128, :]).then_inc(q_rot, 1)
                pool.wait_ge(q_rot, 4 * p + 2)
                g.tensor_tensor(Q[0:64, v_, 1, 0, :], rt[0:64, :], Q[0:64, v_, 0, 0, :], ALU.subtract).then_inc(q_rot, 1)
                g.tensor_tensor(Q[64:128, v_, 1, 1, :], rt[64:128, :], Q[64:128, v_, 0, 1, :], ALU.subtract).then_inc(q_rot, 1)

            rt = view(11264, S)
            rope(0, 0)
            rope(1, 1)
            with pool.Fori(1, NP // 2) as i:
                rope(2 * i, 0)
                rope(2 * i + 1, 1)
            barrier(pool, 3)


def kernel(**inputs):
    import concourse.bacc as _bacc
    from concourse.bass_utils import run_bass_kernel_spmd as _run

    def host(name):
        return np.asarray(inputs["L0_" + name])

    x = host("attn_hidden_states").reshape(S, HID)
    qb = host("attn_q_b_w").reshape(QR, H, NOPE + ROPE)
    kvb = host("attn_kv_b_w").reshape(KVR, H, NOPE + VD)
    twice = np.r_[0:QR, P:QR]
    freq = (np.float32(1.0) / np.float32(10000.0) ** (np.arange(0, ROPE, 2, dtype=np.float32) / np.float32(ROPE))).astype(np.float32)
    ang = np.arange(S, dtype=np.float32)[:, None] * freq[None, :]
    cos, sin = np.cos(ang).astype(np.float32), np.sin(ang).astype(np.float32)
    cos_rows = np.repeat(cos.T, 2, axis=0)
    sin_rows = np.repeat(sin.T, 2, axis=0) * np.tile(np.array([-1.0, 1.0], np.float32), ROPE // 2)[:, None]
    arrays = {
        "x": x,
        "wcat": np.concatenate([host("attn_q_a_w"), host("attn_kv_a_w"), host("attn_idx_weights_w"),
                                host("ffn_router_w").T, host("ffn_A").reshape(E * R, HID).T], axis=1),
        "wik": host("attn_idx_wk_w"),
        "wiq": host("attn_idx_wq_w"),
        "qbT": qb[twice, :, :NOPE].transpose(2, 1, 0),
        "wkT": kvb[:, :, :NOPE].transpose(2, 1, 0),
        "wvT": kvb[:, :, NOPE:].transpose(2, 1, 0),
        "qpe": qb[twice, :, NOPE:].reshape(2, P, H, ROPE).transpose(1, 0, 2, 3),
        "ow": host("attn_o_w"),
        "bm": host("ffn_Bm").transpose(0, 2, 1).reshape(E * R, HID),
        "qnorm": np.broadcast_to(host("attn_q_a_norm_w"), (P, QR)),
        "kvnorm": np.broadcast_to(host("attn_kv_a_norm_w"), (P, KVR)),
        "rbias": np.broadcast_to(host("ffn_router_b"), (P, E)),
        "cosq": np.concatenate([cos_rows, cos_rows]),
        "sinq": np.concatenate([sin_rows, sin_rows]),
        "cosk": cos,
        "sink": sin,
        "ident": np.eye(P, dtype=np.float32),
        "causal": np.triu(np.full((P, P), NEG, np.float32), 1),
    }
    nc = _bacc.Bacc("TRN2", target_bir_lowering=False, num_devices=1)
    given, args = {}, []
    for name, a in arrays.items():
        given["in_" + name] = np.ascontiguousarray(a)
        args.append(nc.dram_tensor("in_" + name, a.shape, F32, kind="ExternalInput").ap())
    result = nc.dram_tensor("out_0", (S, HID), F32, kind="ExternalOutput").ap()
    block_kernel(nc, *args, result)
    r = _run(nc, [given], core_ids=[0])
    return r.results[0]["out_0"].reshape(1, S, HID)
```

```python
from contextlib import ExitStack

import numpy as np

import concourse.bass as bass
from concourse import mybir

F32 = mybir.dt.float32
F16 = mybir.dt.float16
ALU = mybir.AluOpType
ACT = mybir.ActivationFunctionType
AX = mybir.AxisListType

P = 128
S, HID = 1024, 512
NT = S // P
KT = HID // P
H, NOPE, ROPE, VD = 32, 128, 64, 128
NP = H // 2
QR, KVR = 192, 64
IH, ID, TOPK = 16, 128, 128
E, R = 8, 16
EPS = 1e-5
SCALING = 8.0 / R

C_Q, C_KV, C_IW, C_R, C_H = 0, QR, QR + KVR + ROPE, QR + KVR + ROPE + IH, QR + KVR + ROPE + IH + E
CW = C_H + E * R

NEG = -1e30
TAKEN = -3e38
HALF_TAKEN = -2e38

X_S, W_S, IQ_S, QL_S, WQ_S, Q_S, K_S = 64.0, 128.0, 32.0, 32.0, 64.0, 16.0, 16.0
PR_S, O_S, WVO_S, HW_S, B_S = 1024.0, 16.0, 256.0, 32.0, 128.0
OUT_S = O_S * WVO_S
assert HW_S * B_S == OUT_S

ORDER = [7, 0, 6, 1, 5, 2, 4, 3]
GROUPS = [[7, 6], [5, 4], [3, 2, 1]]
CH = 512
ARENA = 15040


def block_kernel(nc, x, wcat, wik, wiq, qbT, wkT, wvT, qpe, ow, bm, qnorm, kvnorm, rbias,
                 cosq, sinq, cosk, sink, ident_d, causal_d, out):
    with ExitStack() as ctx:
        def sb(name, shape, dt=F32):
            return ctx.enter_context(nc.sbuf_tensor(name, shape, dt))

        def sem(name):
            return ctx.enter_context(nc.semaphore(name))

        big = sb("big", [P, 2, NP, S], F16)
        iq = big[:, :, 0:IH, :]
        w1hi = sb("w1hi", [P, NP, 256], F16)
        w1lo = sb("w1lo", [P, NP, 256], F16)
        w2s = sb("w2s", [P, NP, 256], F16)
        TOFF = [P * t * (t + 1) // 2 for t in range(NT + 1)]
        bias = sb("bias", [P, TOFF[NT]])
        cq = sb("cq", [P, S])
        sq = sb("sq", [P, S])
        keyT = sb("keyT", [P, 2, 2, S], F16)
        val = sb("val", [P, 2, NT, KVR], F16)
        qlT = sb("qlT", [P, 4, S], F16)
        hwT = sb("hwT", [P, 2, S], F16)
        bmp = sb("bmp", [P, 2, HID], F16)
        ikT = sb("ikT", [P, 2, S], F16)
        ident = sb("ident", [P, P])
        causal = sb("causal", [P, P])
        m8 = sb("m8", [P, 3, 8])
        small = sb("small", [P, 512])
        arena = sb("arena", [P, ARENA])

        def view(at, n, dt=F32):
            words = n if dt == F32 else n // 2
            assert at + words <= ARENA
            v = arena[:, at:at + words]
            return v if dt == F32 else v.bitcast(dt)

        half0 = big[:, 0, :, :].rearrange("p a b -> p (a b)")
        half1 = big[:, 1, :, :].rearrange("p a b -> p (a b)")
        x_sb = half0[:, 0:2 * NT * HID].bitcast(F32).rearrange("p (t d) -> p t d", t=NT)
        xn = half0[:, 8192:8192 + 4 * HID].bitcast(F32).rearrange("p (u d) -> p u d", u=2)
        wc = half1[:, 0:2 * KT * CW].bitcast(F32).rearrange("p (k n) -> p k n", k=KT)
        wcp = half1[:, 2 * KT * CW:4 * KT * CW].rearrange("p (s k n) -> p s k n", s=2, k=KT)
        wk32 = half1[:, 4 * KT * CW:4 * KT * CW + 2 * KT * ID].bitcast(F32).rearrange("p (k n) -> p k n", k=KT)
        bm32 = half1[:, 4 * KT * CW + 2 * KT * ID:4 * KT * CW + 2 * KT * ID + 2 * HID].bitcast(F32)
        xnT = view(0, 2 * KT * S, F16).rearrange("p (s k q) -> p s k q", s=2, k=KT)
        proj = view(4096, NT * CW).rearrange("p (t n) -> p t n", t=NT)
        o = 4096 + NT * CW
        qn = view(o, NT * 256).rearrange("p (t n) -> p t n", t=NT)
        relu = view(o, 2 * S).rearrange("p (u n) -> p u n", u=2)
        kc = view(o + 2048, NT * 192).rearrange("p (t n) -> p t n", t=NT)
        tmp = view(o + 2048 + 1536, NT * QR).rearrange("p (t n) -> p t n", t=NT)
        o += 2048 + 1536 + 1536
        wq32 = view(o, 2 * HID).rearrange("p (u k n) -> p u k n", u=2, k=KT)
        wqp = view(o + 1024, 4 * HID, F16).rearrange("p (u s k n) -> p u s k n", u=2, s=2, k=KT)
        wikp = keyT[:, 0, 0, :].rearrange("p (s k n) -> p s k n", s=2, k=KT)
        qb_s = view(0, 2 * 512).rearrange("p (u h r) -> p u h r", u=2, h=2)
        wk_s = view(1024, 2 * 128).rearrange("p (u h r) -> p u h r", u=2, h=2)
        pe_s = view(1280, 2 * 256).rearrange("p (u k n) -> p u k n", u=2, k=2)
        Q = view(0, 8 * S, F16).rearrange("p (v s h q) -> p v s h q", v=2, s=2, h=2)
        raw = view(4096, S)
        swp = view(4096 + S, S)
        rt = view(6144, S)
        pr = view(7168, 4 * S).rearrange("p (u k) -> p u k", u=4)
        pT = view(11264, 4 * S, F16).rearrange("p (u s k) -> p u s k", u=2, s=2)
        op = view(13312, NT * P).rearrange("p (k r) -> p k r", k=NT)
        wvo = view(0, 2 * NP * HID, F16).rearrange("p (s k n) -> p s k n", s=2, k=NP)
        ow_s = view(8192, 2 * 2 * HID).rearrange("p (u h n) -> p u h n", u=2, h=2)
        wv_s = view(10240, 2 * P).rearrange("p (u h r) -> p u h r", u=2, h=2)
        xr = view(10496, 2 * HID).rearrange("p (u n) -> p u n", u=2)
        res = view(10496 + 2 * HID, 2 * HID).rearrange("p (u n) -> p u n", u=2)

        st = small[:, 0:NT * 6].rearrange("p (t n) -> p t n", t=NT)
        mv = small[:, 48:64].rearrange("p (t n) -> p t n", t=NT)
        ve = small[:, 64:72]
        sd = small[:, 72:80]
        rstd = small[:, 80:88]
        ssq = small[:, 88:104].rearrange("p (w t) -> p w t", w=2)
        sdn = small[:, 104:120].rearrange("p (w t) -> p w t", w=2)
        rsn = small[:, 120:136].rearrange("p (w t) -> p w t", w=2)
        gm = small[:, 136:144]
        gden = small[:, 144:152]
        grd = small[:, 152:160]
        gl = small[:, 160:224].rearrange("p (t e) -> p t e", t=NT)
        gmx = small[:, 224:288].rearrange("p (t e) -> p t e", t=NT)
        gw = small[:, 288:352].rearrange("p (t e) -> p t e", t=NT)
        rbs = small[:, 352:360]
        nmax = small[:, 360:364]
        rsum = small[:, 364:380].rearrange("p (h t) -> p h t", h=2)
        rinv = small[:, 380:388]
        gwork = sb("gwork", [P, NT, 16])
        grep = sb("grep", [P, NT, 8])
        gout = sb("gout", [P, NT, 16])
        qnw = sb("qnw", [P, QR])
        kvw = sb("kvw", [P, KVR])
        ckv = w2s[:].rearrange("p a b -> p (a b)")
        ck = ckv[:, 0:512].bitcast(F32).rearrange("p (t j) -> p t j", t=NT)
        sk = ckv[:, 512:1024].bitcast(F32).rearrange("p (t j) -> p t j", t=NT)

        psS = [ctx.enter_context(nc.psum_tensor(f"psS{u}", [P, S], F32)) for u in range(2)]
        psT = [ctx.enter_context(nc.psum_tensor(f"psT{u}", [P, CH], F32)) for u in range(3)]
        psO = ctx.enter_context(nc.psum_tensor("psO", [P, CH], F32))

        ld_x = [sem("ld_x0"), sem("ld_x1")]
        ld_wc = sem("ld_wc"); ld_c = sem("ld_c"); ld_cq = sem("ld_cq")
        wc_hi = sem("wc_hi"); wc_lo = sem("wc_lo")
        st_done = sem("st_done"); ve_done = sem("ve_done"); sd_done = sem("sd_done"); rs_done = sem("rs_done")
        xn_done = sem("xn_done"); xT_done = sem("xT_done"); xhi_done = sem("xhi_done"); xlo_done = sem("xlo_done")
        pj_mm = sem("pj_mm"); pj_done = sem("pj_done")
        bar = sem("bar")
        wik_lo = sem("wik_lo")
        ik_mm = sem("ik_mm"); ik_hi = sem("ik_hi"); ik_lo = sem("ik_lo")
        ld_wq = [sem("ld_wq0"), sem("ld_wq1")]
        wq_sc = sem("wq_sc"); wq_hi = sem("wq_hi"); wq_lo = sem("wq_lo")
        iq_mm = sem("iq_mm"); iq_hi = sem("iq_hi"); iq_lo = sem("iq_lo")
        idx_init = sem("idx_init"); idx_mm = sem("idx_mm"); relu_done = sem("relu_done"); acc_done = sem("acc_done")
        tk_max = sem("tk_max"); tk_rep = sem("tk_rep"); mask_done = sem("mask_done")
        nrm = sem("nrm"); n_sqrt = sem("n_sqrt"); g_exp = sem("g_exp"); g_sub = sem("g_sub")
        tr_mm = sem("tr_mm"); tr_hi = sem("tr_hi"); tr_lo = sem("tr_lo"); v_hi = sem("v_hi")
        kc_done = sem("kc_done"); qn_done = sem("qn_done"); hw_done = sem("hw_done")
        ld_qw = [sem("ld_qw0"), sem("ld_qw1")]
        qw_mm = sem("qw_mm"); qw_hi = sem("qw_hi"); qw_lo = sem("qw_lo")
        s_mm = sem("s_mm"); max_done = sem("max_done"); exp_done = sem("exp_done")
        t_mm = sem("t_mm"); p_hi = sem("p_hi"); p_lo = sem("p_lo"); av_mm = sem("av_mm")
        ri_done = sem("ri_done"); o_done = sem("o_done")
        ot_mm = sem("ot_mm"); ot_hi = sem("ot_hi"); ot_lo = sem("ot_lo")
        qp_mm = sem("qp_mm"); qa_mm = sem("qa_mm"); raw_done = sem("raw_done"); qa_hi = sem("qa_hi"); qa_lo = sem("qa_lo")
        sw_done = sem("sw_done"); rot = sem("rot"); q_rot = sem("q_rot"); rope_h = sem("rope_h")
        ld_ow = [sem("ld_ow0"), sem("ld_ow1")]
        vo_mm = sem("vo_mm"); vo_hi = sem("vo_hi"); vo_lo = sem("vo_lo")
        ld_xr = [sem("ld_xr0"), sem("ld_xr1")]
        fin_mm = sem("fin_mm"); fin_done = sem("fin_done"); stored = [sem("stored0"), sem("stored1")]

        stood = {}

        def wait_alone(eng, semaphore, value):
            if eng not in stood:
                stood[eng] = sem(f"stood{len(stood)}")
            eng.wait_ge(semaphore, value).then_inc(stood[eng], 1)

        block = ctx.enter_context(nc.Block())
        ds = bass.ds

        def barrier(eng, n):
            eng.drain().then_inc(bar, 1)
            eng.wait_ge(bar, 5 * n)

        NB = [t + 1 for t in ORDER]
        NCH = [(b + 3) // 4 for b in NB]
        CUM = [sum(NCH[:k]) for k in range(9)]
        CPH = CUM[8]
        assert CPH % 2 == 0

        def chunks_before(head, k):
            return head * CPH + CUM[k]

        AHEAD = 3
        ROPE_AT = 8
        Q_AT, O_AT = {0: 0, 1: 1, 2: 2, 4: 3}, {5: 0, 6: 1}
        RING = []
        for s_ in range(16):
            RING += [("T", s_, c) for c in range(NCH[s_ % 8])]
            RING += [("Q", Q_AT[s_])] if s_ in Q_AT else []
            RING += [("O", O_AT[s_])] if s_ in O_AT else []
        RING_AT = {use: n for n, use in enumerate(RING)}
        USES = len(RING)
        assert USES % 3 == 0

        def bank_of(*use):
            return psT[RING_AT[use] % 3]

        n_const = 9

        @block.sync
        def _(sp):
            xv = x.rearrange("(t p) d -> p t d", p=P)
            sp.dma_start(x_sb[:, 0:4, :], xv[:, 0:4, :]).then_inc(ld_x[0], 16)
            sp.dma_start(x_sb[:, 4:8, :], xv[:, 4:8, :]).then_inc(ld_x[1], 16)
            sp.dma_start(wc, wcat.rearrange("(k p) n -> p k n", p=P)).then_inc(ld_wc, 16)
            sp.dma_start(wk32, wik.rearrange("(k p) n -> p k n", p=P)).then_inc(ld_c, 16)
            sp.dma_start(ident[:], ident_d).then_inc(ld_c, 16)
            sp.dma_start(causal[:], causal_d).then_inc(ld_c, 16)
            sp.dma_start(qnw[:], qnorm).then_inc(ld_c, 16)
            sp.dma_start(kvw[:], kvnorm).then_inc(ld_c, 16)
            sp.dma_start(rbs, rbias).then_inc(ld_c, 16)
            sp.dma_start(ck, cosk.rearrange("(t p) j -> p t j", p=P)).then_inc(ld_c, 16)
            sp.dma_start(sk, sink.rearrange("(t p) j -> p t j", p=P)).then_inc(ld_c, 16)
            sp.dma_start(bm32, bm).then_inc(ld_c, 16)
            sp.dma_start(cq[:], cosq).then_inc(ld_cq, 16)
            sp.dma_start(sq[:], sinq).then_inc(ld_cq, 16)
            barrier(sp, 1)

            wiq_v = wiq.rearrange("(k p) n -> p k n", p=P)

            def load_iq(n, u, first):
                if not first:
                    wait_alone(sp, wq_lo, n - 1)
                sp.dma_start(wq32[:, u], wiq_v[:, :, ds(n * ID, ID)]).then_inc(ld_wq[u], 16)

            load_iq(0, 0, True)
            load_iq(1, 1, True)
            with sp.Fori(1, IH // 2) as i:
                load_iq(2 * i, 0, False)
                load_iq(2 * i + 1, 1, False)

            wait_alone(sp, iq_mm, 2 * IH)

            def load_qw(p, u, first):
                if not first:
                    wait_alone(sp, qw_lo, 4 * p - 4)
                sp.dma_start(qb_s[:, u], qbT[:, ds(2 * p, 2), :]).then_inc(ld_qw[u], 16)
                sp.dma_start(wk_s[:, u], wkT[:, ds(2 * p, 2), :]).then_inc(ld_qw[u], 16)
                sp.dma_start(pe_s[:, u].rearrange("p k (h r) -> p k h r", h=2),
                             qpe[:, :, ds(2 * p, 2), :]).then_inc(ld_qw[u], 16)

            load_qw(0, 0, True)
            load_qw(1, 1, True)
            with sp.Fori(1, NP // 2) as i:
                load_qw(2 * i, 0, False)
                load_qw(2 * i + 1, 1, False)
            barrier(sp, 2)

            def swap(p):
                wait_alone(sp, raw_done, 2 * p + 2)
                if not (isinstance(p, int) and p == 0):
                    wait_alone(sp, rot, 3 * p)
                sp.dma_start(swp[0:P:2, :], raw[1:P:2, :]).then_inc(sw_done, 16)
                sp.dma_start(swp[1:P:2, :], raw[0:P:2, :]).then_inc(sw_done, 16)

            swap(0)
            with sp.Fori(1, NP) as p:
                swap(p)
            barrier(sp, 3)

            ow_v = ow.rearrange("(h d) n -> d h n", d=P)

            def load_ow(p, u, first):
                if not first:
                    wait_alone(sp, vo_mm, p - 1)
                sp.dma_start(ow_s[:, u], ow_v[:, ds(2 * p, 2), :]).then_inc(ld_ow[u], 16)
                sp.dma_start(wv_s[:, u], wvT[:, ds(2 * p, 2), :]).then_inc(ld_ow[u], 16)

            load_ow(0, 0, True)
            load_ow(1, 1, True)
            with sp.Fori(1, NP // 2) as i:
                load_ow(2 * i, 0, False)
                load_ow(2 * i + 1, 1, False)

            def rows(t, u, first):
                if not first:
                    wait_alone(sp, fin_done, t - 1)
                sp.dma_start(xr[:, u], x[ds(t * P, P), :]).then_inc(ld_xr[u], 16)

            def store(t, u):
                wait_alone(sp, fin_done, t + 1)
                sp.dma_start(out[ds(t * P, P), :], res[:, u]).then_inc(stored[u], 16)

            rows(0, 0, True)
            rows(1, 1, True)
            with sp.Fori(1, NT // 2) as i:
                store(2 * i - 2, 0)
                rows(2 * i, 0, False)
                store(2 * i - 1, 1)
                rows(2 * i + 1, 1, False)
            store(NT - 2, 0)
            store(NT - 1, 1)
            for u in range(2):
                wait_alone(sp, stored[u], 16 * NT // 2)

        @block.tensor
        def _(pe):
            mm = nc.tensor.matmul

            pe.wait_ge(ld_c, 16 * n_const)

            def rows_T(t, u, first):
                pe.wait_ge(xn_done, t + 1)
                if not first:
                    pe.wait_ge(xlo_done, t - 1)
                for k in range(KT):
                    last = nc.tensor.transpose(psT[u][:, k * P:(k + 1) * P], xn[:, u, k * P:(k + 1) * P], ident[:])
                last.then_inc(xT_done, 1)

            def rows_proj(t, u, first):
                pe.wait_ge(xlo_done, t + 1)
                if not first:
                    pe.wait_ge(pj_done, t - 1)
                ins = 0
                for k in range(KT):
                    for a, b in ((0, 0), (0, 1), (1, 0)):
                        last = mm(psS[u][:, 0:CW], xnT[:, a, k, ds(t * P, P)], wcp[:, b, k, :],
                                  start=ins == 0, stop=ins == 3 * KT - 1)
                        ins += 1
                last.then_inc(pj_mm, 1)

            def rows_pair(i, first):
                rows_T(2 * i, 0, first)
                rows_T(2 * i + 1, 1, first)
                if first:
                    pe.wait_ge(wc_lo, 1)
                rows_proj(2 * i, 0, first)
                rows_proj(2 * i + 1, 1, first)

            rows_pair(0, True)
            with pe.Fori(1, NT // 2) as i:
                rows_pair(i, False)
            barrier(pe, 1)

            def indexer(dst, w, c, semaphore):
                ins = 0
                for k in range(KT):
                    for a, b in ((0, 0), (0, 1), (1, 0)):
                        last = mm(dst, w[:, a, k, :], xnT[:, b, k, c * CH:(c + 1) * CH],
                                  start=ins == 0, stop=ins == 3 * KT - 1)
                        ins += 1
                last.then_inc(semaphore, 1)

            for c in range(2):
                indexer(psT[c][:], wikp, c, ik_mm)

            def iq_head(n, u, first):
                pe.wait_ge(wq_lo, n + 1)
                for c in range(2):
                    if not first:
                        pe.wait_ge(iq_lo, 2 * n + c - 3)
                    indexer(psS[u][:, c * CH:(c + 1) * CH], wqp[:, u], c, iq_mm)

            iq_head(0, 0, True)
            iq_head(1, 1, True)
            with pe.Fori(1, IH // 2) as i:
                iq_head(2 * i, 0, False)
                iq_head(2 * i + 1, 1, False)

            def idx_head(t, n, u, base):
                kw = P * (t + 1)
                pe.wait_ge(relu_done, base + n - 1) if not (isinstance(n, int) and base + n - 1 <= 0) else None
                for a, b in ((0, 0), (0, 1), (1, 0)):
                    for c in range(0, kw, CH):
                        w = min(CH, kw - c)
                        last = mm(psS[u][:, c:c + w], iq[:, a, n, t * P:(t + 1) * P], ikT[:, b, c:c + w],
                                  start=(a, b) == (0, 0), stop=(a, b) == (1, 0))
                last.then_inc(idx_mm, 1)

            pe.wait_ge(iq_lo, 2 * IH)
            pe.wait_ge(ik_lo, 2)
            base = 0
            for t in range(NT - 1, 0, -1):
                idx_head(t, 0, 0, base)
                idx_head(t, 1, 1, base)
                with pe.Fori(1, IH // 2) as i:
                    idx_head(t, 2 * i, 0, base)
                    idx_head(t, 2 * i + 1, 1, base)
                base += IH

            job = 0
            for src, ready in ((qn[:, :, 0:P], qn_done), (qn[:, :, P:2 * P], qn_done),
                               (kc[:, :, 0:P], kc_done), (kc[:, :, KVR:KVR + P], kc_done),
                               (tmp[:, :, 0:P], hw_done)):
                pe.wait_ge(ready, 1)
                for c in range(2):
                    if job >= 2:
                        pe.wait_ge(tr_lo, job - 1)
                    for j in range(4):
                        last = nc.tensor.transpose(psT[job % 2][:, j * P:(j + 1) * P], src[:, 4 * c + j, :], ident[:])
                    last.then_inc(tr_mm, 1)
                    job += 1

            def qw_pair(p, u, first):
                pe.wait_ge(ld_qw[u], 48 * (p // 2 + 1) if isinstance(p, int) else 24 * (p - u) + 48)
                if not first:
                    pe.wait_ge(qw_lo, 4 * p - 4)
                for h in range(2):
                    for k in range(2):
                        last = mm(psS[u][:, 128 * k + 64 * (1 - h):128 * k + 64 * (2 - h)],
                                  qb_s[:, u, h, 128 * k:128 * (k + 1)], wk_s[:, u, h, :], start=True, stop=True)
                last.then_inc(qw_mm, 1)

            qw_pair(0, 0, True)
            qw_pair(1, 1, True)
            with pe.Fori(1, NP // 2) as i:
                qw_pair(2 * i, 0, False)
                qw_pair(2 * i + 1, 1, False)
            barrier(pe, 2)

            def wait_bank(p, n, first, last_pair):
                m = n - 3
                while m >= 0 and ((RING[m][0] == "O" and first) or (RING[m][0] == "Q" and last_pair)):
                    m -= 3
                if m < 0 and first:
                    return
                if m < 0:
                    p, m = p - 1, m + USES
                what, at, *c = RING[m]
                if what == "T":
                    pe.wait_ge(p_lo, chunks_before(2 * p + at // 8, at % 8) + c[0] + 1)
                elif what == "O":
                    pe.wait_ge(ot_lo, 2 * p + at - 1)
                elif at < 2:
                    pe.wait_ge(raw_done, 2 * p + at + 3)
                else:
                    pe.wait_ge(qa_lo, 4 * p + 2 * at + 2)

            def q_job(bank, p, j):
                cs = slice((j % 2) * CH, (j % 2 + 1) * CH)
                ws = slice(128 * (j // 2), 128 * (j // 2 + 1))
                mm(bank[:], w1hi[:, p, ws], qlT[:, 0, cs], start=True, stop=False)
                mm(bank[:], w1hi[:, p, ws], qlT[:, 1, cs], start=False, stop=False)
                mm(bank[:], w1lo[:, p, ws], qlT[:, 0, cs], start=False, stop=False)
                mm(bank[:], w2s[:, p, ws], qlT[:, 2, cs], start=False, stop=False)
                mm(bank[:], w2s[0:64, p, ws], qlT[0:64, 3, cs], start=False, stop=True).then_inc(qp_mm if j < 2 else qa_mm, 1)

            def scores(p, v, s, fresh):
                h, k = s // 8, s % 8
                t = ORDER[k]
                kw = P * (t + 1)
                if s == 0:
                    pe.wait_ge(q_rot, 2 * p + 2)
                    pe.wait_ge(qa_lo, 4 * p + 4)
                if not fresh:
                    pe.wait_ge(max_done, 16 * p + s - 1)
                for a, b in ((0, 0), (0, 1), (1, 0)):
                    for c in range(0, kw, CH):
                        w = min(CH, kw - c)
                        last = mm(psS[k % 2][:, c:c + w], Q[:, v, a, h, t * P:(t + 1) * P], keyT[:, b, h, c:c + w],
                                  start=(a, b) == (0, 0), stop=(a, b) == (1, 0))
                last.then_inc(s_mm, 1)

            def values(head, k):
                pe.wait_ge(p_lo, chunks_before(head, k + 1))
                if k == 0 and not (isinstance(head, int) and head == 0):
                    pe.wait_ge(o_done, head)
                dst = psO[:, k * KVR:(k + 1) * KVR]
                for j in range(NB[k]):
                    for n, (a, b) in enumerate(((0, 0), (0, 1), (1, 0))):
                        last = mm(dst, pT[:, k % 2, a, j * P:(j + 1) * P], val[:, b, j, :],
                                  start=j == 0 and n == 0, stop=j == NB[k] - 1 and n == 2)
                last.then_inc(av_mm, 1)

            def out_T(bank, p, c):
                pe.wait_ge(o_done, 2 * p + 2)
                for j in range(4):
                    last = nc.tensor.transpose(bank[:, j * P:(j + 1) * P], op[:, ORDER.index(4 * c + j), :], ident[:])
                last.then_inc(ot_mm, 1)

            def pair(p, v, first, last_pair):
                for n, (what, at, *c) in enumerate(RING):
                    if what == "T":
                        h, k = at // 8, at % 8
                        if c[0] == 0:
                            if at:
                                step_end(p, v, at - 1, first, last_pair)
                            pe.wait_ge(exp_done, 16 * p + at + 1)
                        wait_bank(p, n, first, last_pair)
                        for j in range(4 * c[0], min(4 * c[0] + 4, NB[k])):
                            last = nc.tensor.transpose(psT[n % 3][:, (j % 4) * P:(j % 4 + 1) * P],
                                                       pr[:, k % 4, j * P:(j + 1) * P], ident[:])
                        last.then_inc(t_mm, 1)
                    elif what == "Q" and not last_pair:
                        wait_bank(p, n, first, last_pair)
                        q_job(psT[n % 3], p + 1, at)
                    elif what == "O" and not first:
                        wait_bank(p, n, first, last_pair)
                        out_T(psT[n % 3], p - 1, at)
                step_end(p, v, 15, first, last_pair)

            def step_end(p, v, s, first, last_pair):
                if s + AHEAD < 16:
                    scores(p, v, s + AHEAD, False)
                elif not last_pair:
                    scores(p + 1, 1 - v, s + AHEAD - 16, False)
                if s:
                    values(2 * p + (s - 1) // 8, (s - 1) % 8)
                elif not first:
                    values(2 * p - 1, 7)

            for j in range(4):
                if j == 3:
                    pe.wait_ge(raw_done, 1)
                q_job(psT[j % 3], 0, j)
            scores(0, 0, 0, True)
            scores(0, 0, 1, True)
            scores(0, 0, 2, False)
            pair(0, 0, True, False)
            with pe.Fori(0, NP // 2 - 1) as i:
                pair(2 * i + 1, 1, False, False)
                pair(2 * i + 2, 0, False, False)
            pair(NP - 1, 1, False, True)
            values(H - 1, 7)
            for c in range(2):
                pe.wait_ge(p_lo, H * CPH)
                out_T(psT[c], NP - 1, c)
            barrier(pe, 3)

            def vo_pair(p, u, first):
                pe.wait_ge(ld_ow[u], 32 * (p // 2 + 1) if isinstance(p, int) else 16 * (p - u) + 32)
                if not first:
                    pe.wait_ge(vo_lo, p - 1)
                for h in range(2):
                    last = mm(psT[u][64 * h:64 * (h + 1), :], wv_s[:, u, h, :], ow_s[:, u, h, :], start=True, stop=True)
                last.then_inc(vo_mm, 1)

            vo_pair(0, 0, True)
            vo_pair(1, 1, True)
            with pe.Fori(1, NP // 2) as i:
                vo_pair(2 * i, 0, False)
                vo_pair(2 * i + 1, 1, False)
            pe.wait_ge(vo_lo, NP)

            def final(t, u, first):
                if not first:
                    pe.wait_ge(fin_done, t - 1)
                rows_ = ds(t * P, P)
                for n in range(NP):
                    for a, b in ((0, 0), (0, 1), (1, 0)):
                        mm(psS[u][:, 0:CH], big[:, a, n, rows_], wvo[:, b, n, :], start=n == 0 and (a, b) == (0, 0), stop=False)
                for a, b in ((0, 0), (0, 1), (1, 0)):
                    last = mm(psS[u][:, 0:CH], hwT[:, a, rows_], bmp[:, b, :], start=False, stop=(a, b) == (1, 0))
                last.then_inc(fin_mm, 1)

            final(0, 0, True)
            final(1, 1, True)
            with pe.Fori(1, NT // 2) as i:
                final(2 * i, 0, False)
                final(2 * i + 1, 1, False)

        @block.scalar
        def _(act):
            def copy(dst, src, scale):
                return nc.scalar.activation(dst, src, ACT.Copy, scale=scale)

            act.wait_ge(ld_wc, 16)
            copy(wcp[:, 0], wc, W_S).then_inc(wc_hi, 1)
            act.wait_ge(ld_c, 16 * n_const)
            copy(wikp[:, 0], wk32, W_S).then_inc(wc_hi, 1)
            copy(bmp[:, 0, :], bm32, B_S).then_inc(wc_hi, 1)
            act.wait_ge(ve_done, 1)
            nc.scalar.activation(sd, ve, ACT.Sqrt).then_inc(sd_done, 1)

            def rows_hi(t, u):
                act.wait_ge(xT_done, t + 1)
                copy(xnT[:, 0, :, ds(t * P, P)], psT[u][:].rearrange("p (k q) -> p k q", k=KT), X_S).then_inc(xhi_done, 1)

            def rows_pj(t, u):
                act.wait_ge(pj_mm, t + 1)
                copy(proj[:, t, :], psS[u][:, 0:CW], 1.0 / (X_S * W_S)).then_inc(pj_done, 1)

            def rows_pair(i):
                rows_hi(2 * i, 0)
                rows_hi(2 * i + 1, 1)
                rows_pj(2 * i, 0)
                rows_pj(2 * i + 1, 1)

            with act.Fori(0, NT // 2) as i:
                rows_pair(i)
            barrier(act, 1)

            sc = IQ_S / (X_S * W_S)
            for c in range(2):
                act.wait_ge(ik_mm, c + 1)
                copy(ikT[:, 0, c * CH:(c + 1) * CH], psT[c][:], sc).then_inc(ik_hi, 1)
            with act.Fori(0, IH // 2) as i:
                for u in range(2):
                    for c in range(2):
                        act.wait_ge(iq_mm, 4 * i + 2 * u + c + 1)
                        copy(iq[:, 0, 2 * i + u, c * CH:(c + 1) * CH], psS[u][:, c * CH:(c + 1) * CH], sc).then_inc(iq_hi, 1)

            rsc = IH ** -0.5 * ID ** -0.5 / (IQ_S * IQ_S)
            base = 0
            for t in range(NT - 1, 0, -1):
                kw = P * (t + 1)

                def relu_head(n, u):
                    act.wait_ge(idx_mm, base + n + 1)
                    if not (isinstance(n, int) and base + n < 2):
                        act.wait_ge(acc_done, base + n - 1)
                    nc.scalar.activation(relu[:, u, 0:kw], psS[u][:, 0:kw], ACT.Relu, scale=rsc).then_inc(relu_done, 1)

                relu_head(0, 0)
                relu_head(1, 1)
                with act.Fori(1, IH // 2) as i:
                    relu_head(2 * i, 0)
                    relu_head(2 * i + 1, 1)
                base += IH

            act.wait_ge(nrm, 5)
            nc.scalar.activation(sdn, ssq, ACT.Sqrt).then_inc(n_sqrt, 1)
            act.wait_ge(kc_done, 1)
            copy(val[:, 0], kc[:, :, KVR:2 * KVR], K_S).then_inc(v_hi, 1)
            act.wait_ge(g_sub, 1)
            nc.scalar.activation(gwork[:, :, 0:E], gl, ACT.Exp).then_inc(g_exp, 1)
            for job, (dst, s) in enumerate(((qlT[:, 0], QL_S), (qlT[:, 2], QL_S), (keyT[:, 0, 0], K_S),
                                            (keyT[:, 0, 1], K_S), (hwT[:, 0], HW_S * SCALING))):
                for c in range(2):
                    act.wait_ge(tr_mm, 2 * job + c + 1)
                    copy(dst[:, c * CH:(c + 1) * CH], psT[c][:], s).then_inc(tr_hi, 1)

            with act.Fori(0, NP // 2) as i:
                for u in range(2):
                    p = 2 * i + u
                    act.wait_ge(qw_mm, p + 1)
                    copy(w1hi[:, p, 128:256], psS[u][:, 0:128], WQ_S).then_inc(qw_hi, 1)
                    copy(w2s[:, p, 128:256], psS[u][:, 128:256], WQ_S).then_inc(qw_hi, 1)
                    act.wait_ge(ld_qw[u], 48 * i + 48)
                    copy(w1hi[:, p, 0:128], pe_s[:, u, 0, :], WQ_S).then_inc(qw_hi, 1)
                    copy(w2s[:, p, 0:128], pe_s[:, u, 1, :], WQ_S).then_inc(qw_hi, 1)
            barrier(act, 2)

            qs = 1.0 / (QL_S * WQ_S)

            def q_evac(bank, p, v, j):
                cs = slice((j % 2) * CH, (j % 2 + 1) * CH)
                if j < 2:
                    act.wait_ge(qp_mm, 2 * p + j + 1)
                    if j == 0 and not (isinstance(p, int) and p == 0):
                        act.wait_ge(rot, 3 * p)
                    copy(raw[:, cs], bank[:], qs * Q_S).then_inc(raw_done, 1)
                else:
                    act.wait_ge(qa_mm, 2 * p + j - 1)
                    copy(Q[64:128, v, 0, 0, cs], bank[64:128, :], qs * Q_S).then_inc(qa_hi, 1)
                    copy(Q[0:64, v, 0, 1, cs], bank[0:64, :], qs * Q_S).then_inc(qa_hi, 1)

            def exp_step(p, s):
                h, k = s // 8, s % 8
                kw = P * NB[k]
                act.wait_ge(max_done, 16 * p + s + 1)
                nc.scalar.activation(pr[:, k % 4, 0:kw], pr[:, k % 4, 0:kw], ACT.Exp, bias=nmax[:, k % 4:k % 4 + 1],
                                     scale=-1.0, accum_out=rsum[:, h, k:k + 1]).then_inc(exp_done, 1)

            def p_hi_chunk(bank, p, s, c, fresh):
                h, k = s // 8, s % 8
                w = P * min(4, NB[k] - 4 * c)
                act.wait_ge(t_mm, chunks_before(2 * p + h, k) + c + 1)
                if c == 0 and not fresh:
                    act.wait_ge(av_mm, 16 * p + s - 1)
                copy(pT[:, k % 2, 0, c * CH:c * CH + w], bank[:, 0:w], PR_S).then_inc(p_hi, 1)

            def ot_evac(bank, p, c):
                act.wait_ge(ot_mm, 2 * p + c + 1)
                copy(big[:, 0, p, c * CH:(c + 1) * CH], bank[:], O_S / (PR_S * K_S)).then_inc(ot_hi, 1)

            def pair(p, v, first, last_pair):
                for n, (what, at, *c) in enumerate(RING):
                    if what == "T":
                        p_hi_chunk(psT[n % 3], p, at, c[0], first and at < 2)
                        if c[0] == NCH[at % 8] - 1:
                            if at + AHEAD - 1 < 16:
                                exp_step(p, at + AHEAD - 1)
                            elif not last_pair:
                                exp_step(p + 1, at + AHEAD - 17)
                    elif what == "Q" and not last_pair:
                        q_evac(psT[n % 3], p + 1, 1 - v, at)
                    elif what == "O" and not first:
                        ot_evac(psT[n % 3], p - 1, at)

            for j in range(4):
                q_evac(psT[j % 3], 0, 0, j)
            exp_step(0, 0)
            exp_step(0, 1)
            pair(0, 0, True, False)
            with act.Fori(0, NP // 2 - 1) as i:
                pair(2 * i + 1, 1, False, False)
                pair(2 * i + 2, 0, False, False)
            pair(NP - 1, 1, False, True)
            for c in range(2):
                ot_evac(psT[c], NP - 1, c)
            barrier(act, 3)

            with act.Fori(0, NP // 2) as i:
                for u in range(2):
                    act.wait_ge(vo_mm, 2 * i + u + 1)
                    copy(wvo[:, 0, 2 * i + u, :], psT[u][:], WVO_S).then_inc(vo_hi, 1)

        @block.vector
        def _(dve):
            v = nc.vector
            count = {}

            def link(ins, s=nrm):
                count[s] = count.get(s, 0) + 1
                ins.then_inc(s, 1)
                dve.wait_ge(s, count[s])

            def low(dst, src, scale, hi):
                return v.scalar_tensor_tensor(out=dst, in0=src, scalar=scale, in1=hi, op0=ALU.mult, op1=ALU.subtract)

            for c in range(2):
                dve.wait_ge(ld_x[c], 16)
                with dve.Fori(4 * c, 4 * c + 4) as t:
                    v.bn_stats(st[:, t, :], x_sb[:, t, :]).then_inc(st_done, 1)
            dve.wait_ge(st_done, NT)
            for t in range(NT):
                v.bn_aggr(mv[:, t, :], st[:, t, :]).then_inc(st_done, 1)
            dve.wait_ge(st_done, 2 * NT)
            v.tensor_scalar(ve, mv[:, :, 1], EPS, None, ALU.add).then_inc(ve_done, 1)
            dve.wait_ge(wc_hi, 3)
            low(wcp[:, 1].rearrange("p k n -> p (k n)"), wc.rearrange("p k n -> p (k n)"), W_S,
                wcp[:, 0].rearrange("p k n -> p (k n)")).then_inc(wc_lo, 1)
            low(wikp[:, 1].rearrange("p k n -> p (k n)"), wk32.rearrange("p k n -> p (k n)"), W_S,
                wikp[:, 0].rearrange("p k n -> p (k n)")).then_inc(wc_lo, 1)
            low(bmp[:, 1, :], bm32, B_S, bmp[:, 0, :]).then_inc(wc_lo, 1)
            dve.wait_ge(sd_done, 1)
            v.reciprocal(rstd, sd).then_inc(rs_done, 1)
            dve.wait_ge(rs_done, 1)

            def rows_n(t, u, first):
                if not first:
                    dve.wait_ge(xT_done, t - 1)
                v.tensor_scalar(xn[:, u, :], x_sb[:, t, :], mv[:, t, 0:1], rstd[:, ds(t, 1)],
                                ALU.subtract, ALU.mult).then_inc(xn_done, 1)

            def rows_lo(t, u):
                dve.wait_ge(xhi_done, t + 1)
                low(xnT[:, 1, :, ds(t * P, P)], psT[u][:].rearrange("p (k q) -> p k q", k=KT), X_S,
                    xnT[:, 0, :, ds(t * P, P)]).then_inc(xlo_done, 1)

            def rows_pair(i, first):
                rows_n(2 * i, 0, first)
                rows_n(2 * i + 1, 1, first)
                rows_lo(2 * i, 0)
                rows_lo(2 * i + 1, 1)

            rows_pair(0, True)
            with dve.Fori(1, NT // 2) as i:
                rows_pair(i, False)
            barrier(dve, 1)

            sc = IQ_S / (X_S * W_S)
            for c in range(2):
                dve.wait_ge(ik_hi, c + 1)
                low(ikT[:, 1, c * CH:(c + 1) * CH], psT[c][:], sc, ikT[:, 0, c * CH:(c + 1) * CH]).then_inc(ik_lo, 1)
            with dve.Fori(0, IH // 2) as i:
                for u in range(2):
                    for c in range(2):
                        dve.wait_ge(iq_hi, 4 * i + 2 * u + c + 1)
                        low(iq[:, 1, 2 * i + u, c * CH:(c + 1) * CH], psS[u][:, c * CH:(c + 1) * CH], sc,
                            iq[:, 0, 2 * i + u, c * CH:(c + 1) * CH]).then_inc(iq_lo, 1)

            dve.wait_ge(idx_init, 2)
            def acc(t, n, u, base):
                row = bias[:, TOFF[t]:TOFF[t + 1]]
                dve.wait_ge(relu_done, base + n + 1)
                if not (isinstance(n, int) and base + n == 0):
                    dve.wait_ge(acc_done, base + n)
                v.scalar_tensor_tensor(out=row, in0=relu[:, u, 0:P * (t + 1)], scalar=proj[:, t, ds(C_IW + n, 1)],
                                       in1=row, op0=ALU.mult, op1=ALU.add).then_inc(acc_done, 1)

            base = 0
            done = 0
            for group in GROUPS:
                for t in group:
                    acc(t, 0, 0, base)
                    acc(t, 1, 1, base)
                    with dve.Fori(1, IH // 2) as i:
                        acc(t, 2 * i, 0, base)
                        acc(t, 2 * i + 1, 1, base)
                    base += IH
                dve.wait_ge(acc_done, base)
                m = len(group)
                rows_ = [bias[:, TOFF[t]:TOFF[t + 1]] for t in group]

                def top_round(r, first):
                    for g_, row in enumerate(rows_):
                        if not first:
                            wait_alone(dve, tk_rep, m * r + (done + g_ + 1 - m))
                        v.max(m8[:, g_], row).then_inc(tk_max, 1)
                    for g_, row in enumerate(rows_):
                        wait_alone(dve, tk_max, m * r + (done + g_ + 1))
                        v.match_replace(out=row, in_to_replace=m8[:, g_], in_values=row, imm_value=TAKEN).then_inc(tk_rep, 1)

                top_round(0, True)
                with dve.Fori(1, TOPK // 8) as r:
                    top_round(r, False)
                done += m * (TOPK // 8)
                dve.wait_ge(tk_rep, done)
                for row in rows_:
                    v.tensor_scalar(row, row, HALF_TAKEN, NEG, ALU.is_gt, ALU.mult).then_inc(mask_done, 1)

            pq = proj[:, :, C_Q:C_Q + QR]
            pkv = proj[:, :, C_KV:C_KV + KVR]
            link(v.tensor_tensor(tmp, pq, pq, ALU.mult))
            link(v.tensor_reduce(ssq[:, 0], tmp, AX.X, ALU.add))
            link(v.tensor_tensor(tmp[:, :, 0:KVR], pkv, pkv, ALU.mult))
            link(v.tensor_reduce(ssq[:, 1], tmp[:, :, 0:KVR], AX.X, ALU.add))
            v.tensor_scalar(ssq[:, 0], ssq[:, 0], 1.0 / QR, EPS, ALU.mult, ALU.add).then_inc(st_done, 1)
            dve.wait_ge(st_done, 2 * NT + 1)
            link(v.tensor_scalar(ssq[:, 1], ssq[:, 1], 1.0 / KVR, EPS, ALU.mult, ALU.add))
            dve.wait_ge(n_sqrt, 1)
            link(v.reciprocal(rsn, sdn))
            link(v.tensor_tensor(tmp, pq, rsn[:, 0].unsqueeze(2).broadcast_to([P, NT, QR]), ALU.mult))
            link(v.tensor_tensor(qn[:, :, 0:QR], tmp, qnw[:].unsqueeze(1).broadcast_to([P, NT, QR]), ALU.mult))
            v.tensor_copy(qn[:, :, QR:256], qn[:, :, P:QR]).then_inc(qn_done, 1)
            link(v.tensor_tensor(tmp[:, :, 0:KVR], pkv, rsn[:, 1].unsqueeze(2).broadcast_to([P, NT, KVR]), ALU.mult))
            link(v.tensor_tensor(kc[:, :, KVR:2 * KVR], tmp[:, :, 0:KVR], kvw[:].unsqueeze(1).broadcast_to([P, NT, KVR]), ALU.mult))
            kp = proj[:, :, C_KV + KVR:C_KV + KVR + ROPE].rearrange("p t (j two) -> p t j two", two=2)
            t4 = tmp[:, :, 0:128].rearrange("p t (f j) -> p t f j", f=4)
            link(v.tensor_tensor(t4[:, :, 0], kp[:, :, :, 0], ck, ALU.mult))
            link(v.tensor_tensor(t4[:, :, 1], kp[:, :, :, 1], sk, ALU.mult))
            link(v.tensor_tensor(t4[:, :, 2], kp[:, :, :, 1], ck, ALU.mult))
            link(v.tensor_tensor(t4[:, :, 3], kp[:, :, :, 0], sk, ALU.mult))
            ko = kc[:, :, 0:ROPE].rearrange("p t (j two) -> p t j two", two=2)
            link(v.tensor_tensor(ko[:, :, :, 0], t4[:, :, 0], t4[:, :, 1], ALU.subtract))
            link(v.tensor_tensor(ko[:, :, :, 1], t4[:, :, 2], t4[:, :, 3], ALU.add))
            v.tensor_copy(kc[:, :, 2 * KVR:3 * KVR], kc[:, :, 0:ROPE]).then_inc(kc_done, 1)
            dve.wait_ge(v_hi, 1)
            low(val[:, 1], kc[:, :, KVR:2 * KVR], K_S, val[:, 0])

            link(v.tensor_tensor(gl, proj[:, :, C_R:C_R + E], rbs.unsqueeze(1).broadcast_to([P, NT, E]), ALU.add))
            link(v.tensor_reduce(gm, gl, AX.X, ALU.max))
            v.tensor_tensor(gl, gl, gm.unsqueeze(2).broadcast_to([P, NT, E]), ALU.subtract).then_inc(g_sub, 1)
            v.memset(gwork[:, :, E:2 * E], -1.0).then_inc(st_done, 1)
            v.memset(grep[:], -1.0).then_inc(st_done, 1)
            dve.wait_ge(st_done, 2 * NT + 3)
            dve.wait_ge(g_exp, 1)
            for t in range(NT):
                ins = v.max(gmx[:, t, :], gwork[:, t, 0:E])
                if t < NT - 1:
                    ins.then_inc(st_done, 1)
            link(ins)
            dve.wait_ge(st_done, 3 * NT + 2)
            link(v.tensor_copy(grep[:, :, 0:2], gmx[:, :, 0:2]))
            for t in range(NT):
                ins = v.match_replace(out=gout[:, t, :], in_to_replace=grep[:, t, :], in_values=gwork[:, t, :], imm_value=2.0)
                if t < NT - 1:
                    ins.then_inc(st_done, 1)
            link(ins)
            dve.wait_ge(st_done, 4 * NT + 1)
            link(v.tensor_scalar(gout[:, :, 0:E], gout[:, :, 0:E], 2.0, None, ALU.is_ge))
            link(v.tensor_tensor(gw, gout[:, :, 0:E], gwork[:, :, 0:E], ALU.mult))
            link(v.tensor_tensor(gden, gmx[:, :, 0], gmx[:, :, 1], ALU.add))
            link(v.reciprocal(grd, gden))
            link(v.tensor_tensor(gw, gw, grd.unsqueeze(2).broadcast_to([P, NT, E]), ALU.mult))
            for t in range(NT):
                ins = v.tensor_tensor(tmp[:, t, 0:P].rearrange("p (e r) -> p e r", e=E),
                                      proj[:, t, C_H:C_H + P].rearrange("p (e r) -> p e r", e=E),
                                      gw[:, t, :].unsqueeze(2).broadcast_to([P, E, R]), ALU.mult)
                if t < NT - 1:
                    ins.then_inc(st_done, 1)
            dve.wait_ge(st_done, 5 * NT)
            ins.then_inc(hw_done, 1)

            for job, (dh, dl, s, rows_) in enumerate((
                    (qlT[:, 0], qlT[:, 1], QL_S, P), (qlT[:, 2], qlT[:, 3], QL_S, 64), (keyT[:, 0, 0], keyT[:, 1, 0], K_S, P),
                    (keyT[:, 0, 1], keyT[:, 1, 1], K_S, P), (hwT[:, 0], hwT[:, 1], HW_S * SCALING, P))):
                for c in range(2):
                    dve.wait_ge(tr_hi, 2 * job + c + 1)
                    low(dl[0:rows_, c * CH:(c + 1) * CH], psT[c][0:rows_, :], s, dh[0:rows_, c * CH:(c + 1) * CH]).then_inc(tr_lo, 1)

            with dve.Fori(0, NP // 2) as i:
                for u in range(2):
                    p = 2 * i + u
                    dve.wait_ge(qw_hi, 8 * i + 4 * u + 4)
                    low(w1lo[:, p, 128:256], psS[u][:, 0:128], WQ_S, w1hi[:, p, 128:256]).then_inc(qw_lo, 1)
                    low(w2s[64:128, p, 128:256], psS[u][64:128, 128:256], WQ_S, w2s[64:128, p, 128:256]).then_inc(qw_lo, 1)
                    low(w1lo[:, p, 0:128], pe_s[:, u, 0, :], WQ_S, w1hi[:, p, 0:128]).then_inc(qw_lo, 1)
                    low(w2s[64:128, p, 0:128], pe_s[64:128, u, 1, :], WQ_S, w2s[64:128, p, 0:128]).then_inc(qw_lo, 1)
            barrier(dve, 2)

            c_s = (NOPE + ROPE) ** -0.5 / (Q_S * K_S)
            qs = Q_S / (QL_S * WQ_S)

            def q_low(bank, p, v_, j):
                cs = slice((j % 2) * CH, (j % 2 + 1) * CH)
                dve.wait_ge(qa_hi, 4 * p + 2 * j - 2)
                low(Q[64:128, v_, 1, 0, cs], bank[64:128, :], qs, Q[64:128, v_, 0, 0, cs]).then_inc(qa_lo, 1)
                low(Q[0:64, v_, 1, 1, cs], bank[0:64, :], qs, Q[0:64, v_, 0, 1, cs]).then_inc(qa_lo, 1)

            def rope_hi(p, v_):
                dve.wait_ge(rot, 3 * p + 3)
                v.tensor_copy(Q[0:64, v_, 0, 0, :], rt[0:64, :]).then_inc(rope_h, 1)
                v.tensor_copy(Q[64:128, v_, 0, 1, :], rt[64:128, :]).then_inc(rope_h, 1)

            def row_max(p, s, fresh):
                k = s % 8
                t, kw = ORDER[k], P * NB[k]
                if not fresh:
                    head = 2 * p + s // 8
                    prev = chunks_before(head, k - 3) if k >= 3 else chunks_before(head - 1, k + 5)
                    wait_alone(dve, t_mm, prev)
                    wait_alone(dve, exp_done, 16 * p + s - 3)
                wait_alone(dve, s_mm, 16 * p + s + 1)
                v.tensor_tensor_reduce(out=pr[:, k % 4, 0:kw], in0=psS[k % 2][:, 0:kw], in1=bias[:, TOFF[t]:TOFF[t + 1]],
                                       scale=-c_s, scalar=3e38, op0=ALU.add, op1=ALU.min,
                                       accum_out=nmax[:, k % 4:k % 4 + 1]).then_inc(max_done, 1)

            def p_low_chunk(bank, p, s, c):
                h, k = s // 8, s % 8
                w = P * min(4, NB[k] - 4 * c)
                dve.wait_ge(p_hi, chunks_before(2 * p + h, k) + c + 1)
                low(pT[:, k % 2, 1, c * CH:c * CH + w], bank[:, 0:w], PR_S,
                    pT[:, k % 2, 0, c * CH:c * CH + w]).then_inc(p_lo, 1)

            def head_out(p, h):
                head = 2 * p + h
                dve.wait_ge(exp_done, 8 * head + 8)
                v.reciprocal(rinv, rsum[:, h, :]).then_inc(ri_done, 1)
                dve.wait_ge(av_mm, 8 * head + 8)
                dve.wait_ge(ri_done, head + 1)
                if not (isinstance(p, int) and p == 0):
                    dve.wait_ge(ot_mm, 2 * p)
                v.tensor_tensor(op[:, :, h * KVR:(h + 1) * KVR], psO[:].rearrange("p (k r) -> p k r", k=NT),
                                rinv.unsqueeze(2).broadcast_to([P, NT, KVR]), ALU.mult).then_inc(o_done, 1)

            def ot_low(bank, p, c):
                dve.wait_ge(ot_hi, 2 * p + c + 1)
                low(big[:, 1, p, c * CH:(c + 1) * CH], bank[:], O_S / (PR_S * K_S),
                    big[:, 0, p, c * CH:(c + 1) * CH]).then_inc(ot_lo, 1)

            def pair(p, v_, first, last_pair):
                for n, (what, at, *c) in enumerate(RING):
                    if what == "T":
                        p_low_chunk(psT[n % 3], p, at, c[0])
                        if c[0] == NCH[at % 8] - 1:
                            if at + AHEAD < 16:
                                row_max(p, at + AHEAD, first and at + AHEAD < 4)
                            elif not last_pair:
                                row_max(p + 1, at + AHEAD - 16, False)
                        if at % 8 == 0 and c[0] == NCH[0] - 1 and not (first and at == 0):
                            head_out(p if at else p - 1, 0 if at else 1)
                        if at == ROPE_AT and c[0] == NCH[at % 8] - 1 and not last_pair:
                            rope_hi(p + 1, 1 - v_)
                    elif what == "Q" and at >= 2 and not last_pair:
                        q_low(psT[n % 3], p + 1, 1 - v_, at)
                    elif what == "O" and not first:
                        ot_low(psT[n % 3], p - 1, at)

            for j in (2, 3):
                q_low(psT[j % 3], 0, 0, j)
            rope_hi(0, 0)
            for s in range(3):
                row_max(0, s, True)
            pair(0, 0, True, False)
            with dve.Fori(0, NP // 2 - 1) as i:
                pair(2 * i + 1, 1, False, False)
                pair(2 * i + 2, 0, False, False)
            pair(NP - 1, 1, False, True)
            head_out(NP - 1, 1)
            for c in range(2):
                ot_low(psT[c], NP - 1, c)
            barrier(dve, 3)

            with dve.Fori(0, NP // 2) as i:
                for u in range(2):
                    dve.wait_ge(vo_hi, 2 * i + u + 1)
                    low(wvo[:, 1, 2 * i + u, :], psT[u][:], WVO_S, wvo[:, 0, 2 * i + u, :]).then_inc(vo_lo, 1)

            def final(t, u, first):
                dve.wait_ge(fin_mm, t + 1)
                dve.wait_ge(ld_xr[u], 16 if first else 8 * (t - u) + 16)
                if not first:
                    dve.wait_ge(stored[u], 8 * (t - u))
                v.scalar_tensor_tensor(out=res[:, u], in0=psS[u][:, 0:CH], scalar=1.0 / OUT_S, in1=xr[:, u],
                                       op0=ALU.mult, op1=ALU.add).then_inc(fin_done, 1)

            final(0, 0, True)
            final(1, 1, True)
            with dve.Fori(1, NT // 2) as i:
                final(2 * i, 0, False)
                final(2 * i + 1, 1, False)

        @block.gpsimd
        def _(pool):
            g = nc.gpsimd
            g.memset(bias[:], 0.0).then_inc(idx_init, 1)
            pool.wait_ge(idx_init, 1)
            pool.wait_ge(ld_c, 16 * n_const)
            for t in range(NT):
                ins = g.tensor_copy(bias[:, TOFF[t + 1] - P:TOFF[t + 1]], causal[:])
            ins.then_inc(idx_init, 1)
            barrier(pool, 1)

            def wq_parts(n, u, first):
                wait_alone(pool, ld_wq[u], 16 if first else 8 * (n - u) + 16)
                g.tensor_scalar(wq32[:, u], wq32[:, u], W_S, 1.0, ALU.mult, ALU.mult).then_inc(wq_sc, 1)
                wait_alone(pool, wq_sc, n + 1)
                if not first:
                    wait_alone(pool, iq_mm, 2 * n - 2)
                g.tensor_copy(wqp[:, u, 0], wq32[:, u]).then_inc(wq_hi, 1)
                pool.wait_ge(wq_hi, n + 1)
                g.tensor_tensor(wqp[:, u, 1], wq32[:, u], wqp[:, u, 0], ALU.subtract).then_inc(wq_lo, 1)

            wq_parts(0, 0, True)
            wq_parts(1, 1, True)
            with pool.Fori(1, IH // 2) as i:
                wq_parts(2 * i, 0, False)
                wq_parts(2 * i + 1, 1, False)
            barrier(pool, 2)

            pool.wait_ge(ld_cq, 32)

            def rope(p, v_):
                pool.wait_ge(sw_done, 32 * p + 32)
                g.tensor_tensor(swp, swp, sq[:], ALU.mult).then_inc(rot, 1)
                g.tensor_tensor(raw, raw, cq[:], ALU.mult).then_inc(rot, 1)
                pool.wait_ge(rot, 3 * p + 2)
                if not (isinstance(p, int) and p == 0):
                    pool.wait_ge(q_rot, 2 * p)
                g.tensor_tensor(rt, raw, swp, ALU.add).then_inc(rot, 1)
                pool.wait_ge(rope_h, 2 * p + 2)
                g.tensor_tensor(Q[0:64, v_, 1, 0, :], rt[0:64, :], Q[0:64, v_, 0, 0, :], ALU.subtract).then_inc(q_rot, 1)
                g.tensor_tensor(Q[64:128, v_, 1, 1, :], rt[64:128, :], Q[64:128, v_, 0, 1, :], ALU.subtract).then_inc(q_rot, 1)

            rope(0, 0)
            rope(1, 1)
            with pool.Fori(1, NP // 2) as i:
                rope(2 * i, 0)
                rope(2 * i + 1, 1)
            barrier(pool, 3)


def kernel(**inputs):
    import concourse.bacc as _bacc
    from concourse.bass_utils import run_bass_kernel_spmd as _run

    def host(name):
        return np.asarray(inputs["L0_" + name])

    x = host("attn_hidden_states").reshape(S, HID)
    qb = host("attn_q_b_w").reshape(QR, H, NOPE + ROPE)
    kvb = host("attn_kv_b_w").reshape(KVR, H, NOPE + VD)
    twice = np.r_[0:QR, P:QR]
    freq = (np.float32(1.0) / np.float32(10000.0) ** (np.arange(0, ROPE, 2, dtype=np.float32) / np.float32(ROPE))).astype(np.float32)
    ang = np.arange(S, dtype=np.float32)[:, None] * freq[None, :]
    cos, sin = np.cos(ang).astype(np.float32), np.sin(ang).astype(np.float32)
    cos_rows = np.repeat(cos.T, 2, axis=0)
    sin_rows = np.repeat(sin.T, 2, axis=0) * np.tile(np.array([-1.0, 1.0], np.float32), ROPE // 2)[:, None]
    arrays = {
        "x": x,
        "wcat": np.concatenate([host("attn_q_a_w"), host("attn_kv_a_w"), host("attn_idx_weights_w"),
                                host("ffn_router_w").T, host("ffn_A").reshape(E * R, HID).T], axis=1),
        "wik": host("attn_idx_wk_w"),
        "wiq": host("attn_idx_wq_w"),
        "qbT": qb[twice, :, :NOPE].transpose(2, 1, 0),
        "wkT": kvb[:, :, :NOPE].transpose(2, 1, 0),
        "wvT": kvb[:, :, NOPE:].transpose(2, 1, 0),
        "qpe": qb[twice, :, NOPE:].reshape(2, P, H, ROPE).transpose(1, 0, 2, 3),
        "ow": host("attn_o_w"),
        "bm": host("ffn_Bm").transpose(0, 2, 1).reshape(E * R, HID),
        "qnorm": np.broadcast_to(host("attn_q_a_norm_w"), (P, QR)),
        "kvnorm": np.broadcast_to(host("attn_kv_a_norm_w"), (P, KVR)),
        "rbias": np.broadcast_to(host("ffn_router_b"), (P, E)),
        "cosq": np.concatenate([cos_rows, cos_rows]),
        "sinq": np.concatenate([sin_rows, sin_rows]),
        "cosk": cos,
        "sink": sin,
        "ident": np.eye(P, dtype=np.float32),
        "causal": np.triu(np.full((P, P), NEG, np.float32), 1),
    }
    nc = _bacc.Bacc("TRN2", target_bir_lowering=False, num_devices=1)
    given, args = {}, []
    for name, a in arrays.items():
        given["in_" + name] = np.ascontiguousarray(a)
        args.append(nc.dram_tensor("in_" + name, a.shape, F32, kind="ExternalInput").ap())
    result = nc.dram_tensor("out_0", (S, HID), F32, kind="ExternalOutput").ap()
    block_kernel(nc, *args, result)
    r = _run(nc, [given], core_ids=[0])
    return r.results[0]["out_0"].reshape(1, S, HID)
```

```python
from contextlib import ExitStack

import numpy as np

import concourse.bass as bass
from concourse import mybir

F32 = mybir.dt.float32
F16 = mybir.dt.float16
ALU = mybir.AluOpType
ACT = mybir.ActivationFunctionType
AX = mybir.AxisListType

P = 128
S, HID = 1024, 512
NT = S // P
KT = HID // P
H, NOPE, ROPE, VD = 32, 128, 64, 128
NP = H // 2
QR, KVR = 192, 64
IH, ID, TOPK = 16, 128, 128
E, R = 8, 16
EPS = 1e-5
SCALING = 8.0 / R

C_Q, C_KV, C_IW, C_R, C_H = 0, QR, QR + KVR + ROPE, QR + KVR + ROPE + IH, QR + KVR + ROPE + IH + E
CW = C_H + E * R

NEG = -1e30
TAKEN = -3e38
HALF_TAKEN = -2e38

X_S, W_S, IQ_S, QL_S, WQ_S, Q_S, K_S = 64.0, 128.0, 32.0, 32.0, 64.0, 16.0, 16.0
PR_S, O_S, WVO_S, HW_S, B_S = 1024.0, 16.0, 256.0, 32.0, 128.0
OUT_S = O_S * WVO_S
assert HW_S * B_S == OUT_S

ORDER = [7, 1, 6, 0, 5, 2, 4, 3]
GROUPS = [[7, 6], [5, 4], [3, 2, 1]]
CH = 512
OW_DEEP = 4
ARENA = 15040


def block_kernel(nc, x, wcat, wik, wiq, qbT, wkT, wvT, qpe, ow, bm, qnorm, kvnorm, rbias,
                 cosq, sinq, cosk, sink, ident_d, causal_d, out):
    with ExitStack() as ctx:
        def sb(name, shape, dt=F32):
            return ctx.enter_context(nc.sbuf_tensor(name, shape, dt))

        def sem(name):
            return ctx.enter_context(nc.semaphore(name))

        big = sb("big", [P, 2, NP, S], F16)
        iq = big[:, :, 0:IH, :]
        w1hi = sb("w1hi", [P, NP, 256], F16)
        w1lo = sb("w1lo", [P, NP, 256], F16)
        w2s = sb("w2s", [P, NP, 256], F16)
        TOFF = [P * t * (t + 1) // 2 for t in range(NT + 1)]
        bias = sb("bias", [P, TOFF[NT]])
        cq = sb("cq", [P, S])
        sq = sb("sq", [P, S])
        keyT = sb("keyT", [P, 2, 2, S], F16)
        val = sb("val", [P, 2, NT, KVR], F16)
        qlT = sb("qlT", [P, 4, S], F16)
        hwT = sb("hwT", [P, 2, S], F16)
        bmp = sb("bmp", [P, 2, HID], F16)
        ikT = sb("ikT", [P, 2, S], F16)
        ident = sb("ident", [P, P])
        causal = sb("causal", [P, P])
        m8 = sb("m8", [P, 3, 8])
        small = sb("small", [P, 512])
        arena = sb("arena", [P, ARENA])

        def view(at, n, dt=F32):
            words = n if dt == F32 else n // 2
            assert at + words <= ARENA
            v = arena[:, at:at + words]
            return v if dt == F32 else v.bitcast(dt)

        half0 = big[:, 0, :, :].rearrange("p a b -> p (a b)")
        half1 = big[:, 1, :, :].rearrange("p a b -> p (a b)")
        x_sb = half0[:, 0:2 * NT * HID].bitcast(F32).rearrange("p (t d) -> p t d", t=NT)
        xn = half0[:, 8192:8192 + 4 * HID].bitcast(F32).rearrange("p (u d) -> p u d", u=2)
        wc = half1[:, 0:2 * KT * CW].bitcast(F32).rearrange("p (k n) -> p k n", k=KT)
        wcp = half1[:, 2 * KT * CW:4 * KT * CW].rearrange("p (s k n) -> p s k n", s=2, k=KT)
        wk32 = half1[:, 4 * KT * CW:4 * KT * CW + 2 * KT * ID].bitcast(F32).rearrange("p (k n) -> p k n", k=KT)
        bm32 = half1[:, 4 * KT * CW + 2 * KT * ID:4 * KT * CW + 2 * KT * ID + 2 * HID].bitcast(F32)
        xnT = view(0, 2 * KT * S, F16).rearrange("p (s k q) -> p s k q", s=2, k=KT)
        proj = view(4096, NT * CW).rearrange("p (t n) -> p t n", t=NT)
        o = 4096 + NT * CW
        qn = w1hi[:].bitcast(F32).rearrange("p a b -> p (a b)").rearrange("p (t n) -> p t n", t=NT)
        relu_a = view(o, 2 * S).rearrange("p (u n) -> p u n", u=2)
        kc = view(o + 2048, NT * 192).rearrange("p (t n) -> p t n", t=NT)
        tmp = view(o + 2048 + 1536, NT * QR).rearrange("p (t n) -> p t n", t=NT)
        o += 2048 + 1536 + 1536
        sqd = kc[:, 0:4, :]
        wq32 = view(o, 2 * HID).rearrange("p (u k n) -> p u k n", u=2, k=KT)
        wqp = view(o + 1024, 4 * HID, F16).rearrange("p (u s k n) -> p u s k n", u=2, s=2, k=KT)
        wikp = keyT[:, 0, 0, :].rearrange("p (s k n) -> p s k n", s=2, k=KT)
        relu_b = view(o, 2 * S).rearrange("p (u n) -> p u n", u=2)
        src3 = (relu_b[:, 0, 0:CH], relu_b[:, 1, 0:CH], relu_b[:, 0, CH:S])
        vo32 = view(o, 2 * HID).rearrange("p (u n) -> p u n", u=2)
        qb_s = view(0, 2 * 512).rearrange("p (u h r) -> p u h r", u=2, h=2)
        wk_s = view(1024, 2 * 128).rearrange("p (u h r) -> p u h r", u=2, h=2)
        pe_s = view(1280, 2 * 256).rearrange("p (u k n) -> p u k n", u=2, k=2)
        OW_AT = 8192
        ow_s = view(OW_AT, OW_DEEP * 2 * HID).rearrange("p (u h n) -> p u h n", u=OW_DEEP, h=2)
        wv_s = view(OW_AT + OW_DEEP * 2 * HID, OW_DEEP * P).rearrange("p (u h r) -> p u h r", u=OW_DEEP, h=2)
        vo_s = view(2048, OW_DEEP * 2 * HID, F16).rearrange("p (u s n) -> p u s n", u=OW_DEEP, s=2)
        Q = view(0, 8 * S, F16).rearrange("p (v s h q) -> p v s h q", v=2, s=2, h=2)
        raw = view(4096, S)
        swp = view(4096 + S, S)
        rt = view(6144, S)
        pr = view(7168, 4 * S).rearrange("p (u k) -> p u k", u=4)
        pT = view(11264, 4 * S, F16).rearrange("p (u s k) -> p u s k", u=2, s=2)
        op = view(13312, NT * P).rearrange("p (k r) -> p k r", k=NT)
        lat32 = view(13312 + NT * P, CH)
        xr = view(0, 2 * HID).rearrange("p (u n) -> p u n", u=2)
        res = view(2 * HID, 2 * HID).rearrange("p (u n) -> p u n", u=2)
        wvo = []
        for w_ in (w1hi, w1lo, w2s):
            wvo += [w_[:].rearrange("p a b -> p (a b)")[:, 1024 * j:1024 * (j + 1)].rearrange("p (s n) -> p s n", s=2)
                    for j in range(4)]
        for w_ in (cq, sq):
            wvo += [w_[:].bitcast(F16)[:, 1024 * j:1024 * (j + 1)].rearrange("p (s n) -> p s n", s=2) for j in range(2)]
        wvo_d = nc.dram_tensor("wvo_parts", [NP, P, 2 * HID], F16, kind="Internal").ap()

        st = small[:, 0:NT * 6].rearrange("p (t n) -> p t n", t=NT)
        mv = small[:, 48:64].rearrange("p (t n) -> p t n", t=NT)
        ve = small[:, 64:72]
        sd = small[:, 72:80]
        rstd = small[:, 80:88]
        ssq = small[:, 88:104].rearrange("p (w t) -> p w t", w=2)
        sdn = small[:, 104:120].rearrange("p (w t) -> p w t", w=2)
        rsn = small[:, 120:136].rearrange("p (w t) -> p w t", w=2)
        gm = small[:, 136:144]
        gden = small[:, 144:152]
        grd = small[:, 152:160]
        gl = small[:, 160:224].rearrange("p (t e) -> p t e", t=NT)
        gmx = small[:, 224:288].rearrange("p (t e) -> p t e", t=NT)
        gw = small[:, 288:352].rearrange("p (t e) -> p t e", t=NT)
        rbs = small[:, 352:360]
        nmax = small[:, 360:364]
        rsum = small[:, 364:380].rearrange("p (h t) -> p h t", h=2)
        rinv = small[:, 380:388]
        eps_t = small[:, 400:401]
        gwork = sb("gwork", [P, NT, 16])
        grep = sb("grep", [P, NT, 8])
        gout = sb("gout", [P, NT, 16])
        qnw = sb("qnw", [P, QR])
        kvw = sb("kvw", [P, KVR])
        ckv = hwT[:].rearrange("p a b -> p (a b)")
        ck = ckv[:, 0:512].bitcast(F32).rearrange("p (t j) -> p t j", t=NT)
        sk = ckv[:, 512:1024].bitcast(F32).rearrange("p (t j) -> p t j", t=NT)

        psS = [ctx.enter_context(nc.psum_tensor(f"psS{u}", [P, S], F32)) for u in range(2)]
        psT = [ctx.enter_context(nc.psum_tensor(f"psT{u}", [P, CH], F32)) for u in range(3)]
        psO = ctx.enter_context(nc.psum_tensor("psO", [P, CH], F32))
        tr_bank = [psT[2], psO]
        TR_JOBS, TR_FROM = 10, IH - 6

        def tr_jobs_after(n):
            j = 2 * (n - (TR_FROM + 1))
            return range(max(j, 0), j + 2)

        q0_bank = [psS[j // 2][:, (j % 2) * CH:(j % 2 + 1) * CH] for j in range(4)]

        ld_x = [sem(f"ld_x{c}") for c in range(3)]
        ld_wc = sem("ld_wc"); ld_id = sem("ld_id"); ld_c = sem("ld_c"); ld_cq = sem("ld_cq")
        st_done = sem("st_done")
        ve_done = sem("ve_done"); rs_done = sem("rs_done")
        sd_done = sem("sd_done")
        wc_hi = sem("wc_hi"); wc_lo = sem("wc_lo")
        xn_done = sem("xn_done"); xT_done = sem("xT_done")
        xhi_done = sem("xhi_done"); xlo_done = sem("xlo_done")
        pj_mm = sem("pj_mm"); pj_done = sem("pj_done")
        sq_done = sem("sq_done"); n_sqrt = sem("n_sqrt")
        rsn_done = sem("rsn_done"); eps_ok = sem("eps_ok")
        g_sub = sem("g_sub"); g_exp = sem("g_exp"); gw_done = sem("gw_done")
        nrm = sem("nrm"); pool_n = sem("pool_n")
        ik_mm = sem("ik_mm"); ik_hi = sem("ik_hi"); ik_lo = sem("ik_lo")
        ld_wq = [sem("ld_wq0"), sem("ld_wq1")]
        wq_hi = sem("wq_hi"); wq_lo = sem("wq_lo")
        iq_mm = sem("iq_mm"); iq_hi = sem("iq_hi"); iq_lo = sem("iq_lo")
        idx_init = sem("idx_init")
        idx_mm = sem("idx_mm"); relu_done = sem("relu_done")
        acc_done = sem("acc_done")
        wt_done = sem("wt_done"); sum_done = sem("sum_done")
        tk_max = sem("tk_max"); tk_rep = sem("tk_rep"); mask_done = sem("mask_done")
        qn_done = sem("qn_done"); kc_done = sem("kc_done"); hw_done = sem("hw_done")
        tr_mm = sem("tr_mm"); tr_hi = sem("tr_hi"); tr_lo = sem("tr_lo")
        v_hi = sem("v_hi"); v_lo = sem("v_lo")
        ld_qw = [sem("ld_qw0"), sem("ld_qw1")]
        qw_mm = sem("qw_mm"); qw_hi = sem("qw_hi"); qw_lo = sem("qw_lo")
        ld_ow = [sem(f"ld_ow{u}") for u in range(OW_DEEP)]
        vo_mm = sem("vo_mm"); vo_hi = sem("vo_hi"); vo_lo = sem("vo_lo")
        vo_st = [sem(f"vo_st{u}") for u in range(OW_DEEP)]; ld_vo = sem("ld_vo")
        qp_mm = sem("qp_mm"); raw_done = sem("raw_done")
        sw_done = sem("sw_done"); rot = sem("rot")
        rope_h = sem("rope_h"); q_rot = sem("q_rot")
        qa_mm = sem("qa_mm"); qa_hi = sem("qa_hi"); qa_lo = sem("qa_lo")
        s_mm = sem("s_mm"); max_done = sem("max_done"); exp_done = sem("exp_done")
        t_mm = sem("t_mm"); p_hi = sem("p_hi"); p_lo = sem("p_lo")
        av_mm = sem("av_mm")
        ri_done = sem("ri_done"); o_done = sem("o_done")
        ot_mm = sem("ot_mm"); ot_hi = sem("ot_hi"); ot_lo = sem("ot_lo")
        ld_xr = [sem("ld_xr0"), sem("ld_xr1")]
        fin_mm = sem("fin_mm"); fin_done = sem("fin_done"); stored = [sem("stored0"), sem("stored1")]

        stood = {}

        def wait_alone(eng, semaphore, value):
            if eng not in stood:
                stood[eng] = sem(f"stood{len(stood)}")
            eng.wait_ge(semaphore, value).then_inc(stood[eng], 1)

        block = ctx.enter_context(nc.Block())
        ds = bass.ds

        NB = [t + 1 for t in ORDER]
        NCH = [(b + 3) // 4 for b in NB]
        CUM = [sum(NCH[:k]) for k in range(9)]
        CPH = CUM[8]
        assert CPH % 2 == 0

        def chunks_before(head, k):
            return head * CPH + CUM[k]

        AHEAD = 3
        ROPE_AT = 8
        Q_AT, O_AT = {0: 0, 2: 1, 5: 2, 9: 3}, {4: 0, 8: 1}
        RING = []
        for s_ in range(16):
            RING += [("T", s_, c) for c in range(NCH[s_ % 8])]
            RING += [("Q", Q_AT[s_])] if s_ in Q_AT else []
            RING += [("O", O_AT[s_])] if s_ in O_AT else []
        RING_AT = {use: n for n, use in enumerate(RING)}
        USES = len(RING)
        assert USES % 3 == 0

        n_const = 8
        PARTS = ((0, 2), (2, 4), (4, NT))

        @block.sync
        def _(sp):
            xv = x.rearrange("(t p) d -> p t d", p=P)
            sp.dma_start(x_sb[:, 0:2, :], xv[:, 0:2, :]).then_inc(ld_x[0], 16)
            sp.dma_start(ident[:], ident_d).then_inc(ld_id, 16)
            sp.dma_start(wc, wcat.rearrange("(k p) n -> p k n", p=P)).then_inc(ld_wc, 16)
            for c in (1, 2):
                a, b = PARTS[c]
                sp.dma_start(x_sb[:, a:b, :], xv[:, a:b, :]).then_inc(ld_x[c], 16)
            sp.dma_start(wk32, wik.rearrange("(k p) n -> p k n", p=P)).then_inc(ld_c, 16)
            sp.dma_start(causal[:], causal_d).then_inc(ld_c, 16)
            sp.dma_start(qnw[:], qnorm).then_inc(ld_c, 16)
            sp.dma_start(kvw[:], kvnorm).then_inc(ld_c, 16)
            sp.dma_start(rbs, rbias).then_inc(ld_c, 16)
            sp.dma_start(ck, cosk.rearrange("(t p) j -> p t j", p=P)).then_inc(ld_c, 16)
            sp.dma_start(sk, sink.rearrange("(t p) j -> p t j", p=P)).then_inc(ld_c, 16)
            sp.dma_start(bm32, bm).then_inc(ld_c, 16)
            sp.dma_start(cq[:], cosq).then_inc(ld_cq, 16)
            sp.dma_start(sq[:], sinq).then_inc(ld_cq, 16)

            wiq_v = wiq.rearrange("(k p) n -> p k n", p=P)

            def load_iq(n, u, again, first):
                if not first:
                    wait_alone(sp, wq_lo, n + again - 1)
                sp.dma_start(wq32[:, u], wiq_v[:, :, ds(n * ID, ID)]).then_inc(ld_wq[u], 16)

            load_iq(0, 0, 0, True)
            load_iq(1, 1, 0, True)
            with sp.Fori(1, IH // 2) as i:
                load_iq(2 * i, 0, 0, False)
                load_iq(2 * i + 1, 1, 0, False)
            with sp.Fori(0, IH // 2) as i:
                load_iq(2 * i, 0, IH, False)
                load_iq(2 * i + 1, 1, IH, False)

            wait_alone(sp, iq_mm, 2 * IH)

            def load_qw(p, u, first):
                if not first:
                    wait_alone(sp, qw_lo, 4 * p - 4)
                sp.dma_start(qb_s[:, u], qbT[:, ds(2 * p, 2), :]).then_inc(ld_qw[u], 16)
                sp.dma_start(wk_s[:, u], wkT[:, ds(2 * p, 2), :]).then_inc(ld_qw[u], 16)
                sp.dma_start(pe_s[:, u].rearrange("p k (h r) -> p k h r", h=2),
                             qpe[:, :, ds(2 * p, 2), :]).then_inc(ld_qw[u], 16)

            load_qw(0, 0, True)
            load_qw(1, 1, True)
            with sp.Fori(1, NP // 2) as i:
                load_qw(2 * i, 0, False)
                load_qw(2 * i + 1, 1, False)

            def swap(p):
                wait_alone(sp, raw_done, 2 * p + 2)
                if not (isinstance(p, int) and p == 0):
                    wait_alone(sp, rot, 3 * p)
                sp.dma_start(swp[0:P:2, :], raw[1:P:2, :]).then_inc(sw_done, 16)
                sp.dma_start(swp[1:P:2, :], raw[0:P:2, :]).then_inc(sw_done, 16)

            ow_v = ow.rearrange("(h d) n -> d h n", d=P)

            def load_ow(p, u, first):
                if not first:
                    wait_alone(sp, vo_mm, p - (OW_DEEP - 1))
                sp.dma_start(ow_s[:, u], ow_v[:, ds(2 * p, 2), :]).then_inc(ld_ow[u], 16)
                sp.dma_start(wv_s[:, u], wvT[:, ds(2 * p, 2), :]).then_inc(ld_ow[u], 16)

            def store_vo(p, u):
                wait_alone(sp, vo_lo, p + 1)
                sp.dma_start(wvo_d[ds(p, 1)].rearrange("a p n -> (a p) n"),
                             vo_s[:, u].rearrange("p s n -> p (s n)")).then_inc(vo_st[u], 16)

            wait_alone(sp, sum_done, 2 * IH)
            wait_alone(sp, tr_mm, TR_JOBS)
            wait_alone(sp, v_lo, 1)
            for u in range(OW_DEEP):
                load_ow(u, u, True)
            swap(0)
            with sp.Fori(1, NP // OW_DEEP) as i:
                for u in range(OW_DEEP):
                    load_ow(OW_DEEP * i + u, u, False)
                    store_vo(OW_DEEP * i + (u - OW_DEEP), u)
            for p in range(NP - OW_DEEP, NP):
                store_vo(p, p % OW_DEEP)

            with sp.Fori(1, NP) as p:
                swap(p)
            for u in range(OW_DEEP):
                wait_alone(sp, vo_st[u], 16 * NP // OW_DEEP)
            wait_alone(sp, qa_mm, 2 * NP)
            for j, w_ in enumerate((w1hi, w1lo, w2s)):
                sp.dma_start(w_[:].rearrange("p (a b) n -> p a (b n)", b=4),
                             wvo_d[4 * j:4 * j + 4].rearrange("a p n -> p a n")).then_inc(ld_vo, 16)
            wait_alone(sp, rot, 3 * NP)
            for j, w_ in enumerate((cq, sq)):
                sp.dma_start(w_[:].bitcast(F16).rearrange("p (a n) -> p a n", a=2),
                             wvo_d[12 + 2 * j:14 + 2 * j].rearrange("a p n -> p a n")).then_inc(ld_vo, 16)

            wait_alone(sp, s_mm, 16 * NP)

            def rows(t, u, first):
                if not first:
                    wait_alone(sp, fin_done, t - 1)
                sp.dma_start(xr[:, u], x[ds(t * P, P), :]).then_inc(ld_xr[u], 16)

            def store(t, u):
                wait_alone(sp, fin_done, t + 1)
                sp.dma_start(out[ds(t * P, P), :], res[:, u]).then_inc(stored[u], 16)

            rows(0, 0, True)
            rows(1, 1, True)
            with sp.Fori(1, NT // 2) as i:
                store(2 * i - 2, 0)
                rows(2 * i, 0, False)
                store(2 * i - 1, 1)
                rows(2 * i + 1, 1, False)
            store(NT - 2, 0)
            store(NT - 1, 1)
            for u in range(2):
                wait_alone(sp, stored[u], 16 * NT // 2)

        @block.tensor
        def _(pe):
            mm = nc.tensor.matmul

            pe.wait_ge(ld_id, 16)

            def rows_T(t, u, first):
                pe.wait_ge(xn_done, t + 1)
                if not first:
                    pe.wait_ge(xlo_done, t - 1)
                for k in range(KT):
                    last = nc.tensor.transpose(psT[u][:, k * P:(k + 1) * P], xn[:, u, k * P:(k + 1) * P], ident[:])
                last.then_inc(xT_done, 1)

            def rows_proj(t, u, first):
                pe.wait_ge(xlo_done, t + 1)
                if not first:
                    pe.wait_ge(pj_done, t - 1)
                ins = 0
                for k in range(KT):
                    for a, b in ((0, 0), (0, 1), (1, 0)):
                        last = mm(psS[u][:, 0:CW], xnT[:, a, k, ds(t * P, P)], wcp[:, b, k, :],
                                  start=ins == 0, stop=ins == 3 * KT - 1)
                        ins += 1
                last.then_inc(pj_mm, 1)

            rows_T(0, 0, True)
            rows_T(1, 1, True)
            pe.wait_ge(wc_lo, 1)
            for t in range(2):
                rows_proj(t, t, True)
                rows_T(t + 2, t, False)
            with pe.Fori(1, NT // 2 - 1) as i:
                for u in range(2):
                    rows_proj(2 * i + u, u, False)
                    rows_T(2 * i + 2 + u, u, False)
            for u in range(2):
                rows_proj(NT - 2 + u, u, False)

            def indexer(dst, w, c, semaphore):
                ins = 0
                for k in range(KT):
                    for a, b in ((0, 0), (0, 1), (1, 0)):
                        last = mm(dst, w[:, a, k, :], xnT[:, b, k, c * CH:(c + 1) * CH],
                                  start=ins == 0, stop=ins == 3 * KT - 1)
                        ins += 1
                last.then_inc(semaphore, 1)

            pe.wait_ge(wc_lo, 2)
            for c in range(2):
                indexer(psT[c][:], wikp, c, ik_mm)

            def iq_head(q, u, c, first):
                pe.wait_ge(wq_lo, q + 1)
                if not first:
                    pe.wait_ge(iq_lo, q - 1)
                indexer(psT[u][:], wqp[:, u], c, iq_mm)

            def idx_head(t, n, bank, job, back):
                kw = P * (t + 1)
                if back:
                    pe.wait_ge(relu_done, job - back + 1)
                for a, b in ((0, 0), (0, 1), (1, 0)):
                    for c in range(0, kw, CH):
                        w = min(CH, kw - c)
                        last = mm(bank[:, c:c + w], iq[:, a, n, t * P:(t + 1) * P], ikT[:, b, c:c + w],
                                  start=(a, b) == (0, 0), stop=(a, b) == (1, 0))
                last.then_inc(idx_mm, 1)

            def first_idx(n, u, first, last_pair):
                if not (last_pair and u == 1):
                    iq_head(n + 1, 1 - u, 1, first and u == 0)
                pe.wait_ge(iq_lo, n + 1)
                for g_, t in enumerate(GROUPS[0]):
                    idx_head(t, n, psS[g_], 2 * n + g_, 0 if first and u == 0 else 2)

            def transposes(job):
                src, ready, n = ((qn[:, :, 0:P], qn_done, 2), (qn[:, :, P:2 * P], qn_done, 2),
                                 (kc[:, :, 0:P], kc_done, 1), (kc[:, :, KVR:KVR + P], kc_done, 1),
                                 (tmp[:, :, 0:P], hw_done, NT))[job // 2]
                pe.wait_ge(ready, n)
                if job >= 2:
                    pe.wait_ge(tr_lo, job - 1)
                for j in range(4):
                    last = nc.tensor.transpose(tr_bank[job % 2][:, j * P:(j + 1) * P], src[:, 4 * (job % 2) + j, :], ident[:])
                last.then_inc(tr_mm, 1)

            pe.wait_ge(ik_lo, 2)
            iq_head(0, 0, 1, True)
            for u in range(2):
                first_idx(u, u, True, False)
            with pe.Fori(1, TR_FROM // 2) as i:
                for u in range(2):
                    first_idx(2 * i + u, u, False, False)
            for n in range(TR_FROM, IH):
                first_idx(n, n % 2, False, n >= IH - 2)
                for job in tr_jobs_after(n):
                    transposes(job)

            def second_idx(n, u, last):
                if not last:
                    iq_head(n + (IH + 1), 1 - u, 0, False)
                pe.wait_ge(iq_lo, n + (IH + 1))
                for g_, t in enumerate(GROUPS[1]):
                    idx_head(t, n, psS[g_], 2 * n + (2 * IH + g_), 2)

            iq_head(IH, 0, 0, False)
            with pe.Fori(0, IH // 2 - 1) as i:
                for u in range(2):
                    second_idx(2 * i + u, u, False)
            for u in range(2):
                second_idx(IH - 2 + u, u, u == 1)

            pe.wait_ge(iq_lo, 2 * IH)
            pe.wait_ge(relu_done, 4 * IH)

            def qw_pair(p, u, first):
                pe.wait_ge(ld_qw[u], 48 if first else 24 * (p - u) + 48)
                if not first:
                    pe.wait_ge(qw_lo, 4 * p - 4)
                for h in range(2):
                    for k in range(2):
                        last = mm(psT[u][:, 128 * k + 64 * (1 - h):128 * k + 64 * (2 - h)],
                                  qb_s[:, u, h, 128 * k:128 * (k + 1)], wk_s[:, u, h, :], start=True, stop=True)
                last.then_inc(qw_mm, 1)

            def third_idx(n, u, first):
                for g_, t in enumerate(GROUPS[2]):
                    bank = (psS[0][:, 0:CH], psS[1][:, 0:CH], psS[0][:, CH:S])[g_]
                    idx_head(t, n, bank, 3 * n + (4 * IH + g_), 0 if first and u == 0 else 3)
                qw_pair(n, u, first)

            for u in range(2):
                third_idx(u, u, True)
            with pe.Fori(1, IH // 2) as i:
                for u in range(2):
                    third_idx(2 * i + u, u, False)

            def q_job(bank, p, j):
                cs = slice((j % 2) * CH, (j % 2 + 1) * CH)
                ws = slice(128 * (j // 2), 128 * (j // 2 + 1))
                mm(bank, w1hi[:, p, ws], qlT[:, 0, cs], start=True, stop=False)
                mm(bank, w1hi[:, p, ws], qlT[:, 1, cs], start=False, stop=False)
                mm(bank, w1lo[:, p, ws], qlT[:, 0, cs], start=False, stop=False)
                mm(bank, w2s[:, p, ws], qlT[:, 2, cs], start=False, stop=False)
                mm(bank, w2s[0:64, p, ws], qlT[0:64, 3, cs], start=False, stop=True).then_inc(qp_mm if j < 2 else qa_mm, 1)

            def scores(p, v, s, fresh):
                h, k = s // 8, s % 8
                t = ORDER[k]
                kw = P * (t + 1)
                if s == 0:
                    pe.wait_ge(q_rot, 2 * p + 2)
                    pe.wait_ge(qa_lo, 4 * p + 4)
                if not fresh:
                    pe.wait_ge(max_done, 16 * p + s - 1)
                for a, b in ((0, 0), (0, 1), (1, 0)):
                    for c in range(0, kw, CH):
                        w = min(CH, kw - c)
                        last = mm(psS[k % 2][:, c:c + w], Q[:, v, a, h, t * P:(t + 1) * P], keyT[:, b, h, c:c + w],
                                  start=(a, b) == (0, 0), stop=(a, b) == (1, 0))
                last.then_inc(s_mm, 1)

            pe.wait_ge(qw_lo, 4 * NP)
            pe.wait_ge(tr_lo, TR_JOBS)
            pe.wait_ge(relu_done, 7 * IH)
            for j in range(4):
                q_job(q0_bank[j], 0, j)


            def vo_pair(p, u, first):
                pe.wait_ge(ld_ow[u], 32 if first else 32 // OW_DEEP * (p - u) + 32)
                if not (first and u < 2):
                    pe.wait_ge(vo_hi, 2 * p - 2)
                for h in range(2):
                    last = mm(psT[u % 2][64 * h:64 * (h + 1), :], wv_s[:, u, h, :], ow_s[:, u, h, :], start=True, stop=True)
                last.then_inc(vo_mm, 1)

            for u in range(OW_DEEP):
                vo_pair(u, u, True)
            with pe.Fori(1, NP // OW_DEEP - 1) as i:
                for u in range(OW_DEEP):
                    vo_pair(OW_DEEP * i + u, u, False)
            scores(0, 0, 0, True)
            scores(0, 0, 1, True)
            for u in range(OW_DEEP):
                vo_pair(NP - OW_DEEP + u, u, False)

            def wait_bank(p, n, first, last_pair):
                m = n - 3
                while m >= 0 and ((RING[m][0] == "O" and first) or (RING[m][0] == "Q" and last_pair)):
                    m -= 3
                if m < 0 and first:
                    return
                if m < 0:
                    p, m = p - 1, m + USES
                what, at, *c = RING[m]
                if what == "T":
                    pe.wait_ge(p_lo, chunks_before(2 * p + at // 8, at % 8) + c[0] + 1)
                elif what == "O":
                    pe.wait_ge(ot_lo, 2 * p + at - 1)
                elif at in (0, 1):
                    pe.wait_ge(raw_done, 2 * p + at + 3)
                else:
                    pe.wait_ge(qa_hi, 6 * p + 3 * at + 3)

            def values(head, k):
                pe.wait_ge(p_lo, chunks_before(head, k + 1))
                if k == 0 and not (isinstance(head, int) and head == 0):
                    pe.wait_ge(o_done, head)
                dst = psO[:, k * KVR:(k + 1) * KVR]
                for j in range(NB[k]):
                    for n, (a, b) in enumerate(((0, 0), (0, 1), (1, 0))):
                        last = mm(dst, pT[:, k % 2, a, j * P:(j + 1) * P], val[:, b, j, :],
                                  start=j == 0 and n == 0, stop=j == NB[k] - 1 and n == 2)
                last.then_inc(av_mm, 1)

            def out_T(bank, p, c):
                pe.wait_ge(o_done, 2 * p + 2)
                for j in range(4):
                    last = nc.tensor.transpose(bank[:, j * P:(j + 1) * P], op[:, ORDER.index(4 * c + j), :], ident[:])
                last.then_inc(ot_mm, 1)

            def pair(p, v, first, last_pair):
                for s in range(16):
                    k = s % 8
                    pe.wait_ge(exp_done, 16 * p + s + 1)
                    for c in range(NCH[k]):
                        n = RING_AT[("T", s, c)]
                        wait_bank(p, n, first, last_pair)
                        for j in range(4 * c, min(4 * c + 4, NB[k])):
                            last = nc.tensor.transpose(psT[n % 3][:, (j % 4) * P:(j % 4 + 1) * P],
                                                       pr[:, k % 4, j * P:(j + 1) * P], ident[:])
                        last.then_inc(t_mm, 1)
                    if s in Q_AT and not last_pair:
                        n = RING_AT[("Q", Q_AT[s])]
                        wait_bank(p, n, first, last_pair)
                        q_job(psT[n % 3][:], p + 1, Q_AT[s])
                    if s in O_AT and not first:
                        n = RING_AT[("O", O_AT[s])]
                        wait_bank(p, n, first, last_pair)
                        out_T(psT[n % 3], p - 1, O_AT[s])
                    if s + AHEAD < 16:
                        scores(p, v, s + AHEAD, False)
                    elif not last_pair:
                        scores(p + 1, 1 - v, s + AHEAD - 16, False)
                    if s:
                        values(2 * p + (s - 1) // 8, (s - 1) % 8)
                    elif not first:
                        values(2 * p - 1, 7)

            scores(0, 0, 2, False)
            pair(0, 0, True, False)
            with pe.Fori(0, NP // 2 - 1) as i:
                pair(2 * i + 1, 1, False, False)
                pair(2 * i + 2, 0, False, False)
            pair(NP - 1, 1, False, True)
            values(H - 1, 7)

            def products(t, u, pairs):
                for n in pairs:
                    for a, b in ((0, 0), (0, 1), (1, 0)):
                        mm(psS[u][:, 0:CH], big[:, a, n, ds(t * P, P)], wvo[n][:, b, :],
                           start=n == 0 and (a, b) == (0, 0), stop=False)

            def experts(t, u):
                for a, b in ((0, 0), (0, 1), (1, 0)):
                    last = mm(psS[u][:, 0:CH], hwT[:, a, ds(t * P, P)], bmp[:, b, :], start=False, stop=(a, b) == (1, 0))
                last.then_inc(fin_mm, 1)

            pe.wait_ge(ld_vo, 80)
            pe.wait_ge(max_done, 16 * NP)
            pe.wait_ge(ot_lo, 2 * NP - 2)
            products(0, 0, range(NP - 1))
            pe.wait_ge(p_lo, H * CPH)
            for c in range(2):
                out_T(psT[c], NP - 1, c)
            products(1, 1, range(NP - 1))
            pe.wait_ge(ot_lo, 2 * NP)
            for u in range(2):
                products(u, u, [NP - 1])
                experts(u, u)
            with pe.Fori(1, NT // 2) as i:
                for u in range(2):
                    pe.wait_ge(fin_done, 2 * i + (u - 1))
                    products(2 * i + u, u, range(NP))
                    experts(2 * i + u, u)

        @block.scalar
        def _(act):
            def copy(dst, src, scale):
                return nc.scalar.activation(dst, src, ACT.Copy, scale=scale)

            act.wait_ge(ve_done, 1)
            nc.scalar.activation(sd[:, 0:2], ve[:, 0:2], ACT.Sqrt).then_inc(sd_done, 1)

            def rows_hi(t, u):
                act.wait_ge(xT_done, t + 1)
                copy(xnT[:, 0, :, ds(t * P, P)], psT[u][:].rearrange("p (k q) -> p k q", k=KT), X_S).then_inc(xhi_done, 1)

            def rows_pj(t, u):
                act.wait_ge(pj_mm, t + 1)
                copy(proj[:, t, :], psS[u][:, 0:CW], 1.0 / (X_S * W_S)).then_inc(pj_done, 1)

            def squares(i, first):
                if not first:
                    act.wait_ge(sq_done, 4 * i)
                for u in range(2):
                    t = 2 * i + u
                    act.wait_ge(pj_done, t + 1)
                    col = slice(t, t + 1) if isinstance(t, int) else ds(t, 1)
                    nc.scalar.activation(sqd[:, 2 * u, 0:QR], proj[:, t, C_Q:C_Q + QR], ACT.Square,
                                         accum_out=ssq[:, 0, col]).then_inc(sq_done, 1)
                    nc.scalar.activation(sqd[:, 2 * u + 1, 0:KVR], proj[:, t, C_KV:C_KV + KVR], ACT.Square,
                                         accum_out=ssq[:, 1, col]).then_inc(sq_done, 1)

            rows_hi(0, 0)
            rows_hi(1, 1)
            act.wait_ge(ld_wc, 16)
            copy(wcp[:, 0], wc, W_S).then_inc(wc_hi, 1)
            for c in (1, 2):
                a, b = PARTS[c]
                act.wait_ge(ve_done, c + 1)
                nc.scalar.activation(sd[:, a:b], ve[:, a:b], ACT.Sqrt).then_inc(sd_done, 1)
            for u in range(2):
                rows_hi(2 + u, u)
                rows_pj(u, u)
            squares(0, True)
            with act.Fori(1, NT // 2 - 1) as i:
                for u in range(2):
                    rows_hi(2 * i + 2 + u, u)
                    rows_pj(2 * i + u, u)
                squares(i, False)
            act.wait_ge(ld_c, 16 * n_const)
            copy(wikp[:, 0], wk32, W_S).then_inc(wc_hi, 1)
            copy(bmp[:, 0, :], bm32, B_S).then_inc(wc_hi, 1)
            def weights(q, u, first):
                act.wait_ge(ld_wq[u], 16 if first else 8 * (q - u) + 16)
                copy(wqp[:, u, 0], wq32[:, u], W_S).then_inc(wq_hi, 1)
                copy(wq32[:, u], wq32[:, u], W_S).then_inc(wq_hi, 1)

            weights(0, 0, True)
            weights(1, 1, True)
            rows_pj(NT - 2, 0)
            rows_pj(NT - 1, 1)
            squares(NT // 2 - 1, False)
            act.wait_ge(sq_done, 2 * NT)
            act.wait_ge(eps_ok, 1)
            nc.scalar.activation(sdn[:, 0], ssq[:, 0], ACT.Sqrt, bias=eps_t, scale=1.0 / QR).then_inc(n_sqrt, 1)
            nc.scalar.activation(sdn[:, 1], ssq[:, 1], ACT.Sqrt, bias=eps_t, scale=1.0 / KVR).then_inc(n_sqrt, 1)

            def weighted(dst, t, n, job):
                kw = P * (t + 1)
                act.wait_ge(relu_done, job + 1)
                nc.scalar.activation(dst[:, 0:kw], dst[:, 0:kw], ACT.Copy, scale=proj[:, t, ds(C_IW + n, 1)]).then_inc(wt_done, 1)

            sc = IQ_S / (X_S * W_S)
            for c in range(2):
                act.wait_ge(ik_mm, c + 1)
                copy(ikT[:, 0, c * CH:(c + 1) * CH], psT[c][:], sc).then_inc(ik_hi, 1)
            rsc = IH ** -0.5 * ID ** -0.5 / (IQ_S * IQ_S)

            def iq_hi_(n, q, u, c, last=False):
                act.wait_ge(iq_mm, q + 1)
                copy(iq[:, 0, n, c * CH:(c + 1) * CH], psT[u][:], sc).then_inc(iq_hi, 1)
                if not last:
                    weights(q + 2, u, False)

            def relu_head(dst, bank, t, job, back, read, jobs0):
                kw = P * (t + 1)
                act.wait_ge(idx_mm, job + 1)
                if back:
                    act.wait_ge(read, job - (jobs0 + back - 1))
                nc.scalar.activation(dst[:, 0:kw], bank[:, 0:kw], ACT.Relu, scale=rsc).then_inc(relu_done, 1)

            def first_relu(n, u, first, last_pair):
                if not (last_pair and u == 1):
                    iq_hi_(n + 1, n + 1, 1 - u, 1)
                for g_, t in enumerate(GROUPS[0]):
                    relu_head(relu_a[:, g_], psS[g_], t, 2 * n + g_, 0 if first and u == 0 else 2, acc_done, 0)

            iq_hi_(0, 0, 0, 1)
            for u in range(2):
                first_relu(u, u, True, False)
            act.wait_ge(g_sub, 1)
            nc.scalar.activation(gwork[:, :, 0:E], gl, ACT.Exp).then_inc(g_exp, 1)
            with act.Fori(1, TR_FROM // 2) as i:
                for u in range(2):
                    first_relu(2 * i + u, u, False, False)
            def transposed(job):
                dst, s = ((qlT[:, 0], QL_S), (qlT[:, 2], QL_S), (keyT[:, 0, 0], K_S),
                          (keyT[:, 0, 1], K_S), (hwT[:, 0], HW_S * SCALING))[job // 2]
                act.wait_ge(tr_mm, job + 1)
                copy(dst[:, (job % 2) * CH:(job % 2 + 1) * CH], tr_bank[job % 2][:], s).then_inc(tr_hi, 1)

            for n in range(TR_FROM, IH):
                first_relu(n, n % 2, False, n >= IH - 2)
                for job in tr_jobs_after(n):
                    transposed(job)
            act.wait_ge(kc_done, 1)
            copy(val[:, 0], kc[:, :, KVR:2 * KVR], K_S).then_inc(v_hi, 1)

            def second_relu(n, u, first, last=False, weighed=False):
                if not last:
                    iq_hi_(n + 1, n + (IH + 1), 1 - u, 0, weighed)
                for g_, t in enumerate(GROUPS[1]):
                    relu_head(relu_a[:, g_], psS[g_], t, 2 * n + (2 * IH + g_), 0 if first else 2, sum_done, 2 * IH)
                    weighted(relu_a[:, g_], t, n, 2 * n + (2 * IH + g_))

            act.wait_ge(acc_done, 2 * IH)
            iq_hi_(0, IH, 0, 0)
            second_relu(0, 0, True)
            second_relu(1, 1, False)
            with act.Fori(1, IH // 2 - 2) as i:
                for u in range(2):
                    second_relu(2 * i + u, u, False)
            for n in range(IH - 4, IH):
                second_relu(n, n % 2, False, n == IH - 1, n >= IH - 3)

            def third_relu(n, u, first):
                for g_, t in enumerate(GROUPS[2]):
                    bank = (psS[0][:, 0:CH], psS[1][:, 0:CH], psS[0][:, CH:S])[g_]
                    relu_head(src3[g_], bank, t, 3 * n + (4 * IH + g_), 0 if first and u == 0 else 3, sum_done, 2 * IH)
                for g_, t in enumerate(GROUPS[2]):
                    weighted(src3[g_], t, n, 3 * n + (4 * IH + g_))
                act.wait_ge(qw_mm, n + 1)
                copy(w1hi[:, n, 0:128], pe_s[:, u, 0, :], WQ_S).then_inc(qw_hi, 1)
                copy(w2s[:, n, 0:128], pe_s[:, u, 1, :], WQ_S).then_inc(qw_hi, 1)
                copy(w1hi[:, n, 128:256], psT[u][:, 0:128], WQ_S).then_inc(qw_hi, 1)
                copy(w2s[:, n, 128:256], psT[u][:, 128:256], WQ_S).then_inc(qw_hi, 1)

            act.wait_ge(wq_lo, 2 * IH)
            act.wait_ge(iq_mm, 2 * IH)
            for u in range(2):
                third_relu(u, u, True)
            with act.Fori(1, IH // 2) as i:
                for u in range(2):
                    third_relu(2 * i + u, u, False)

            qs = 1.0 / (QL_S * WQ_S)

            def q_evac(bank, p, v, j):
                cs = slice((j % 2) * CH, (j % 2 + 1) * CH)
                if j < 2:
                    act.wait_ge(qp_mm, 2 * p + j + 1)
                    if j == 0 and not (isinstance(p, int) and p == 0):
                        act.wait_ge(rot, 3 * p)
                    copy(raw[:, cs], bank, qs * Q_S).then_inc(raw_done, 1)
                else:
                    act.wait_ge(qa_mm, 2 * p + j - 1)
                    copy(Q[64:128, v, 0, 0, cs], bank[64:128, :], qs * Q_S).then_inc(qa_hi, 1)
                    copy(Q[0:64, v, 0, 1, cs], bank[0:64, :], qs * Q_S).then_inc(qa_hi, 1)
                    if not (isinstance(p, int) and p == 0 and j == 2):
                        act.wait_ge(qa_lo, 4 * p + 2 * j - 4)
                    copy(lat32, bank, qs * Q_S).then_inc(qa_hi, 1)

            act.wait_ge(sum_done, 5 * IH)
            act.wait_ge(qw_lo, 4 * NP)
            for j in range(4):
                q_evac(q0_bank[j], 0, 0, j)

            def vo_hi_(p, u, first):
                act.wait_ge(vo_mm, p + 1)
                if not first:
                    act.wait_ge(vo_st[u], 16 // OW_DEEP * (p - u))
                copy(vo_s[:, u, 0, :], psT[u % 2][:], WVO_S).then_inc(vo_hi, 1)
                if not (first and u < 2):
                    act.wait_ge(vo_lo, p - 1)
                copy(vo32[:, u % 2], psT[u % 2][:], WVO_S).then_inc(vo_hi, 1)

            for u in range(OW_DEEP):
                vo_hi_(u, u, True)
            with act.Fori(1, NP // OW_DEEP) as i:
                for u in range(OW_DEEP):
                    vo_hi_(OW_DEEP * i + u, u, False)

            def exp_step(p, s):
                h, k = s // 8, s % 8
                kw = P * NB[k]
                act.wait_ge(max_done, 16 * p + s + 1)
                nc.scalar.activation(pr[:, k % 4, 0:kw], pr[:, k % 4, 0:kw], ACT.Exp, bias=nmax[:, k % 4:k % 4 + 1],
                                     scale=-1.0, accum_out=rsum[:, h, k:k + 1]).then_inc(exp_done, 1)

            def p_hi_chunk(bank, p, s, c, fresh):
                h, k = s // 8, s % 8
                w = P * min(4, NB[k] - 4 * c)
                act.wait_ge(t_mm, chunks_before(2 * p + h, k) + c + 1)
                if c == 0 and not fresh:
                    act.wait_ge(av_mm, 16 * p + s - 1)
                copy(pT[:, k % 2, 0, c * CH:c * CH + w], bank[:, 0:w], PR_S).then_inc(p_hi, 1)

            def ot_evac(bank, p, c):
                act.wait_ge(ot_mm, 2 * p + c + 1)
                copy(big[:, 0, p, c * CH:(c + 1) * CH], bank[:], O_S / (PR_S * K_S)).then_inc(ot_hi, 1)

            def pair(p, v, first, last_pair):
                for n, (what, at, *c) in enumerate(RING):
                    if what == "T":
                        p_hi_chunk(psT[n % 3], p, at, c[0], first and at < 2)
                        if c[0] == NCH[at % 8] - 1:
                            if at + AHEAD - 1 < 16:
                                exp_step(p, at + AHEAD - 1)
                            elif not last_pair:
                                exp_step(p + 1, at + AHEAD - 17)
                    elif what == "Q" and not last_pair:
                        q_evac(psT[n % 3][:], p + 1, 1 - v, at)
                    elif what == "O" and not first:
                        ot_evac(psT[n % 3], p - 1, at)

            exp_step(0, 0)
            exp_step(0, 1)
            for u in range(OW_DEEP):
                act.wait_ge(vo_st[u], 16 * NP // OW_DEEP)
            pair(0, 0, True, False)
            with act.Fori(0, NP // 2 - 1) as i:
                pair(2 * i + 1, 1, False, False)
                pair(2 * i + 2, 0, False, False)
            pair(NP - 1, 1, False, True)
            for c in range(2):
                ot_evac(psT[c], NP - 1, c)

        @block.vector
        def _(dve):
            v = nc.vector
            count = {}

            def link(ins, s=nrm):
                count[s] = count.get(s, 0) + 1
                ins.then_inc(s, 1)
                dve.wait_ge(s, count[s])

            def low(dst, src, scale, hi):
                return v.scalar_tensor_tensor(out=dst, in0=src, scalar=scale, in1=hi, op0=ALU.mult, op1=ALU.subtract)

            def stats(c, a, b):
                dve.wait_ge(ld_x[c], 16)
                for t in range(a, b):
                    v.bn_stats(st[:, t, :], x_sb[:, t, :]).then_inc(st_done, 1)
                dve.wait_ge(st_done, a + b)
                for t in range(a, b):
                    v.bn_aggr(mv[:, t, :], st[:, t, :]).then_inc(st_done, 1)
                dve.wait_ge(st_done, 2 * b)
                v.tensor_scalar(ve[:, a:b], mv[:, a:b, 1], EPS, None, ALU.add).then_inc(ve_done, 1)

            def deviations(c, a, b):
                dve.wait_ge(sd_done, c + 1)
                v.reciprocal(rstd[:, a:b], sd[:, a:b]).then_inc(rs_done, 1)
                dve.wait_ge(rs_done, c + 1)

            def rows_n(t, u, first):
                if not first:
                    dve.wait_ge(xT_done, t - 1)
                v.tensor_scalar(xn[:, u, :], x_sb[:, t, :], mv[:, t, 0:1], rstd[:, ds(t, 1)],
                                ALU.subtract, ALU.mult).then_inc(xn_done, 1)

            def rows_lo(t, u):
                dve.wait_ge(xhi_done, t + 1)
                low(xnT[:, 1, :, ds(t * P, P)], psT[u][:].rearrange("p (k q) -> p k q", k=KT), X_S,
                    xnT[:, 0, :, ds(t * P, P)]).then_inc(xlo_done, 1)

            stats(0, 0, 2)
            deviations(0, 0, 2)
            rows_n(0, 0, True)
            rows_n(1, 1, True)
            rows_lo(0, 0)
            rows_lo(1, 1)
            dve.wait_ge(wc_hi, 1)
            low(wcp[:, 1].rearrange("p k n -> p (k n)"), wc.rearrange("p k n -> p (k n)"), W_S,
                wcp[:, 0].rearrange("p k n -> p (k n)")).then_inc(wc_lo, 1)
            for c in (1, 2):
                stats(c, *PARTS[c])
                deviations(c, *PARTS[c])
                if c == 1:
                    rows_n(2, 0, False)
                    rows_n(3, 1, False)
            with dve.Fori(1, NT // 2 - 1) as i:
                for u in range(2):
                    rows_lo(2 * i + u, u)
                    rows_n(2 * i + 2 + u, u, False)
            for u in range(2):
                rows_lo(NT - 2 + u, u)
            dve.wait_ge(wc_hi, 3)
            low(wikp[:, 1].rearrange("p k n -> p (k n)"), wk32.rearrange("p k n -> p (k n)"), W_S,
                wikp[:, 0].rearrange("p k n -> p (k n)")).then_inc(wc_lo, 1)
            low(bmp[:, 1, :], bm32, B_S, bmp[:, 0, :]).then_inc(wc_lo, 1)

            dve.wait_ge(pj_done, NT)
            link(v.tensor_tensor(gl, proj[:, :, C_R:C_R + E], rbs.unsqueeze(1).broadcast_to([P, NT, E]), ALU.add))
            link(v.tensor_reduce(gm, gl, AX.X, ALU.max))
            v.tensor_tensor(gl, gl, gm.unsqueeze(2).broadcast_to([P, NT, E]), ALU.subtract).then_inc(g_sub, 1)
            v.memset(gwork[:, :, E:2 * E], -1.0).then_inc(st_done, 1)
            v.memset(grep[:], -1.0).then_inc(st_done, 1)
            dve.wait_ge(n_sqrt, 2)
            v.reciprocal(rsn, sdn).then_inc(rsn_done, 1)

            sc = IQ_S / (X_S * W_S)
            for c in range(2):
                dve.wait_ge(ik_hi, c + 1)
                low(ikT[:, 1, c * CH:(c + 1) * CH], psT[c][:], sc, ikT[:, 0, c * CH:(c + 1) * CH]).then_inc(ik_lo, 1)
            dve.wait_ge(idx_init, 2)

            def iq_lo_(n, q, u, c):
                dve.wait_ge(iq_hi, q + 1)
                cs = slice(c * CH, (c + 1) * CH)
                low(iq[:, 1, n, cs], psT[u][:], sc, iq[:, 0, n, cs]).then_inc(iq_lo, 1)

            def acc(src, t, n, job, back):
                row = bias[:, TOFF[t]:TOFF[t + 1]]
                dve.wait_ge(relu_done, job + 1)
                if back:
                    dve.wait_ge(acc_done, job - back + 1)
                v.scalar_tensor_tensor(out=row, in0=src[:, 0:P * (t + 1)], scalar=proj[:, t, ds(C_IW + n, 1)],
                                       in1=row, op0=ALU.mult, op1=ALU.add).then_inc(acc_done, 1)

            def first_acc(n, u, first, last_pair):
                if not (last_pair and u == 1):
                    iq_lo_(n + 1, n + 1, 1 - u, 1)
                for g_, t in enumerate(GROUPS[0]):
                    acc(relu_a[:, g_], t, n, 2 * n + g_, 0 if first and u == 0 else 2)

            iq_lo_(0, 0, 0, 1)
            for u in range(2):
                first_acc(u, u, True, False)
            dve.wait_ge(st_done, 2 * NT + 2)
            dve.wait_ge(g_exp, 1)
            for t in range(NT):
                v.max(gmx[:, t, :], gwork[:, t, 0:E]).then_inc(st_done, 1)
            dve.wait_ge(st_done, 3 * NT + 2)
            link(v.tensor_copy(grep[:, :, 0:2], gmx[:, :, 0:2]))
            for t in range(NT):
                v.match_replace(out=gout[:, t, :], in_to_replace=grep[:, t, :], in_values=gwork[:, t, :], imm_value=2.0).then_inc(st_done, 1)
            dve.wait_ge(st_done, 4 * NT + 2)
            link(v.tensor_scalar(gout[:, :, 0:E], gout[:, :, 0:E], 2.0, None, ALU.is_ge))
            link(v.tensor_tensor(gw, gout[:, :, 0:E], gwork[:, :, 0:E], ALU.mult))
            link(v.tensor_tensor(gden, gmx[:, :, 0], gmx[:, :, 1], ALU.add))
            link(v.reciprocal(grd, gden))
            v.tensor_tensor(gw, gw, grd.unsqueeze(2).broadcast_to([P, NT, E]), ALU.mult).then_inc(gw_done, 1)

            with dve.Fori(1, TR_FROM // 2) as i:
                for u in range(2):
                    first_acc(2 * i + u, u, False, False)
            def transposed_lo(job):
                dh, dl, s, rows_ = ((qlT[:, 0], qlT[:, 1], QL_S, P), (qlT[:, 2], qlT[:, 3], QL_S, 64),
                                    (keyT[:, 0, 0], keyT[:, 1, 0], K_S, P), (keyT[:, 0, 1], keyT[:, 1, 1], K_S, P),
                                    (hwT[:, 0], hwT[:, 1], HW_S * SCALING, P))[job // 2]
                cs = slice((job % 2) * CH, (job % 2 + 1) * CH)
                dve.wait_ge(tr_hi, job + 1)
                low(dl[0:rows_, cs], tr_bank[job % 2][0:rows_, :], s, dh[0:rows_, cs]).then_inc(tr_lo, 1)

            for n in range(TR_FROM, IH):
                first_acc(n, n % 2, False, n >= IH - 2)
                for job in tr_jobs_after(n):
                    transposed_lo(job)
            dve.wait_ge(v_hi, 1)
            low(val[:, 1], kc[:, :, KVR:2 * KVR], K_S, val[:, 0]).then_inc(v_lo, 1)

            def top_max(group, r, g_, rows_, done, first):
                if not first:
                    wait_alone(dve, tk_rep, len(group) * r + (done + g_ + 1 - len(group)))
                v.max(m8[:, g_], rows_[g_]).then_inc(tk_max, 1)

            def top_mark(group, r, g_, rows_, done):
                wait_alone(dve, tk_max, len(group) * r + (done + g_ + 1))
                v.match_replace(out=rows_[g_], in_to_replace=m8[:, g_], in_values=rows_[g_], imm_value=TAKEN).then_inc(tk_rep, 1)

            def mask(rows_, done):
                dve.wait_ge(tk_rep, done)
                for row in rows_:
                    v.tensor_scalar(row, row, HALF_TAKEN, NEG, ALU.is_gt, ALU.mult).then_inc(mask_done, 1)

            def rows_of(group):
                return [bias[:, TOFF[t]:TOFF[t + 1]] for t in group]

            g0, g1, g2 = GROUPS
            dve.wait_ge(acc_done, 2 * IH)

            def second(n, u, first, last=False):
                top_max(g0, n, 0, rows_of(g0), 0, first)
                top_max(g0, n, 1, rows_of(g0), 0, first)
                top_mark(g0, n, 0, rows_of(g0), 0)
                top_mark(g0, n, 1, rows_of(g0), 0)
                if not last:
                    iq_lo_(n + 1, n + (IH + 1), 1 - u, 0)

            iq_lo_(0, IH, 0, 0)
            second(0, 0, True)
            second(1, 1, False)
            with dve.Fori(1, IH // 2 - 1) as i:
                for u in range(2):
                    second(2 * i + u, u, False)
            for u in range(2):
                second(IH - 2 + u, u, False, u == 1)
            done = 2 * (TOPK // 8)
            mask(rows_of(g0), done)

            dve.wait_ge(sum_done, 2 * IH)

            def third(n, u, first):
                top_max(g1, n, 0, rows_of(g1), done, first and u == 0)
                top_max(g1, n, 1, rows_of(g1), done, first and u == 0)
                top_mark(g1, n, 0, rows_of(g1), done)
                top_mark(g1, n, 1, rows_of(g1), done)
                dve.wait_ge(qw_hi, 4 * n + 2)
                low(w1lo[:, n, 0:128], pe_s[:, u, 0, :], WQ_S, w1hi[:, n, 0:128]).then_inc(qw_lo, 1)
                low(w2s[64:128, n, 0:128], pe_s[64:128, u, 1, :], WQ_S, w2s[64:128, n, 0:128]).then_inc(qw_lo, 1)
                dve.wait_ge(qw_hi, 4 * n + 4)
                low(w1lo[:, n, 128:256], psT[u][:, 0:128], WQ_S, w1hi[:, n, 128:256]).then_inc(qw_lo, 1)
                low(w2s[64:128, n, 128:256], psT[u][64:128, 128:256], WQ_S, w2s[64:128, n, 128:256]).then_inc(qw_lo, 1)

            for u in range(2):
                third(u, u, True)
            with dve.Fori(1, IH // 2) as i:
                for u in range(2):
                    third(2 * i + u, u, False)
            done3 = done + 2 * (TOPK // 8)
            mask(rows_of(g1), done3)

            def rope_hi(p, v_):
                dve.wait_ge(rot, 3 * p + 3)
                v.tensor_copy(Q[0:64, v_, 0, 0, :], rt[0:64, :]).then_inc(rope_h, 1)
                v.tensor_copy(Q[64:128, v_, 0, 1, :], rt[64:128, :]).then_inc(rope_h, 1)

            dve.wait_ge(sum_done, 5 * IH)

            def fourth(n, u, first):
                for g_ in range(3):
                    top_max(g2, n, g_, rows_of(g2), done3, first and u == 0)
                for g_ in range(3):
                    top_mark(g2, n, g_, rows_of(g2), done3)

            for u in range(2):
                fourth(u, u, True)
            for n in range(2, 8):
                fourth(n, n % 2, False)
            rope_hi(0, 0)
            with dve.Fori(4, IH // 2) as i:
                for u in range(2):
                    fourth(2 * i + u, u, False)
            mask(rows_of(g2), done3 + 3 * (TOPK // 8))
            dve.wait_ge(mask_done, 7)

            c_s = (NOPE + ROPE) ** -0.5 / (Q_S * K_S)

            def row_max(p, s, fresh):
                k = s % 8
                t, kw = ORDER[k], P * NB[k]
                if not fresh:
                    head = 2 * p + s // 8
                    prev = chunks_before(head, k - 3) if k >= 3 else chunks_before(head - 1, k + 5)
                    wait_alone(dve, t_mm, prev)
                    wait_alone(dve, exp_done, 16 * p + s - 3)
                wait_alone(dve, s_mm, 16 * p + s + 1)
                v.tensor_tensor_reduce(out=pr[:, k % 4, 0:kw], in0=psS[k % 2][:, 0:kw], in1=bias[:, TOFF[t]:TOFF[t + 1]],
                                       scale=-c_s, scalar=3e38, op0=ALU.add, op1=ALU.min,
                                       accum_out=nmax[:, k % 4:k % 4 + 1]).then_inc(max_done, 1)

            def p_low_chunk(bank, p, s, c):
                h, k = s // 8, s % 8
                w = P * min(4, NB[k] - 4 * c)
                dve.wait_ge(p_hi, chunks_before(2 * p + h, k) + c + 1)
                low(pT[:, k % 2, 1, c * CH:c * CH + w], bank[:, 0:w], PR_S,
                    pT[:, k % 2, 0, c * CH:c * CH + w]).then_inc(p_lo, 1)

            def head_inv(p, h):
                dve.wait_ge(exp_done, 8 * (2 * p + h) + 8)
                v.reciprocal(rinv, rsum[:, h, :]).then_inc(ri_done, 1)

            def head_out(p, h):
                head = 2 * p + h
                dve.wait_ge(av_mm, 8 * head + 8)
                dve.wait_ge(ri_done, head + 1)
                if not (isinstance(p, int) and p == 0):
                    dve.wait_ge(ot_mm, 2 * p)
                v.tensor_tensor(op[:, :, h * KVR:(h + 1) * KVR], psO[:].rearrange("p (k r) -> p k r", k=NT),
                                rinv.unsqueeze(2).broadcast_to([P, NT, KVR]), ALU.mult).then_inc(o_done, 1)

            def ot_low(bank, p, c):
                dve.wait_ge(ot_hi, 2 * p + c + 1)
                low(big[:, 1, p, c * CH:(c + 1) * CH], bank[:], O_S / (PR_S * K_S),
                    big[:, 0, p, c * CH:(c + 1) * CH]).then_inc(ot_lo, 1)

            def pair(p, v_, first, last_pair):
                for n, (what, at, *c) in enumerate(RING):
                    if what == "T":
                        new_head = at % 8 == 0 and not (first and at == 0)
                        ended = (p if at else p - 1, 0 if at else 1)
                        if new_head and c[0] == 0:
                            head_inv(*ended)
                        p_low_chunk(psT[n % 3], p, at, c[0])
                        if new_head and c[0] == NCH[0] - 1:
                            head_out(*ended)
                        if c[0] == NCH[at % 8] - 1:
                            if at + AHEAD < 16:
                                row_max(p, at + AHEAD, first and at + AHEAD < 4)
                            elif not last_pair:
                                row_max(p + 1, at + AHEAD - 16, False)
                        if at == ROPE_AT and c[0] == NCH[at % 8] - 1 and not last_pair:
                            rope_hi(p + 1, 1 - v_)
                    elif what == "O" and not first:
                        ot_low(psT[n % 3], p - 1, at)

            for s in range(3):
                if s == 1:
                    dve.wait_ge(vo_mm, NP)
                row_max(0, s, True)
            pair(0, 0, True, False)
            with dve.Fori(0, NP // 2 - 1) as i:
                pair(2 * i + 1, 1, False, False)
                pair(2 * i + 2, 0, False, False)
            pair(NP - 1, 1, False, True)
            head_inv(NP - 1, 1)
            head_out(NP - 1, 1)
            for c in range(2):
                ot_low(psT[c], NP - 1, c)

            def final(t, u, first):
                dve.wait_ge(fin_mm, t + 1)
                dve.wait_ge(ld_xr[u], 16 if first else 8 * (t - u) + 16)
                if not first:
                    dve.wait_ge(stored[u], 8 * (t - u))
                v.scalar_tensor_tensor(out=res[:, u], in0=psS[u][:, 0:CH], scalar=1.0 / OUT_S, in1=xr[:, u],
                                       op0=ALU.mult, op1=ALU.add).then_inc(fin_done, 1)

            final(0, 0, True)
            final(1, 1, True)
            with dve.Fori(1, NT // 2) as i:
                final(2 * i, 0, False)
                final(2 * i + 1, 1, False)

        @block.gpsimd
        def _(pool):
            g = nc.gpsimd
            g.memset(eps_t, EPS).then_inc(eps_ok, 1)
            g.memset(bias[:], 0.0).then_inc(idx_init, 1)
            pool.wait_ge(idx_init, 1)
            pool.wait_ge(ld_c, 16 * n_const)
            for t in range(NT):
                ins = g.tensor_copy(bias[:, TOFF[t + 1] - P:TOFF[t + 1]], causal[:])
            ins.then_inc(idx_init, 1)

            def wq_parts(q, u):
                pool.wait_ge(wq_hi, 2 * q + 2)
                g.tensor_tensor(wqp[:, u, 1], wq32[:, u], wqp[:, u, 0], ALU.subtract).then_inc(wq_lo, 1)

            pn = [0]

            def link(ins):
                pn[0] += 1
                ins.then_inc(pool_n, 1)
                pool.wait_ge(pool_n, pn[0])

            def mul(dst, a, b):
                return g.tensor_tensor(dst, a, b, ALU.mult)

            def query_latents():
                pool.wait_ge(rsn_done, 1)
                link(mul(tmp, proj[:, :, C_Q:C_Q + QR], rsn[:, 0].unsqueeze(2).broadcast_to([P, NT, QR])))
                mul(qn[:, :, 0:QR], tmp, qnw[:].unsqueeze(1).broadcast_to([P, NT, QR])).then_inc(qn_done, 1)
                mul(qn[:, :, QR:256], tmp[:, :, P:QR], qnw[:, P:QR].unsqueeze(1).broadcast_to([P, NT, QR - P])).then_inc(qn_done, 1)

            def key_latents():
                pool.wait_ge(qn_done, 2)
                link(mul(tmp[:, :, 0:KVR], proj[:, :, C_KV:C_KV + KVR], rsn[:, 1].unsqueeze(2).broadcast_to([P, NT, KVR])))
                link(mul(kc[:, :, KVR:2 * KVR], tmp[:, :, 0:KVR], kvw[:].unsqueeze(1).broadcast_to([P, NT, KVR])))

            def key_rope():
                kp = proj[:, :, C_KV + KVR:C_KV + KVR + ROPE].rearrange("p t (j two) -> p t j two", two=2)
                t4 = tmp[:, :, 0:128].rearrange("p t (f j) -> p t f j", f=4)
                for f, (part, table) in enumerate(((0, ck), (1, sk), (1, ck), (0, sk))):
                    link(mul(t4[:, :, f], kp[:, :, :, part], table))
                for at in (0, 2 * KVR):
                    ko = kc[:, :, at:at + ROPE].rearrange("p t (j two) -> p t j two", two=2)
                    link(g.tensor_tensor(ko[:, :, :, 0], t4[:, :, 0], t4[:, :, 1], ALU.subtract))
                    ins = g.tensor_tensor(ko[:, :, :, 1], t4[:, :, 2], t4[:, :, 3], ALU.add)
                    if at:
                        ins.then_inc(kc_done, 1)
                    else:
                        link(ins)

            def gated_rows():
                pool.wait_ge(kc_done, 1)
                pool.wait_ge(gw_done, 1)
                for t in range(NT):
                    mul(tmp[:, t, 0:P].rearrange("p (e r) -> p e r", e=E),
                        proj[:, t, C_H:C_H + P].rearrange("p (e r) -> p e r", e=E),
                        gw[:, t, :].unsqueeze(2).broadcast_to([P, E, R])).then_inc(hw_done, 1)

            wq_parts(0, 0)
            wq_parts(1, 1)
            wq_parts(2, 0)
            query_latents()
            wq_parts(3, 1)
            key_latents()
            wq_parts(4, 0)
            key_rope()
            wq_parts(5, 1)
            gated_rows()
            with pool.Fori(3, IH // 2 + 1) as i:
                wq_parts(2 * i, 0)
                wq_parts(2 * i + 1, 1)

            def join(src, t, job, back):
                row = bias[:, TOFF[t]:TOFF[t + 1]]
                pool.wait_ge(wt_done, job + 1)
                if back:
                    pool.wait_ge(sum_done, job - back + 1)
                g.tensor_tensor(row, src[:, 0:P * (t + 1)], row, ALU.add).then_inc(sum_done, 1)

            def second_sums(n, first):
                for g_, t in enumerate(GROUPS[1]):
                    join(relu_a[:, g_], t, 2 * n + g_, 0 if first else 2)

            wq_parts(IH + 2, 0)
            wq_parts(IH + 3, 1)
            second_sums(0, True)
            wq_parts(IH + 4, 0)
            second_sums(1, False)
            with pool.Fori(1, IH // 2 - 2) as i:
                for u in range(2):
                    wq_parts(2 * i + (IH + 3 + u), 1 - u)
                    second_sums(2 * i + u, False)
            wq_parts(2 * IH - 1, 1)
            for n in range(IH - 4, IH):
                second_sums(n, False)

            def third_sums(n, first):
                for g_, t in enumerate(GROUPS[2]):
                    join(src3[g_], t, 3 * n + (2 * IH + g_), 0 if first else 3)

            third_sums(0, True)
            third_sums(1, False)
            with pool.Fori(1, IH // 2) as i:
                for u in range(2):
                    third_sums(2 * i + u, False)

            pool.wait_ge(ld_cq, 32)

            def rope_turn(p):
                pool.wait_ge(raw_done, 2 * p + 2)
                if not (isinstance(p, int) and p == 0):
                    pool.wait_ge(q_rot, 2 * p)
                g.tensor_tensor(rt, raw, cq[:], ALU.mult).then_inc(rot, 1)
                pool.wait_ge(sw_done, 32 * p + 32)
                g.tensor_tensor(swp, swp, sq[:], ALU.mult).then_inc(rot, 1)
                pool.wait_ge(rot, 3 * p + 2)
                g.tensor_tensor(rt, rt, swp, ALU.add).then_inc(rot, 1)

            def rope_low(p, v_):
                pool.wait_ge(rope_h, 2 * p + 1)
                g.tensor_tensor(Q[0:64, v_, 1, 0, :], rt[0:64, :], Q[0:64, v_, 0, 0, :], ALU.subtract).then_inc(q_rot, 1)
                pool.wait_ge(rope_h, 2 * p + 2)
                g.tensor_tensor(Q[64:128, v_, 1, 1, :], rt[64:128, :], Q[64:128, v_, 0, 1, :], ALU.subtract).then_inc(q_rot, 1)
                pool.wait_ge(q_rot, 2 * p + 2)

            def q_low(p, v_, j):
                cs = slice((j % 2) * CH, (j % 2 + 1) * CH)
                pool.wait_ge(qa_hi, 6 * p + 3 * j - 3)
                g.tensor_tensor(Q[64:128, v_, 1, 0, cs], lat32[64:128, :], Q[64:128, v_, 0, 0, cs], ALU.subtract).then_inc(qa_lo, 1)
                pool.wait_ge(qa_lo, 4 * p + 2 * j - 3)
                g.tensor_tensor(Q[0:64, v_, 1, 1, cs], lat32[0:64, :], Q[0:64, v_, 0, 1, cs], ALU.subtract).then_inc(qa_lo, 1)
                pool.wait_ge(qa_lo, 4 * p + 2 * j - 2)

            q_low(0, 0, 2)
            q_low(0, 0, 3)

            def vo_low(p, u):
                pool.wait_ge(vo_hi, 2 * p + 2)
                g.tensor_tensor(vo_s[:, u, 1, :], vo32[:, u % 2], vo_s[:, u, 0, :], ALU.subtract).then_inc(vo_lo, 1)

            rope_turn(0)
            for p in range(OW_DEEP):
                vo_low(p, p)
            pool.wait_ge(vo_lo, OW_DEEP)
            rope_low(0, 0)
            with pool.Fori(1, NP // OW_DEEP) as i:
                for u in range(OW_DEEP):
                    vo_low(OW_DEEP * i + u, u)

            def rope(p, v_):
                rope_turn(p)
                pool.wait_ge(rot, 3 * p + 3)
                q_low(p, v_, 2)
                rope_low(p, v_)
                q_low(p, v_, 3)

            rope(1, 1)
            with pool.Fori(1, NP // 2) as i:
                rope(2 * i, 0)
                rope(2 * i + 1, 1)


def kernel(**inputs):
    import concourse.bacc as _bacc
    from concourse.bass_utils import run_bass_kernel_spmd as _run

    def host(name):
        return np.asarray(inputs["L0_" + name])

    x = host("attn_hidden_states").reshape(S, HID)
    qb = host("attn_q_b_w").reshape(QR, H, NOPE + ROPE)
    kvb = host("attn_kv_b_w").reshape(KVR, H, NOPE + VD)
    twice = np.r_[0:QR, P:QR]
    freq = (np.float32(1.0) / np.float32(10000.0) ** (np.arange(0, ROPE, 2, dtype=np.float32) / np.float32(ROPE))).astype(np.float32)
    ang = np.arange(S, dtype=np.float32)[:, None] * freq[None, :]
    cos, sin = np.cos(ang).astype(np.float32), np.sin(ang).astype(np.float32)
    cos_rows = np.repeat(cos.T, 2, axis=0)
    sin_rows = np.repeat(sin.T, 2, axis=0) * np.tile(np.array([-1.0, 1.0], np.float32), ROPE // 2)[:, None]
    arrays = {
        "x": x,
        "wcat": np.concatenate([host("attn_q_a_w"), host("attn_kv_a_w"), host("attn_idx_weights_w"),
                                host("ffn_router_w").T, host("ffn_A").reshape(E * R, HID).T], axis=1),
        "wik": host("attn_idx_wk_w"),
        "wiq": host("attn_idx_wq_w"),
        "qbT": qb[twice, :, :NOPE].transpose(2, 1, 0),
        "wkT": kvb[:, :, :NOPE].transpose(2, 1, 0),
        "wvT": kvb[:, :, NOPE:].transpose(2, 1, 0),
        "qpe": qb[twice, :, NOPE:].reshape(2, P, H, ROPE).transpose(1, 0, 2, 3),
        "ow": host("attn_o_w"),
        "bm": host("ffn_Bm").transpose(0, 2, 1).reshape(E * R, HID),
        "qnorm": np.broadcast_to(host("attn_q_a_norm_w"), (P, QR)),
        "kvnorm": np.broadcast_to(host("attn_kv_a_norm_w"), (P, KVR)),
        "rbias": np.broadcast_to(host("ffn_router_b"), (P, E)),
        "cosq": np.concatenate([cos_rows, cos_rows]),
        "sinq": np.concatenate([sin_rows, sin_rows]),
        "cosk": cos,
        "sink": sin,
        "ident": np.eye(P, dtype=np.float32),
        "causal": np.triu(np.full((P, P), NEG, np.float32), 1),
    }
    nc = _bacc.Bacc("TRN2", target_bir_lowering=False, num_devices=1)
    given, args = {}, []
    for name, a in arrays.items():
        given["in_" + name] = np.ascontiguousarray(a)
        args.append(nc.dram_tensor("in_" + name, a.shape, F32, kind="ExternalInput").ap())
    result = nc.dram_tensor("out_0", (S, HID), F32, kind="ExternalOutput").ap()
    block_kernel(nc, *args, result)
    r = _run(nc, [given], core_ids=[0])
    return r.results[0]["out_0"].reshape(1, S, HID)
```
